# Optimizing a Trainium2 kernel written in Bass

```python
import numpy as np
import jax
import jax.numpy as jnp

def _softmax(x, axis=-1):
    return jax.nn.softmax(x, axis=axis)

def _gelu(x):
    return jax.nn.gelu(x, approximate=True)

def _silu(x):
    return jax.nn.silu(x)

def _sigmoid(x):
    return jax.nn.sigmoid(x)

def _layernorm(x, axis=-1, eps=1e-05):
    m = jnp.mean(x, axis=axis, keepdims=True)
    v = jnp.var(x, axis=axis, keepdims=True)
    return (x - m) / jnp.sqrt(v + eps)

def _scatter_add(tgt, idx, src, axis=0):
    return tgt.at[idx].add(src)

def _segment_sum(src, seg, n):
    return jax.ops.segment_sum(src, seg, n)
kernel_name = 'mk_cond_resid_d4_seqx_r8_154bd7'

def setup_inputs(seed: int=0):
    np.random.seed(seed)
    _w = jnp.asarray

    def _rec_inputs():
        import jax
        import jax.numpy as jnp
        _rk = jax.random.key(seed)
        x = -7.109e-05 + 0.9999 * jax.random.normal(jax.random.fold_in(_rk, 1), (128, 32, 256), jnp.float32)
        _lenS = 32 - jax.random.randint(jax.random.fold_in(_rk, 7), (128,), 0, max(1, 32 // 4) + 1, jnp.int32)
        _lenS2 = 32 - jax.random.randint(jax.random.fold_in(_rk, 8), (128,), 0, max(1, 32 // 4) + 1, jnp.int32)
        itok_B_0_7 = jax.random.randint(jax.random.fold_in(_rk, 11), (128,), 0, 8, jnp.int32)
        itok_B_1_198 = jax.random.randint(jax.random.fold_in(_rk, 12), (128,), 1, 199, jnp.int32)
        itok_Bx257_0_4111 = jax.random.randint(jax.random.fold_in(_rk, 13), (128, 257), 0, 514, jnp.int32)
        itok_B_37_3939 = jax.random.randint(jax.random.fold_in(_rk, 14), (128,), 37, 3940, jnp.int32)
        itok_B_0_6 = jax.random.randint(jax.random.fold_in(_rk, 15), (128,), 0, 7, jnp.int32)
        return (x, itok_B_0_7, itok_B_1_198, itok_Bx257_0_4111, itok_B_37_3939, itok_B_0_6)
    x, itok_B_0_7, itok_B_1_198, itok_Bx257_0_4111, itok_B_37_3939, itok_B_0_6 = _rec_inputs()

    def _L0_cond_setup():
        import jax, jax.numpy as jnp
        import numpy as np
        B, C, D, T, N_SUBJECTS = (128, 32, 32, 256, 8)
        key = jax.random.key(seed)
        kx, ks, kw = jax.random.split(key, 3)
        x = jax.random.normal(kx, (B, C, T), dtype=jnp.float32)
        subjects = jax.random.randint(ks, (B,), 0, N_SUBJECTS, dtype=jnp.int64)
        weights = jax.random.normal(kw, (N_SUBJECTS, C, D), dtype=jnp.float32) * (1.0 / C ** 0.5)
        return {'x': x, 'subjects': subjects, 'weights': weights}
    _L0_cond_all = _L0_cond_setup()
    _L0_cond_in = {k: v for k, v in _L0_cond_all.items() if k in ('weights',)}
    del _L0_cond_all

    def _L1_cond_setup():
        import jax, jax.numpy as jnp
        import numpy as np
        B, C, T = (128, 32, 256)
        S, D = (200, 32)
        key = jax.random.key(seed)
        k1, k2, k3 = jax.random.split(key, 3)
        x = jax.random.normal(k1, (B, C, T), dtype=jnp.float32)
        conditions = jax.random.randint(k2, (B,), 0, S, dtype=jnp.int64)
        weights = jax.random.normal(k3, (S, C, D), dtype=jnp.float32) / jnp.sqrt(jnp.float32(C))
        return {'x': x, 'conditions': conditions, 'weights': weights}
    _L1_cond_all = _L1_cond_setup()
    _L1_cond_in = {k: v for k, v in _L1_cond_all.items() if k in ('weights',)}
    del _L1_cond_all

    def _L2_cond_setup():
        import jax, jax.numpy as jnp
        import numpy as np
        H, G, HD = (8, 4, 32)
        GSZ = H // G
        BLOCK = 16
        WINDOW = 128
        SCALE = 256.0 ** (-0.5)
        EPS = 1e-06
        THETA = 10000.0
        B, T, D = (16, 4, 256)
        NBLK = 257

        def _rms(x, scale):
            var = jnp.mean(x * x, axis=-1, keepdims=True)
            return x * jax.lax.rsqrt(var + EPS) * (1.0 + scale)

        def _rope(x, pos):
            half = HD // 2
            inv = 1.0 / THETA ** (jnp.arange(half, dtype=jnp.float32) / half)
            ang = pos[:, :, None].astype(jnp.float32) * inv
            cos = jnp.cos(ang)[:, None, :, :]
            sin = jnp.sin(ang)[:, None, :, :]
            x1, x2 = (x[..., :half], x[..., half:])
            return jnp.concatenate([x1 * cos - x2 * sin, x2 * cos + x1 * sin], axis=-1)
        key = jax.random.key(seed)
        ks = jax.random.split(key, 10)
        inv_d = 1.0 / np.sqrt(D)
        return {'x': jax.random.normal(ks[0], (B, T, D), jnp.float32), 'Wq': jax.random.normal(ks[1], (H * HD, D), jnp.float32) * inv_d, 'Wk': jax.random.normal(ks[2], (G * HD, D), jnp.float32) * inv_d, 'Wv': jax.random.normal(ks[3], (G * HD, D), jnp.float32) * inv_d, 'Wo': jax.random.normal(ks[4], (D, H * HD), jnp.float32) * inv_d, 'q_norm_scale': jax.random.normal(ks[5], (HD,), jnp.float32) * 0.02, 'k_norm_scale': jax.random.normal(ks[6], (HD,), jnp.float32) * 0.02, 'k_blocks': jax.random.normal(ks[7], (B * NBLK, G, BLOCK, HD), jnp.float32), 'v_blocks': jax.random.normal(ks[8], (B * NBLK, G, BLOCK, HD), jnp.float32), 'block_tables': jnp.arange(B * NBLK, dtype=jnp.int32).reshape(B, NBLK), 'kv_lens': jax.random.randint(ks[9], (B,), 0, 512, dtype=jnp.int32)}
    _L2_cond_all = _L2_cond_setup()
    _L2_cond_in = {k: v for k, v in _L2_cond_all.items() if k in ('Wq', 'Wk', 'Wv', 'Wo', 'q_norm_scale', 'k_norm_scale', 'k_blocks', 'v_blocks')}
    del _L2_cond_all

    def _L3_cond_setup():
        import jax, jax.numpy as jnp
        import numpy as np
        B, T, D_IN, D_OUT = (16, 256, 256, 256)
        N_ADAPTERS, RANK = (8, 16)
        key = jax.random.key(seed)
        k_x, k_w, k_a, k_b, k_s, k_idx = jax.random.split(key, 6)
        x = jax.random.normal(k_x, (B, T, D_IN), dtype=jnp.float32)
        W = jax.random.normal(k_w, (D_OUT, D_IN), dtype=jnp.float32) * (1.0 / np.sqrt(D_IN))
        A = jax.random.normal(k_a, (N_ADAPTERS, RANK, D_IN), dtype=jnp.float32) * 0.02
        Bm = jax.random.normal(k_b, (N_ADAPTERS, D_OUT, RANK), dtype=jnp.float32) * 0.02
        scalings = jnp.ones((N_ADAPTERS,), dtype=jnp.float32)
        adapter_idx = jax.random.randint(k_idx, (B,), 0, N_ADAPTERS, dtype=jnp.int32)
        return {'x': x, 'W': W, 'A': A, 'Bm': Bm, 'scalings': scalings, 'adapter_idx': adapter_idx}
    _L3_cond_all = _L3_cond_setup()
    _L3_cond_in = {k: v for k, v in _L3_cond_all.items() if k in ('W', 'A', 'Bm', 'scalings')}
    del _L3_cond_all
    return {'x': x, 'itok_B_0_7': itok_B_0_7, 'itok_B_1_198': itok_B_1_198, 'itok_Bx257_0_4111': itok_Bx257_0_4111, 'itok_B_37_3939': itok_B_37_3939, 'itok_B_0_6': itok_B_0_6, 'L0_cond_weights': _L0_cond_in['weights'], 'L1_cond_weights': _L1_cond_in['weights'], 'L2_cond_Wq': _L2_cond_in['Wq'], 'L2_cond_Wk': _L2_cond_in['Wk'], 'L2_cond_Wv': _L2_cond_in['Wv'], 'L2_cond_Wo': _L2_cond_in['Wo'], 'L2_cond_q_norm_scale': _L2_cond_in['q_norm_scale'], 'L2_cond_k_norm_scale': _L2_cond_in['k_norm_scale'], 'L2_cond_k_blocks': _L2_cond_in['k_blocks'], 'L2_cond_v_blocks': _L2_cond_in['v_blocks'], 'L3_cond_W': _L3_cond_in['W'], 'L3_cond_A': _L3_cond_in['A'], 'L3_cond_Bm': _L3_cond_in['Bm'], 'L3_cond_scalings': _L3_cond_in['scalings']}

def reference(x, itok_B_0_7, itok_B_1_198, itok_Bx257_0_4111, itok_B_37_3939, itok_B_0_6, L0_cond_weights, L1_cond_weights, L2_cond_Wq, L2_cond_Wk, L2_cond_Wv, L2_cond_Wo, L2_cond_q_norm_scale, L2_cond_k_norm_scale, L2_cond_k_blocks, L2_cond_v_blocks, L3_cond_W, L3_cond_A, L3_cond_Bm, L3_cond_scalings):
    import jax
    import jax.numpy as jnp

    def _L0_cond_ref(x, subjects, weights):
        import jax, jax.numpy as jnp
        import numpy as np
        B, C, D, T, N_SUBJECTS = (128, 32, 32, 256, 8)
        w = weights[subjects]
        out = jnp.einsum('bct,bcd->bdt', x, w)
        return out

    def _L1_cond_ref(x, conditions, weights):
        import jax, jax.numpy as jnp
        import numpy as np
        B, C, T = (128, 32, 256)
        S, D = (200, 32)
        w = weights[conditions]
        return jnp.einsum('bct,bcd->bdt', x, w)

    def _L2_cond_ref(x, Wq, Wk, Wv, Wo, q_norm_scale, k_norm_scale, k_blocks, v_blocks, block_tables, kv_lens):
        import jax, jax.numpy as jnp
        import numpy as np
        H, G, HD = (8, 4, 32)
        GSZ = H // G
        BLOCK = 16
        WINDOW = 128
        SCALE = 256.0 ** (-0.5)
        EPS = 1e-06
        THETA = 10000.0
        B, T, D = (16, 4, 256)
        NBLK = 257

        def _rms(x, scale):
            var = jnp.mean(x * x, axis=-1, keepdims=True)
            return x * jax.lax.rsqrt(var + EPS) * (1.0 + scale)

        def _rope(x, pos):
            half = HD // 2
            inv = 1.0 / THETA ** (jnp.arange(half, dtype=jnp.float32) / half)
            ang = pos[:, :, None].astype(jnp.float32) * inv
            cos = jnp.cos(ang)[:, None, :, :]
            sin = jnp.sin(ang)[:, None, :, :]
            x1, x2 = (x[..., :half], x[..., half:])
            return jnp.concatenate([x1 * cos - x2 * sin, x2 * cos + x1 * sin], axis=-1)
        Bx, Tx, _ = x.shape
        q = jnp.einsum('btd,od->bto', x, Wq).reshape(Bx, Tx, H, HD).transpose(0, 2, 1, 3)
        k = jnp.einsum('btd,od->bto', x, Wk).reshape(Bx, Tx, G, HD).transpose(0, 2, 1, 3)
        v = jnp.einsum('btd,od->bto', x, Wv).reshape(Bx, Tx, G, HD).transpose(0, 2, 1, 3)
        q = _rms(q, q_norm_scale)
        k = _rms(k, k_norm_scale)
        pos = kv_lens[:, None] + jnp.arange(Tx, dtype=jnp.int32)
        q = _rope(q, pos)
        k = _rope(k, pos)
        slot = pos // BLOCK
        off = pos % BLOCK
        blk = jnp.take_along_axis(block_tables, slot, axis=1)
        k_blocks = k_blocks.at[blk, :, off, :].set(k.transpose(0, 2, 1, 3))
        v_blocks = v_blocks.at[blk, :, off, :].set(v.transpose(0, 2, 1, 3))
        k_all = k_blocks[block_tables].transpose(0, 2, 1, 3, 4).reshape(Bx, G, -1, HD)
        v_all = v_blocks[block_tables].transpose(0, 2, 1, 3, 4).reshape(Bx, G, -1, HD)
        S = k_all.shape[2]
        qg = q.reshape(Bx, G, GSZ, Tx, HD)
        scores = jnp.einsum('bghtd,bgsd->bghts', qg, k_all) * SCALE
        kpos = jnp.arange(S, dtype=jnp.int32)
        allowed = (kpos[None, None, :] <= pos[:, :, None]) & (kpos[None, None, :] > pos[:, :, None] - WINDOW)
        scores = jnp.where(allowed[:, None, None, :, :], scores, -jnp.inf)
        p = jax.nn.softmax(scores, axis=-1)
        o = jnp.einsum('bghts,bgsd->bghtd', p, v_all).reshape(Bx, H, Tx, HD)
        o = o.transpose(0, 2, 1, 3).reshape(Bx, Tx, H * HD)
        return jnp.einsum('bto,do->btd', o, Wo)

    def _L3_cond_ref(x, W, A, Bm, scalings, adapter_idx):
        import jax, jax.numpy as jnp
        import numpy as np
        B, T, D_IN, D_OUT = (16, 256, 256, 256)
        N_ADAPTERS, RANK = (8, 16)
        H = jnp.einsum('btd,od->bto', x, W)
        A_b = A[adapter_idx]
        B_b = Bm[adapter_idx]
        s_b = scalings[adapter_idx]
        xa = jnp.einsum('btd,brd->btr', x, A_b)
        delta = jnp.einsum('btr,bor->bto', xa, B_b)
        delta = jax.lax.stop_gradient(delta * s_b[:, None, None])
        return H + delta
    x = x + _L0_cond_ref(x, itok_B_0_7, L0_cond_weights)
    x = x + _L1_cond_ref(x, itok_B_1_198, L1_cond_weights)
    x = x + _L2_cond_ref(x, L2_cond_Wq, L2_cond_Wk, L2_cond_Wv, L2_cond_Wo, L2_cond_q_norm_scale, L2_cond_k_norm_scale, L2_cond_k_blocks, L2_cond_v_blocks, itok_Bx257_0_4111, itok_B_37_3939)
    x = x + _L3_cond_ref(x, L3_cond_W, L3_cond_A, L3_cond_Bm, L3_cond_scalings, itok_B_0_6)
    return x

_drawn_inputs = setup_inputs


def setup_inputs(seed=0):
    import zlib

    import numpy as np

    out = dict(_drawn_inputs(seed))
    spreads = {'L3_cond_scalings': (1.0, 0.6)}
    factors = {'L2_cond_q_norm_scale': 8.0,
     'L2_cond_k_norm_scale': 64.0,
     'L2_cond_k_blocks': 4.887,
     'L3_cond_A': 2.965,
     'L3_cond_Bm': 2.966,
     'L2_cond_Wk': 4.348}
    for name, (base, spread) in spreads.items():
        noise = np.random.default_rng([zlib.crc32(name.encode()), seed]).standard_normal(out[name].shape)
        drawn = base * np.exp(spread * noise) if base else spread * noise
        out[name] = jnp.asarray(drawn.astype(out[name].dtype))
    for name, factor in factors.items():
        out[name] = (out[name] * factor).astype(out[name].dtype)
    return out
```

```python
from contextlib import ExitStack

import numpy as np

import concourse.bass as bass
from concourse import mybir

ALU = mybir.AluOpType
ACT = mybir.ActivationFunctionType
F32 = mybir.dt.float32
BF16 = mybir.dt.bfloat16
I32 = mybir.dt.int32
AX_X = mybir.AxisListType.X

P = 128
SEQS = 128
ROWS = 32
FEAT = 256
TILES = 32
SPT = 4
HEADS, KVH, HD = 8, 4, 32
BLOCK = 16
BLKW = KVH * BLOCK * HD
NBLOCKS = 16 * 257
SLOTS = 257
WINDOW = 128
WB = 11
WS = 12
SPG = 8
GROUPS = SEQS // SPG
GR = SPG * WS
KEYS = WB * BLOCK
HALF = KEYS // 2
ENT = 3 * SEQS
FIRST_ENT = WINDOW // BLOCK
SKIP = 65536
ADAPTERS, RANK = 8, 16
UNITS = 12
UNITS_AT = ((0, 1), (2, 3), (4, 5), (6, 7), (8,), (9,), (10,), (11,))
NEG = -1.0e30
EPS = 1e-6
MAGIC = 12582912.0
TWO_PI = 6.283185307179586
PI2_HI = 6.28125
PI2_MID = float(np.float32(round((TWO_PI - PI2_HI) * 2**21) / 2**21))
PI2_LO = TWO_PI - PI2_HI - PI2_MID


class Chain:

    def __init__(self, engine, sem):
        self.engine, self.sem, self.base, self.n = engine, sem, 0, 0

    def mark(self, instruction):
        instruction.then_inc(self.sem, 1)
        self.n += 1

    def wait(self):
        self.engine.wait_ge(self.sem, self.base + self.n)

    def link(self, instruction):
        self.mark(instruction)
        self.wait()

    def start(self, base):
        self.base, self.n = base, 0


def spread(ap, axis, n):
    ap = ap.unsqueeze(axis)
    shape = list(ap.shape)
    shape[axis] = n
    return ap.broadcast_to(shape)


def drop(ap):
    return ap.rearrange("p o n -> p (o n)")


def wait_from(engine, sem, value):
    if isinstance(value, int) and value <= 0:
        return
    engine.wait_ge(sem, value)


def build(nc, x, subj, cond, table, lens, adapt, w0, w1, wq, wk, wv, wo, qns, kns, kblk, vblk,
          w3, la, lb, lsc, out):
    with ExitStack() as ctx:
        ctx.enter_context(nc.allow_non_contiguous_dma(reason="index columns and adapter factors"))

        def sb(name, shape, dt=F32):
            return ctx.enter_context(nc.sbuf_tensor(name, shape, dt))

        def sem(name):
            return ctx.enter_context(nc.semaphore(name))

        def dram(name, shape, dt=F32):
            return nc.dram_tensor(name, shape, dt).ap()

        d_mix = dram("mix_scratch", [2, SEQS, ROWS * ROWS])
        d_ent = dram("entry_scratch", [SEQS, 3])
        d_win = dram("window_scratch", [2, SEQS, WS], I32)
        d_row = dram("row_scratch", [SEQS, ROWS], I32)
        d_new = dram("new_scratch", [ENT * BLOCK, 2 * KVH * HD])
        d_k2 = dram("patched_k", [ENT, BLKW])
        d_v2 = dram("patched_v", [ENT, BLKW])

        xres = sb("xres", [P, TILES, FEAT])
        qtres = sb("qtres", [P, TILES, 256])
        block_in = sb("block_in", [P, 2, 2, BLKW])
        r1 = sb("window", [P, 2 * 1536 + 1536 + 2 * 2048])
        region = r1[:, 0:2 * 4096].rearrange("p (a n) -> p a n", a=2)
        rp = sb("rope", [P, TILES * 4 * HD])
        rope = rp[:].rearrange("p (t w d) -> p t w d", w=4, d=HD)
        ident = sb("ident", [P, P])
        wqkvT = sb("wqkvT", [P, 2, 512])
        woT = sb("woT", [P, 2, 256])
        w3T = sb("w3T", [P, 2, 256])
        laT = sb("laT", [P, 2, P])
        lbT = sb("lbT", [P, 256])
        mixw = sb("mixw", [P, 2, TILES, ROWS])
        bdmask = sb("bdmask", [P, SPT, ROWS])
        maskA = sb("maskA", [96, SEQS, ROWS], BF16)
        maskB = sb("maskB", [96, BLOCK, WB], BF16)
        mask4 = sb("mask4", [96, 2, SPT, P], BF16)
        admask = sb("admask", [P, SEQS])
        rowidx = sb("rowidx", [P, TILES], I32)
        winidx = sb("winidx", [GR, 2, GROUPS], I32)
        rowcol = sb("rowcol", [P, 2], I32)
        wincol = sb("wincol", [GR, 2], I32)

        kT = r1[:, 0:2 * 1536].rearrange("p (u o r) -> p u o r", u=2, r=GR)
        vT = r1[:, 3072:3072 + SPG * KEYS].rearrange("p (b k) -> p b k", b=SPG)
        vnat = r1[:, 4608:4608 + 4096].rearrange("p (u n) -> p u n", u=2)

        q1 = qtres[:].rearrange("p a n -> p (a n)")
        used = [0]

        def tmp(n, dt=F32):
            a = q1[:, used[0]:used[0] + n]
            used[0] += n
            return a if dt == F32 else a.bitcast(dt)

        eqall = tmp(WB * ENT)
        bounds = tmp(2 * ENT)
        blk_bc = tmp(ENT)
        e_plus = tmp(ENT)
        v_upper = tmp(ENT)
        v_lower = tmp(ENT)
        rel = tmp(SLOTS)
        tabf = tmp(SLOTS)
        junk = tmp(SLOTS)

        tabi = tmp(SLOTS, I32)
        leni = sb("leni", [P, 1], I32)
        remi = sb("remi", [P, 1], I32)
        lens_bc = sb("lens_bc", [P, SEQS], I32)
        rem_bci = sb("rem_bci", [P, SEQS], I32)
        lent = sb("lent", [P, TILES], I32)
        adapt_bc = sb("adapt_bc", [P, SEQS], I32)
        mixi = sb("mixi", [P, 2], I32)
        sc_bc = sb("sc_bc", [P, ADAPTERS])
        ns_bc = sb("ns_bc", [P, 2, HD])
        idf = sb("idf", [P, 24])
        rem_bc = sb("rem_bc", [P, SEQS])
        len_f = sb("len_f", [P, SEQS])
        start_bc = sb("start_bc", [P, SEQS])
        blkw = sb("blkw", [P, WS])
        entf = sb("entf", [P, WS])
        enti = sb("enti", [P, 3], I32)
        own = sb("own", [P, 3])
        ub = sb("ub", [P, 3])
        lo = sb("lo", [P, 3])
        difs = sb("difs", [P, 3, 2])
        tok = sb("tok", [P, 12, ROWS])
        rows_i = sb("rows_i", [P, ROWS], I32)
        win_i = sb("win_i", [P, 2, WS], I32)
        pidx = sb("pidx", [P, 4], I32)
        pf = sb("pf", [P, 4])
        ad_f = sb("ad_f", [P, SEQS])
        kmt = sb("kmt", [64, ROWS])
        negk = sb("negk", [P, 1])
        iota8 = sb("iota8", [P, ADAPTERS])
        iotat = sb("iotat", [P, ROWS])
        j8 = sb("j8", [P, ADAPTERS])
        invf = sb("invf", [P, 16])
        pos = sb("pos", [P, TILES])
        nscale = sb("nscale", [P, 2, 2, HD])
        halfpi = sb("halfpi", [P, 1])
        gates = sb("gates", [1, 4])
        epsb = sb("epsb", [P, 1])
        ang = r1[:, 0:512].rearrange("p (t j) -> p t j", j=16)
        kq = r1[:, 512:1024].rearrange("p (t j) -> p t j", j=16)
        cosb = r1[:, 1024:1536].rearrange("p (t j) -> p t j", j=16)
        sinb = r1[:, 1536:2048].rearrange("p (t j) -> p t j", j=16)

        wraw = block_in[:, 1].rearrange("p a n -> p (a n)")
        wqkv_raw = wraw[:, 0:1024].rearrange("p (o f) -> p o f", o=4)
        wo_raw = wraw[:, 1024:1536].rearrange("p (o f) -> p o f", o=2)
        w3_raw = wraw[:, 1536:2048].rearrange("p (o f) -> p o f", o=2)
        la_raw = wraw[:, 2048:2304]
        lb_raw = wraw[:, 2304:2560].rearrange("p (c n) -> p c n", c=2)
        mix_raw = r1[:, 2048:4096].rearrange("p (l n) -> p l n", l=2)

        wbd = sb("wbd", [P, 2, 2, SPT * ROWS])
        x1s = sb("x1s", [P, 2, FEAT])
        x2s = sb("x2s", [P, 2, FEAT])
        x2T = sb("x2T", [P, 2, 2, P])
        early = sb("early", [P, 4, 2, 384])
        sq, qn, rc, rs = (early[:, k] for k in range(4))
        ss = sb("ss", [P, 2, 12])
        sd = sb("sd", [P, 2, 12])
        ri = sb("ri", [P, 2, 12])
        stage = sb("stage", [P, 2, 512])

        qbd = rp[:, 0:2048].rearrange("p (a b c q) -> p a b c q", a=2, b=SPT, c=2)
        prob = rp[:, 2048:2048 + 4 * KEYS].rearrange("p (a c k) -> p a c k", a=2, c=2)
        negm = sb("negm", [P, 2, 2])
        sums = sb("sums", [P, 2, SPT, 2])
        rinv = sb("rinv", [P, SPT, 2])
        probT = rp[0:HALF, 3072:4096].rearrange("p (a h c q) -> p a h c q", a=2, h=2, c=2)
        e1 = early[:].rearrange("p a b n -> p (a b n)")
        osb = e1[:, 0:256].rearrange("p (c b d) -> p c b d", c=2, b=SPT)
        oT = e1[:, 256:512].rearrange("p (c n) -> p c n", c=2)
        x3s = e1[:, 512:768]
        x3T = e1[:, 768:1024].rearrange("p (c n) -> p c n", c=2)
        xam = e1[:, 1024:1152]
        ys = e1[:, 1152:1664].rearrange("p (a n) -> p a n", a=2)

        ps = [ctx.enter_context(nc.psum_tensor(f"bank{i}", [P, 512], F32)) for i in range(8)]
        psMix, psT, psQKV = [ps[0], ps[1]], [ps[2], ps[3]], [ps[4], ps[5]]
        psS = [ps[0], ps[1]]
        psP = [ps[2], ps[3]]
        psR = [ps[4], ps[5]]
        psO, psZ = ps[6], ps[7]

        s = {n: sem(n) for n in (
            "ld_idx", "ld_w", "ld_x", "consts", "mix_col", "mix_gather", "mix_store", "mix_load",
            "ent_out", "ent_bc", "win_out", "win_in", "row_out", "row_in", "ent_idx", "angles", "trig",
            "blk_in0", "blk_in1", "blk_re", "blk_st0", "blk_st1", "wt_pe", "wt_ev", "pool_chain", "dve_chain",
            "wbd", "l0", "x1", "l1", "x2", "xcopy", "xt", "xte", "qkv", "square", "sumsq", "root", "norm",
            "swap", "roped", "vcopy", "qt", "qte", "scat0", "scat1",
            "pk_in0", "pk_in1", "pk_out0", "pk_out1", "raw_v", "raw_k",
            "scores", "negmax", "expd", "pt", "pte", "pv", "unit", "unite", "qbd", "oev", "oT", "win_idx", "row_idx", "pk_rek", "turned", "mask4", "qzero", "masks", "pk_rev",
            "wo", "x3", "x3t", "x3te", "xa", "xam", "l3", "y", "out0", "out1")}
        s_scat = [s["scat0"], s["scat1"]]
        s_out = [s["out0"], s["out1"]]
        s_blk_in, s_blk_st = [s["blk_in0"], s["blk_in1"]], [s["blk_st0"], s["blk_st1"]]
        s_pk_in, s_pk_out = [s["pk_in0"], s["pk_in1"]], [s["pk_out0"], s["pk_out1"]]
        N_IDX, N_W = 14, 16

        d_new_blocks = d_new.rearrange("(b s t) n -> s b (t n)", s=3, t=BLOCK)
        k2_by = d_k2.rearrange("(b s) n -> s b n", s=3)
        v2_by = d_v2.rearrange("(b s) n -> s b n", s=3)
        kflat = kblk.rearrange("n g t d -> n (g t d)")
        vflat = vblk.rearrange("n g t d -> n (g t d)")

        def col(v):
            return v.rearrange("(b o) -> b o", o=1)

        def bcast(v, n):
            return v.partition_broadcast(n)

        block = ctx.enter_context(nc.Block())

        @block.sync
        def _(sp):
            il = s["ld_idx"]
            sp.dma_start(mixi[:, 0:1], col(subj)).then_inc(il, 16)
            sp.dma_start(mixi[:, 1:2], col(cond)).then_inc(il, 16)
            sp.dma_start(leni[:], col(lens)).then_inc(il, 16)
            sp.dma_start(tabi, table).then_inc(il, 16)
            sp.dma_start(lens_bc[:], bcast(lens, P)).then_inc(il, 16)
            for b in range(SPT):
                sp.dma_start(lent[32 * b:32 * b + 32, :],
                             lens.rearrange("(t b) -> b t", b=SPT)[b].partition_broadcast(ROWS)).then_inc(il, 16)
            sp.dma_start(adapt_bc[:], bcast(adapt, P)).then_inc(il, 16)
            sp.dma_start(sc_bc[:], bcast(lsc, P)).then_inc(il, 16)
            sp.dma_start(ns_bc[:, 0, :], bcast(qns, P)).then_inc(il, 16)
            sp.dma_start(ns_bc[:, 1, :], bcast(kns, P)).then_inc(il, 16)
            sp.dma_start(la_raw, la.rearrange("a r f -> (a r) f")).then_inc(il, 16)
            wl = s["ld_w"]
            for o in range(2):
                for h in range(KVH):
                    sp.dma_start(wqkv_raw[HD * h:HD * h + HD, o, :],
                                 wq[HD * (2 * h + o):HD * (2 * h + o) + HD, :]).then_inc(wl, 16)
                sp.dma_start(wo_raw[:, o, :], wo[P * o:P * o + P, :]).then_inc(wl, 16)
                sp.dma_start(w3_raw[:, o, :], w3[P * o:P * o + P, :]).then_inc(wl, 16)
                sp.dma_start(lb_raw[:, o, :].rearrange("p (a r) -> p a r", a=ADAPTERS),
                             lb[:, P * o:P * o + P, :].rearrange("a o r -> o a r")).then_inc(wl, 16)
            sp.dma_start(wqkv_raw[:, 2, :], wk).then_inc(wl, 16)
            sp.dma_start(wqkv_raw[:, 3, :], wv).then_inc(wl, 16)
            sp.dma_start(xres[:], x.rearrange("(t b) c f -> (b c) t f", b=SPT)).then_inc(s["ld_x"], 16)
            sp.wait_ge(s["mix_gather"], 32)
            sp.dma_start(d_mix.rearrange("l b n -> b l n"), mix_raw).then_inc(s["mix_store"], 16)
            sp.wait_ge(s["mix_store"], 16)
            for l in range(2):
                sp.dma_start(mixw[:, l, :, :], d_mix[l].rearrange("(t b) (c d) -> (b c) t d", b=SPT, d=ROWS)
                             ).then_inc(s["mix_load"], 16)
            sp.wait_ge(s["ent_idx"], 1)
            sp.dma_start(d_ent, blkw[:, FIRST_ENT:FIRST_ENT + 3]).then_inc(s["ent_out"], 16)
            sp.wait_ge(s["ent_out"], 16)
            sp.dma_start(blk_bc, d_ent.rearrange("b s -> (b s)").partition_broadcast(P)).then_inc(s["ent_bc"], 16)
            sp.wait_ge(s["row_idx"], 1)
            sp.dma_start(d_row, rows_i[:]).then_inc(s["row_out"], 16)
            sp.wait_ge(s["win_idx"], 2)
            sp.dma_start(d_win.rearrange("k b i -> b k i"), win_i[:]).then_inc(s["win_out"], 16)
            sp.wait_ge(s["row_out"], 16)
            sp.dma_start(rowidx[:], d_row.rearrange("(t b) c -> (b c) t", b=SPT)).then_inc(s["row_in"], 16)
            sp.wait_ge(s["win_out"], 16)
            for k in range(2):
                sp.dma_start(winidx[:, k, :], d_win[k].rearrange("(g b) i -> (b i) g", b=SPG)).then_inc(s["win_in"], 16)
            for e in range(3):
                sp.wait_ge(s["blk_re"], 2 * e + 2)
                sp.dma_start(d_new_blocks[e], region[:, e % 2, :]).then_inc(s_blk_st[e % 2], 16)
            for e in range(3):
                if e == 0:
                    sp.wait_ge(s_scat[0], 16 * TILES // 2)
                    sp.wait_ge(s_scat[1], 16 * TILES // 2)
                if e == 2:
                    sp.wait_ge(s["pk_rek"], 1)
                    sp.wait_ge(s["pk_rev"], 1)
                sp.dma_start(region[:, e % 2, :], d_new_blocks[e]).then_inc(s_pk_in[e % 2], 16)
            for e in range(3):
                sp.wait_ge(s["pk_rek"], e + 1)
                sp.wait_ge(s["pk_rev"], e + 1)
                sp.dma_start(k2_by[e], block_in[:, e % 2, 0, :]).then_inc(s_pk_out[e % 2], 16)
                sp.dma_start(v2_by[e], block_in[:, e % 2, 1, :]).then_inc(s_pk_out[e % 2], 16)

            def store(m, par):
                sp.wait_ge(s["y"], m + 1)
                sp.dma_start(out.rearrange("(t b) c f -> t (b c) f", b=SPT)[bass.ds(m, 1)].rearrange("t p f -> p (t f)"),
                             ys[:, par, :]).then_inc(s_out[par], 16)

            with sp.Fori(0, TILES // 2) as i:
                store(i * 2, 0)
                store(i * 2 + 1, 1)
            sp.wait_ge(s_out[0], 16 * TILES // 2)
            sp.wait_ge(s_out[1], 16 * TILES // 2)

        @block.gpsimd
        def _(pool):
            ch = Chain(pool, s["pool_chain"])
            g = nc.gpsimd
            kw = dict(allow_small_or_imprecise_dtypes=True)
            pool.wait_ge(s["ld_idx"], 16 * N_IDX)
            for l, w in ((0, w0), (1, w1)):
                g.indirect_dma_start(mix_raw[:, l, :], None, w.rearrange("n c d -> n (c d)"),
                                     bass.IndirectOffsetOnAxis(ap=mixi[:, l:l + 1], axis=0),
                                     bounds_check=w.shape[0] - 1, oob_is_err=False).then_inc(s["mix_gather"], 16)
            g.iota(rel, pattern=[[1, SLOTS]], base=0, channel_multiplier=0, **kw)
            g.iota(e_plus, pattern=[[1, ENT]], base=1, channel_multiplier=0, **kw)
            g.iota(own[:], pattern=[[1, 3]], base=1, channel_multiplier=3, **kw)
            g.iota(pidx[:, 0:1], pattern=[[0, 1]], base=0, channel_multiplier=1)
            g.iota(kmt[:], pattern=[[-1, ROWS]], base=0, channel_multiplier=1, **kw)
            g.iota(iota8[:], pattern=[[1, ADAPTERS]], base=0, channel_multiplier=0, **kw)
            g.iota(iotat[:], pattern=[[1, ROWS]], base=0, channel_multiplier=0, **kw)
            g.memset(v_upper.rearrange("p (b s) -> p b s", s=3)[:, :, 1:2], 99.0)
            g.memset(v_upper.rearrange("p (b s) -> p b s", s=3)[:, :, 2:3], 0.0)
            g.memset(v_lower.rearrange("p (b s) -> p b s", s=3)[:, :, 0:2], 0.0)
            g.memset(halfpi[:], TWO_PI / 4)
            g.memset(epsb[:], EPS)
            for j in range(16):
                g.memset(invf[:, j:j + 1], float(np.float32(1.0) / np.float32(10000.0 ** (j / 16))))
            ch.mark(g.memset(ident[:], 0.0))
            ch.mark(g.memset(bdmask[:], 1.0))
            ch.link(g.memset(maskB[:], 0.0))
            ch.mark(g.affine_select(out=ident[:], in_=ident[:], compare_op=ALU.not_equal, fill=1.0, base=0,
                                    pattern=[[-1, P]], channel_multiplier=1))
            ch.mark(g.affine_select(out=bdmask[:], in_=bdmask[:], compare_op=ALU.is_ge, fill=0.0, base=0,
                                    pattern=[[-ROWS, SPT], [0, ROWS]], channel_multiplier=1))
            ch.link(g.affine_select(out=maskB[0:64], in_=maskB[0:64], compare_op=ALU.is_ge, fill=NEG, base=-1,
                                    pattern=[[1, BLOCK], [BLOCK, WB]], channel_multiplier=-1))
            ch.mark(g.affine_select(out=maskB[0:64], in_=maskB[0:64], compare_op=ALU.is_ge, fill=NEG, base=WINDOW,
                                    pattern=[[-1, BLOCK], [-BLOCK, WB]], channel_multiplier=1))
            ch.link(g.affine_select(out=bdmask[:], in_=bdmask[:], compare_op=ALU.is_ge, fill=0.0, base=ROWS - 1,
                                    pattern=[[ROWS, SPT], [0, ROWS]], channel_multiplier=-1))
            gates_set = g.memset(gates[:], 0.0)
            gates_set.then_inc(s["consts"], 1)
            pool.wait_ge(s["mix_gather"], 32)
            pool.wait_ge(s["consts"], 1)
            ch.mark(g.iota(negk[64:96, :], pattern=[[0, 1]], base=0, channel_multiplier=-1, **kw))
            ch.link(g.affine_select(out=maskB[64:96], in_=maskB[64:96], compare_op=ALU.not_equal, fill=NEG, base=0,
                                    pattern=[[0, BLOCK], [1, WB]], channel_multiplier=-1))
            g.memset(gates[:], 0.0).then_inc(s["masks"], 1)

            pool.wait_ge(s["ent_idx"], 1)

            def entry_gather(e):
                for kv, src in enumerate((kflat, vflat)):
                    g.indirect_dma_start(block_in[:, e % 2, kv, :], None, src,
                                         bass.IndirectOffsetOnAxis(ap=enti[:, e:e + 1], axis=0),
                                         bounds_check=NBLOCKS - 1, oob_is_err=False).then_inc(s_blk_in[e % 2], 16)

            entry_gather(0)
            pool.wait_ge(s["wt_pe"], 5)
            entry_gather(1)
            pool.wait_ge(s["blk_re"], 2)
            entry_gather(2)

            def gate():
                ch.wait()
                ch.mark(g.tensor_tensor(gates[0:1, 0:1], gates[0:1, 1:2], gates[0:1, 2:3], ALU.add))

            def mix_weights(n, j):
                wait_from(pool,  s["l1"], n - 1)
                for l in range(2):
                    ins = g.tensor_tensor(wbd[:, j, l, :].rearrange("p (b d) -> p b d", b=SPT),
                                          spread(drop(mixw[:, l, bass.ds(n, 1), :]), 1, SPT),
                                          bdmask[:], ALU.mult)
                ins.then_inc(s["wbd"], 1)

            def keep_x(n, j):
                pool.wait_ge(s["x2"], n + 1)
                g.tensor_copy(xres[:, bass.ds(n, 1), :].rearrange("p t f -> p (t f)"), x2s[:, j, :]).then_inc(s["xcopy"], 1)

            def swap(n, j):
                pool.wait_ge(s["norm"], n + 1)
                wait_from(pool,  s["roped"], n - 1)
                src = qn[:, j, :].rearrange("p (h u d) -> p h u d", u=2, d=16)
                dst = rs[:, j, :].rearrange("p (h u d) -> p h u d", u=2, d=16)
                for a, b, w in ((0, 8, 1), (8, 12, 3)):
                    for u in range(2):
                        ins = g.tensor_tensor(dst[:, a:b, u, :], src[:, a:b, 1 - u, :],
                                              spread(drop(rope[:, bass.ds(n, 1), w, 16 * u:16 * u + 16]), 1, b - a), ALU.mult)
                ins.then_inc(s["swap"], 1)

            def scatter(n, j, first):
                if not first:
                    pool.wait_ge(s_scat[j], (n - j) * 8)
                ch.link(g.tensor_copy(rowcol[:, j:j + 1], rowidx[:, bass.ds(n, 1)]))
                pool.wait_ge(s["roped"], n + 1)
                pool.wait_ge(s["vcopy"], n + 1)
                gate()
                g.indirect_dma_start(d_new, bass.IndirectOffsetOnAxis(ap=rowcol[:, j:j + 1], axis=0),
                                     stage[:, j, 256:512], None, bounds_check=ENT * BLOCK - 1, oob_is_err=False
                                     ).then_inc(s_scat[j], 16)

            def part2(i, first, nxt):
                if nxt:
                    mix_weights(i * 2 + 2, 0)
                    mix_weights(i * 2 + 3, 1)
                for j in range(2):
                    swap(i * 2 + j, j)
                if nxt:
                    for j in range(2):
                        keep_x(i * 2 + 2 + j, j)
                if first:
                    pool.wait_ge(s["row_in"], 16)
                    pool.wait_ge(s_blk_st[0], 32)
                    pool.wait_ge(s_blk_st[1], 16)
                for j in range(2):
                    scatter(i * 2 + j, j, first)

            pool.wait_ge(s["mix_load"], 32)
            mix_weights(0, 0)
            mix_weights(1, 1)
            pool.wait_ge(s["ld_x"], 16)
            for j in range(2):
                keep_x(j, j)
            part2(0, True, True)
            base = ch.base + ch.n
            with pool.Fori(1, TILES // 2 - 1) as i:
                ch.start(base + (i - 1) * 4)
                part2(i, False, True)
                assert ch.n == 4
            ch.start(base + 4 * (TILES // 2 - 2))
            part2(TILES // 2 - 1, False, False)

            def gather(grp):
                for k in range(2):
                    for kv, src, done in ((1, (vflat, d_v2)[k], s["raw_v"]), (0, (kflat, d_k2)[k], s["raw_k"])):
                        if k == 1:
                            pool.wait_ge(done, grp * 32 + 16)
                            gate()
                        g.indirect_dma_start(block_in[0:GR, 0, kv, :], None, src,
                                             bass.IndirectOffsetOnAxis(ap=wincol[:, k:k + 1], axis=0),
                                             bounds_check=src.shape[0] - 1, oob_is_err=False).then_inc(done, 16)

            def columns(grp):
                ch.link(g.tensor_copy(wincol[:], winidx[:, :, bass.ds(grp, 1)].rearrange("p k o -> p (k o)")))
                gate()

            def turn(grp, kv):
                pool.wait_ge(s["raw_v" if kv else "raw_k"], grp * 32 + 32)
                gate()
                g.tensor_copy(block_in[0:GR, 1, kv, :].rearrange("p (t g d) -> p t g d", t=BLOCK, g=KVH),
                              block_in[0:GR, 0, kv, :].rearrange("p (g t d) -> p t g d", g=KVH, d=HD)).then_inc(s["turned"], 1)

            def masks(m, par, first):
                if not first:
                    pool.wait_ge(s["scores"], m * 4 - 4)
                g.tensor_copy(mask4[:, par].rearrange("p b (r t) -> p b r t", r=4),
                              spread(maskA[:, bass.ds(m * SPT, SPT), :], 2, 4)).then_inc(s["mask4"], 1)

            pool.wait_ge(s["win_in"], 32)
            pool.wait_ge(s_pk_out[0], 64)
            pool.wait_ge(s_pk_out[1], 32)
            ch.link(g.memset(block_in[0:GR, 0, :, :], 0.0))
            columns(0)
            gather(0)
            pool.wait_ge(s["roped"], TILES)
            g.memset(rp[:, 0:2048], 0.0).then_inc(s["qzero"], 1)
            turn(0, 1)
            turn(0, 0)
            columns(1)
            pool.wait_ge(s["turned"], 2)
            gather(1)
            masks(0, 0, True)
            masks(1, 1, True)

            def part3(grp, more):
                pool.wait_ge(s["unit"], grp * UNITS + 4)
                turn(grp + 1, 1)
                pool.wait_ge(s["unit"], grp * UNITS + 8)
                turn(grp + 1, 0)
                if more:
                    pool.wait_ge(s["turned"], grp * 2 + 4)
                    columns(grp + 2)
                    gather(grp + 2)
                masks(grp * 2 + 2, 0, False)
                masks(grp * 2 + 3, 1, False)

            base = ch.base + ch.n
            with pool.Fori(0, GROUPS - 2) as grp:
                ch.start(base + grp * 6)
                part3(grp, True)
                assert ch.n == 6
            ch.start(base + 6 * (GROUPS - 2))
            part3(GROUPS - 2, False)

        @block.scalar
        def _(act):
            a = nc.scalar
            for n, (dst, w) in enumerate(((wqkvT[:, 0, :], 512), (wqkvT[:, 1, :], 512),
                                          (woT.rearrange("p c n -> p (c n)"), 512),
                                          (w3T[:].rearrange("p c n -> p (c n)"), 512), (None, 0))):
                act.wait_ge(s["wt_pe"], n + 1)
                if dst is not None:
                    a.copy(dst, ps[n % 2][:, 0:w]).then_inc(s["wt_ev"], 1)
                else:
                    a.copy(laT[:].rearrange("p c n -> p (c n)"), ps[n % 2][:, 0:256])
                    a.copy(lbT[:], ps[n % 2][:, 256:512]).then_inc(s["wt_ev"], 1)
            act.wait_ge(s["angles"], 1)
            a.activation(sinb, ang, ACT.Sin)
            a.activation(cosb, kq, ACT.Sin, bias=halfpi[:], scale=-1.0).then_inc(s["trig"], 1)

            for e in range(3):
                act.wait_ge(s_blk_in[e % 2], 32 * (e // 2 + 1))
                if e == 0:
                    act.wait_ge(s["trig"], 2)
                    act.wait_ge(s["mix_store"], 16)
                if e == 2:
                    act.wait_ge(s_blk_st[0], 16)
                for kv in range(2):
                    a.copy(region[:, e % 2, :].rearrange("p (t k g d) -> p k t g d", t=BLOCK, k=2, g=KVH)[:, kv],
                           block_in[:, e % 2, kv, :].rearrange("p (g t d) -> p t g d", g=KVH, d=HD)).then_inc(s["blk_re"], 1)

            def xT_out(n, j):
                act.wait_ge(s["xt"], n + 1)
                wait_from(act, s["qkv"], n - 1)
                a.copy(x2T[:, j].rearrange("p c n -> p (c n)"), psT[j][:, 0:256]).then_inc(s["xte"], 1)

            def squares(n, j):
                act.wait_ge(s["qkv"], n + 1)
                wait_from(act, s["sumsq"], n - 1)
                a.activation(sq[:, j, :], psQKV[j][:, 0:384], ACT.Square).then_inc(s["square"], 1)

            def values(n, j, i):
                wait_from(act, s_scat[j], i * 16)
                a.copy(stage[:, j, 384:512], psQKV[j][:, 384:512]).then_inc(s["vcopy"], 1)

            def root(n, j):
                act.wait_ge(s["sumsq"], n + 1)
                wait_from(act, s["norm"], n - 1)
                a.activation(sd[:, j, :], ss[:, j, :], ACT.Sqrt, bias=epsb[:], scale=1.0 / HD).then_inc(s["root"], 1)

            def qT_out(n, j):
                act.wait_ge(s["qt"], n + 1)
                a.copy(qtres[:, bass.ds(n, 1), :].rearrange("p o n -> p (o n)"), psT[j][:, 0:256]).then_inc(s["qte"], 1)

            def part2(i, nxt):
                for j in range(2):
                    squares(i * 2 + j, j)
                for j in range(2):
                    values(i * 2 + j, j, i)
                for j in range(2):
                    root(i * 2 + j, j)
                if nxt:
                    for j in range(2):
                        xT_out(i * 2 + 2 + j, j)
                for j in range(2):
                    qT_out(i * 2 + j, j)

            for j in range(2):
                xT_out(j, j)
            part2(0, True)
            with act.Fori(1, TILES // 2 - 1) as i:
                part2(i, True)
            part2(TILES // 2 - 1, False)

            for e in range(3):
                act.wait_ge(s_pk_in[e % 2], 16 * (e // 2 + 1))
                if e == 2:
                    act.wait_ge(s_pk_out[0], 32)
                a.copy(block_in[:, e % 2, 1, :].rearrange("p (g t d) -> p g t d", g=KVH, d=HD),
                       region[:, e % 2, :].rearrange("p (t k g d) -> p k g t d", t=BLOCK, k=2, g=KVH)[:, 1]).then_inc(s["pk_rev"], 1)

            def unit_out(grp, par, u):
                act.wait_ge(s["unit"], grp * UNITS + (u + 1))
                src = psR[u % 2]
                if u < 4:
                    ins = a.copy(vT[:, :, 4 * u * WB:4 * (u + 1) * WB].rearrange("p b (o i) -> p o b i", i=WB),
                                 src[:, 0:4 * GR].rearrange("p (o b i) -> p o b i", o=4, b=SPG)[:, :, :, 0:WB])
                elif u < 8:
                    if not (isinstance(grp, int) and grp < 2):
                        act.wait_ge(s["scores"], grp * SPG - SPG)
                    ins = a.copy(r1[:, bass.ds(par * 1536 + 4 * (u - 4) * GR, 4 * GR)], src[:, 0:4 * GR])
                else:
                    if not (isinstance(grp, int) and grp < 2):
                        act.wait_ge(s["pv"], grp * SPG - SPG)
                    ins = a.copy(r1[0:HALF, bass.ds(par * 2048 + (4608 + 512 * (u - 8)), 512)], src[0:HALF, :])
                ins.then_inc(s["unite"], 1)

            def exps(n, b, m, first_tiles):
                act.wait_ge(s["negmax"], n + 1)
                if not (isinstance(n, int) and n < 2):
                    act.wait_ge(s["pt"], n - 1)
                if b % 4 == 0 and not first_tiles:
                    act.wait_ge(s["oev"], m - 1)
                for c in range(2):
                    ins = a.activation(prob[:, b % 2, c, :], psS[b % 2][:, c * KEYS:(c + 1) * KEYS], ACT.Exp,
                                       bias=negm[:, b % 2, c:c + 1],
                                       accum_out=sums[:, (b // 4) % 2, b % 4, c:c + 1])
                ins.then_inc(s["expd"], 1)

            def x3T_out(m):
                act.wait_ge(s["x3t"], m + 1)
                wait_from(act, s["l3"], m)
                a.copy(x3T.rearrange("p c n -> p (c n)"), psZ[:, 256:512]).then_inc(s["x3te"], 1)

            def group(grp, first, last):
                npar = (grp + 1) % 2
                for b in range(SPG):
                    n = grp * SPG + b
                    if not (last and b == SPG - 1):
                        m = grp * 2 + (b + 1) // 4
                        exps(n + 1, (b + 1) % SPG, m, first and b + 1 < SPG)
                    if b % 4 == 2 and not (first and b < 4):
                        x3T_out(grp * 2 + (b // 4 - 1))
                    if not last:
                        for u in UNITS_AT[b]:
                            unit_out(grp + 1, npar, u)

            
            for u in range(UNITS):
                if u == 0:
                    act.wait_ge(s_pk_out[0], 64)
                    act.wait_ge(s_pk_out[1], 32)
                unit_out(0, 0, u)
            exps(0, 0, 0, True)
            group(0, True, False)
            with act.Fori(1, GROUPS - 1) as grp:
                group(grp, False, False)
            group(GROUPS - 1, False, True)
            x3T_out(TILES - 1)

        @block.vector
        def _(dve):
            v = nc.vector
            ch = Chain(dve, s["dve_chain"])
            link = ch.link
            dve.wait_ge(s["consts"], 1)
            dve.wait_ge(s["ld_idx"], 16 * N_IDX)
            ch.mark(v.tensor_scalar(remi[:], leni[:], 15, None, ALU.bitwise_and))
            ch.mark(v.tensor_scalar(rem_bci[:], lens_bc[:], 15, None, ALU.bitwise_and))
            ch.mark(v.tensor_scalar(pidx[:, 1:2], pidx[:, 0:1], 31, None, ALU.bitwise_and))
            ch.mark(v.tensor_scalar(pidx[:, 2:3], pidx[:, 0:1], 4, None, ALU.logical_shift_right))
            ch.mark(v.tensor_copy(idf[:, 3:4], leni[:]))
            ch.mark(v.tensor_copy(tabf, tabi))
            ch.mark(v.tensor_copy(len_f[:], lens_bc[:]))
            ch.mark(v.tensor_copy(pos[:], lent[:]))
            ch.mark(v.tensor_copy(ad_f[:], adapt_bc[:]))
            ch.wait()
            ch.mark(v.tensor_copy(idf[:, 0:1], remi[:]))
            ch.mark(v.tensor_copy(rem_bc[:], rem_bci[:]))
            ch.mark(v.tensor_copy(pf[:, 1:3], pidx[:, 1:3]))
            ch.wait()
            link(v.tensor_tensor(idf[:, 1:2], idf[:, 3:4], idf[:, 0:1], ALU.subtract))
            link(v.tensor_scalar(idf[:, 2:3], idf[:, 1:2], 1.0 / BLOCK, -float(FIRST_ENT), ALU.mult, ALU.add))
            link(v.tensor_scalar(rel, rel, idf[:, 2:3], None, ALU.subtract))
            for i in range(WB):
                link(v.scalar_tensor_tensor(out=junk, in0=rel, scalar=float(i), in1=tabf, op0=ALU.is_equal,
                                            op1=ALU.mult, accum_out=blkw[:, i:i + 1]))
            v.tensor_copy(enti[:], blkw[:, FIRST_ENT:FIRST_ENT + 3]).then_inc(s["ent_idx"], 1)

            link(v.tensor_scalar(pos[:], pos[:], pf[:, 1:2], None, ALU.add))
            link(v.tensor_tensor(ang, spread(pos[:], 2, 16), spread(invf[:], 1, TILES), ALU.mult))
            link(v.tensor_scalar(kq, ang, 1.0 / TWO_PI, MAGIC, ALU.mult, ALU.add))
            link(v.tensor_scalar(kq, kq, MAGIC, None, ALU.subtract))
            for c in (PI2_HI, PI2_MID, PI2_LO):
                link(v.scalar_tensor_tensor(out=ang, in0=kq, scalar=-c, in1=ang, op0=ALU.mult, op1=ALU.add))
            link(v.tensor_scalar(ang, ang, 3.1415925, -3.1415925, ALU.min, ALU.max))
            v.scalar_tensor_tensor(out=kq, in0=ang, scalar=-1.0, in1=ang, op0=ALU.mult, op1=ALU.max).then_inc(s["angles"], 1)
            ch.mark(v.tensor_scalar(nscale[:, 0, 0, :], ns_bc[:, 0, :], 1.0, float(FEAT) ** -0.5, ALU.add, ALU.mult))
            ch.mark(v.tensor_scalar(nscale[:, 1, 0, :], ns_bc[:, 1, :], 1.0, None, ALU.add))
            ch.wait()
            ch.mark(v.tensor_copy(nscale[:, :, 1, 16:32], nscale[:, :, 0, 0:16]))
            ch.mark(v.tensor_scalar(nscale[:, :, 1, 0:16], nscale[:, :, 0, 16:32], -1.0, None, ALU.mult))
            ch.wait()
            dve.wait_ge(s["trig"], 1)
            for t in range(2):
                for w, src in ((0, cosb), (1, sinb)):
                    ins = v.tensor_tensor(
                        rope[:, :, 2 * t + w, :].rearrange("p t (u d) -> p t u d", u=2),
                        spread(src, 2, 2),
                        spread(nscale[:, t, w, :].rearrange("p (u d) -> p u d", u=2), 1, TILES), ALU.mult)
            ins.then_inc(s["trig"], 1)
            link(v.scalar_tensor_tensor(out=j8[:], in0=iota8[:], scalar=pf[:, 2:3], in1=sc_bc[:], op0=ALU.is_equal,
                                        op1=ALU.mult, accum_out=pf[:, 3:4]))
            ch.mark(v.tensor_scalar(admask[:], ad_f[:], pf[:, 2:3], pf[:, 3:4], ALU.is_equal, ALU.mult))
            dve.wait_ge(s["masks"], 1)
            ch.mark(v.tensor_tensor(maskA[0:64], spread(rem_bc[0:64, :], 2, ROWS),
                                    spread(kmt[:], 1, SEQS), ALU.is_equal))
            link(v.tensor_tensor(start_bc[:], len_f[:], rem_bc[:], ALU.subtract))
            link(v.tensor_scalar(start_bc[:], start_bc[:], 1.0 / BLOCK, -float(FIRST_ENT), ALU.mult, ALU.add))
            ch.mark(v.tensor_scalar(maskA[64:96], spread(start_bc[64:96, :], 2, ROWS),
                                    negk[64:96, :], None, ALU.is_lt))
            vu = v_upper.rearrange("p (b s) -> p b s", s=3)
            vl = v_lower.rearrange("p (b s) -> p b s", s=3)
            ch.mark(v.tensor_scalar(vu[:, :, 0], rem_bc[:], -1.0, 99.0, ALU.mult, ALU.add))
            ch.mark(v.tensor_copy(vl[:, :, 2], rem_bc[:]))
            ch.wait()
            dve.wait_ge(s["ent_bc"], 16)
            eq3 = eqall.rearrange("p (i e) -> p i e", e=ENT)
            for i in range(WB):
                ch.mark(v.scalar_tensor_tensor(out=eq3[:, i, :], in0=blk_bc, scalar=blkw[:, i:i + 1], in1=e_plus,
                                               op0=ALU.is_equal, op1=ALU.mult))
            ch.wait()
            link(v.tensor_reduce(entf[:, 0:WB], eq3, axis=AX_X, op=ALU.max))
            bd = bounds.rearrange("p (k e) -> p k e", k=2)
            for e in range(3):
                for k, (tab, dst) in enumerate(((v_upper, ub), (v_lower, lo))):
                    link(v.scalar_tensor_tensor(out=bd[:, k, :], in0=eq3[:, FIRST_ENT + e, :], scalar=own[:, e:e + 1],
                                                in1=tab, op0=ALU.is_gt, op1=ALU.mult))
                    link(v.tensor_reduce(dst[:, e:e + 1], bd[:, k, :], axis=AX_X, op=ALU.max))
            link(v.tensor_scalar(ub[:], ub[:], -1.0, 99.0, ALU.mult, ALU.add))
            T = lambda k: tok[:, k, :]
            link(v.tensor_scalar(T(0), iotat[:], idf[:, 0:1], None, ALU.add))
            ch.mark(v.tensor_scalar(T(1), T(0), float(BLOCK), None, ALU.is_ge))
            ch.mark(v.tensor_scalar(T(2), T(0), float(2 * BLOCK), None, ALU.is_ge))
            for k, src in enumerate((ub[:], lo[:], entf[:, FIRST_ENT:FIRST_ENT + 3])):
                ch.mark(v.tensor_tensor(difs[:, k, :], src[:, 1:3], src[:, 0:2], ALU.subtract))
            ch.wait()
            ch.mark(v.scalar_tensor_tensor(out=T(3), in0=T(1), scalar=-float(BLOCK), in1=T(0), op0=ALU.mult, op1=ALU.add))
            for k, src in enumerate((ub[:], lo[:], entf[:, FIRST_ENT:FIRST_ENT + 3])):
                ch.mark(v.tensor_scalar(T(5 + k), T(1), difs[:, k, 0:1], src[:, 0:1], ALU.mult, ALU.add))
            ch.wait()
            ch.mark(v.scalar_tensor_tensor(out=T(4), in0=T(2), scalar=-float(BLOCK), in1=T(3), op0=ALU.mult, op1=ALU.add))
            for k in range(3):
                ch.mark(v.scalar_tensor_tensor(out=T(8 + k), in0=T(2), scalar=difs[:, k, 1:2], in1=T(5 + k),
                                               op0=ALU.mult, op1=ALU.add))
            ch.wait()
            ch.mark(v.tensor_tensor(T(0), T(4), T(8), ALU.is_lt))
            ch.mark(v.tensor_tensor(T(1), T(4), T(9), ALU.is_ge))
            ch.mark(v.tensor_scalar(T(2), T(10), float(BLOCK), float(SKIP - BLOCK), ALU.mult, ALU.add))
            ch.wait()
            ch.mark(v.tensor_tensor(T(3), T(0), T(1), ALU.mult))
            ch.mark(v.tensor_tensor(T(5), T(2), T(4), ALU.add))
            ch.wait()
            v.scalar_tensor_tensor(out=rows_i[:], in0=T(3), scalar=-float(SKIP), in1=T(5), op0=ALU.mult,
                                   op1=ALU.add).then_inc(s["row_idx"], 1)
            link(v.tensor_scalar(junk[:, 0:WB], entf[:, 0:WB], 0.0, None, ALU.is_gt))
            ch.mark(v.memset(win_i[:], SKIP))
            link(v.tensor_scalar(junk[:, 16:16 + WB], entf[:, 0:WB], float(SKIP - 1), None, ALU.add))
            v.scalar_tensor_tensor(out=win_i[:, 0, 0:WB], in0=junk[:, 0:WB], scalar=float(SKIP), in1=blkw[:, 0:WB],
                                   op0=ALU.mult, op1=ALU.add).then_inc(s["win_idx"], 1)
            v.scalar_tensor_tensor(out=win_i[:, 1, 0:WB], in0=junk[:, 0:WB], scalar=-float(SKIP), in1=junk[:, 16:16 + WB],
                                   op0=ALU.mult, op1=ALU.add).then_inc(s["win_idx"], 1)

            def add1(n, j):
                dve.wait_ge(s["l0"], n + 1)
                wait_from(dve, s["l1"], n - 1)
                v.tensor_tensor(x1s[:, j, :], xres[:, bass.ds(n, 1), :].rearrange("p o f -> p (o f)"),
                                psMix[j][:, 0:256], ALU.add).then_inc(s["x1"], 1)

            def add2(n, j):
                dve.wait_ge(s["l1"], n + 1)
                wait_from(dve, s["xt"], n - 1)
                wait_from(dve, s["xcopy"], n - 1)
                v.tensor_tensor(x2s[:, j, :], x1s[:, j, :], psMix[j][:, 0:256], ALU.add).then_inc(s["x2"], 1)

            def sumsq(n, j):
                dve.wait_ge(s["square"], n + 1)
                wait_from(dve, s["root"], n - 1)
                v.tensor_reduce(ss[:, j, :], sq[:, j, :].rearrange("p (h d) -> p h d", d=HD), axis=AX_X,
                                op=ALU.add).then_inc(s["sumsq"], 1)

            def norm(n, j):
                dve.wait_ge(s["root"], n + 1)
                ch.link(v.reciprocal(ri[:, j, :], sd[:, j, :]))
                wait_from(dve, s["swap"], n - 1)
                v.tensor_tensor(qn[:, j, :].rearrange("p (h d) -> p h d", d=HD),
                                psQKV[j][:, 0:384].rearrange("p (h d) -> p h d", d=HD),
                                spread(ri[:, j, :], 2, HD), ALU.mult
                                ).then_inc(s["norm"], 1)

            def rotate(n, j):
                dve.wait_ge(s["norm"], n + 1)
                for a_, b_, w in ((0, 8, 0), (8, 12, 2)):
                    ch.mark(v.tensor_tensor(rc[:, j, 32 * a_:32 * b_].rearrange("p (h d) -> p h d", d=HD),
                                            qn[:, j, 32 * a_:32 * b_].rearrange("p (h d) -> p h d", d=HD),
                                            spread(drop(rope[:, bass.ds(n, 1), w, :]), 1, b_ - a_), ALU.mult))

            def finish(n, j, i):
                ch.wait()
                dve.wait_ge(s["swap"], n + 1)
                wait_from(dve, s["qt"], n - 1)
                wait_from(dve, s_scat[j], i * 16)
                v.tensor_tensor(stage[:, j, 0:384], rc[:, j, :], rs[:, j, :], ALU.add).then_inc(s["roped"], 1)

            def part2(i, nxt):
                if nxt:
                    for j in range(2):
                        add1(i * 2 + 2 + j, j)
                for j in range(2):
                    sumsq(i * 2 + j, j)
                if nxt:
                    for j in range(2):
                        add2(i * 2 + 2 + j, j)
                for j in range(2):
                    norm(i * 2 + j, j)
                for j in range(2):
                    rotate(i * 2 + j, j)
                for j in range(2):
                    finish(i * 2 + j, j, i)

            dve.wait_ge(s["ld_x"], 16)
            for j in range(2):
                add1(j, j)
            for j in range(2):
                add2(j, j)
            part2(0, True)
            base = ch.base + ch.n
            with dve.Fori(1, TILES // 2 - 1) as i:
                ch.start(base + (i - 1) * 6)
                part2(i, True)
                assert ch.n == 6
            ch.start(base + 6 * (TILES // 2 - 2))
            part2(TILES // 2 - 1, False)

            for e in range(3):
                dve.wait_ge(s_pk_in[e % 2], 16 * (e // 2 + 1))
                if e == 2:
                    dve.wait_ge(s_pk_out[0], 32)
                v.tensor_copy(block_in[:, e % 2, 0, :].rearrange("p (g t d) -> p g t d", g=KVH, d=HD),
                              region[:, e % 2, :].rearrange("p (t k g d) -> p k g t d", t=BLOCK, k=2, g=KVH)[:, 0]
                              ).then_inc(s["pk_rek"], 1)

            def queries(m, par, first):
                if not first:
                    dve.wait_ge(s["scores"], m * 4 - 4)
                for h in range(KVH):
                    ins = v.tensor_copy(
                        qbd[32 * h:32 * h + 32, par, :, h // 2, 64 * (h % 2):64 * (h % 2) + 64].rearrange("p b (u t) -> p b u t", u=2),
                        qtres[32 * h:32 * h + 32, bass.ds(m, 1), :].rearrange("p o (u b t) -> p (o b) u t", u=2, b=SPT))
                    if h < KVH - 1:
                        ch.mark(ins)
                ins.then_inc(s["qbd"], 1)

            def maxes(n, b):
                dve.wait_ge(s["scores"], n + 1)
                v.tensor_reduce(negm[:, b % 2, :], psS[b % 2][:, 0:2 * KEYS].rearrange("p (c k) -> p c k", c=2),
                                axis=AX_X, op=ALU.max, negate=True).then_inc(s["negmax"], 1)

            def probT_out(n, b):
                dve.wait_ge(s["pt"], n + 1)
                if not (isinstance(n, int) and n < 2):
                    dve.wait_ge(s["pv"], n - 1)
                v.tensor_copy(probT[:, b % 2].rearrange("p a c q -> p (a c q)"), psP[b % 2][0:HALF, :]).then_inc(s["pte"], 1)

            def heads_out(m, par):
                dve.wait_ge(s["pv"], m * 4 + 4)
                ch.link(v.reciprocal(rinv[:], sums[:, par]))
                ov = psO[:].rearrange("p (b c g d) -> p g c b d", b=SPT, c=2, g=2)
                for h in range(2):
                    ins = v.tensor_tensor(osb[64 * h:64 * h + 64], ov[64 * h:64 * h + 64, h],
                                          spread(rinv[64 * h:64 * h + 64].rearrange("p b c -> p c b"), 3, HD),
                                          ALU.mult)
                    if h == 0:
                        ch.mark(ins)
                ins.then_inc(s["oev"], 1)
                dve.wait_ge(s["oev"], m + 1)
                ch.wait()
                wait_from(dve, s["wo"], m)
                v.transpose(oT.rearrange("p c n -> p (c n)"), osb.rearrange("p c b d -> p (c b d)")).then_inc(s["oT"], 1)

            def add3(m):
                dve.wait_ge(s["wo"], m + 1)
                v.tensor_tensor(x3s, xres[:, bass.ds(m, 1), :].rearrange("p o f -> p (o f)"), psZ[:, 0:256],
                                ALU.add).then_inc(s["x3"], 1)

            def adapt_in(m):
                dve.wait_ge(s["xa"], m + 1)
                v.tensor_tensor(xam.rearrange("p (b t) -> p b t", b=SPT), psZ[:, 0:P].rearrange("p (b t) -> p b t", b=SPT),
                                spread(admask[:, bass.ds(m * SPT, SPT)], 2, ROWS),
                                ALU.mult).then_inc(s["xam"], 1)

            def add4(m, par):
                dve.wait_ge(s["l3"], m + 1)
                if isinstance(m, int) and m < 2:
                    pass
                else:
                    dve.wait_ge(s_out[par], (m - par) * 8)
                v.tensor_tensor(ys[:, par, :], x3s, psZ[:, 256:512], ALU.add).then_inc(s["y"], 1)

            def group(grp, first, last):
                for b in range(SPG):
                    n = grp * SPG + b
                    if not (last and b == SPG - 1):
                        maxes(n + 1, b + 1)
                    k, t = b % 4, grp * 2 + (b // 4 - 1)
                    if k == 0:
                        if not (first):
                            add4(t - 1, b // 4)
                    elif not (first and b < 4):
                        if k == 1:
                            add3(t)
                        if k == 3:
                            adapt_in(t)
                    probT_out(n, b)
                    if k == 1 and not (last and b > 4):
                        queries(grp * 2 + (b // 4 + 1), (b // 4 + 1) % 2, first and b < 4)
                    if k == 0 and not (first and b == 0):
                        heads_out(t, (b // 4 + 1) % 2)

            dve.wait_ge(s["qte"], TILES)
            dve.wait_ge(s["qzero"], 1)
            queries(0, 0, True)
            maxes(0, 0)
            group(0, True, False)
            base = ch.base + ch.n
            with dve.Fori(1, GROUPS - 1) as grp:
                ch.start(base + (grp - 1) * 10)
                group(grp, False, False)
                assert ch.n == 10
            ch.start(base + 10 * (GROUPS - 2))
            group(GROUPS - 1, False, True)
            add4(TILES - 2, 0)
            heads_out(TILES - 1, 1)
            add3(TILES - 1)
            adapt_in(TILES - 1)
            add4(TILES - 1, 1)

        @block.tensor
        def _(pe):
            t_ = nc.tensor
            pe.wait_ge(s["consts"], 1)
            pe.wait_ge(s["ld_w"], 16 * N_W)
            pe.wait_ge(s["ld_idx"], 16 * N_IDX)
            packs = [[wqkv_raw[:, o, 0:P] for o in range(4)],
                     [wqkv_raw[:, o, P:2 * P] for o in range(4)],
                     [wo_raw[:, o, P * c:P * c + P] for c in range(2) for o in range(2)],
                     [w3_raw[:, o, P * c:P * c + P] for c in range(2) for o in range(2)],
                     [la_raw[:, 0:P], la_raw[:, P:2 * P], lb_raw[:, 0, :], lb_raw[:, 1, :]]]
            for n, pack in enumerate(packs):
                if n >= 2:
                    pe.wait_ge(s["wt_ev"], n - 1)
                for k, src in enumerate(pack):
                    ins = t_.transpose(ps[n % 2][:, P * k:P * k + P], src, ident[:])
                ins.then_inc(s["wt_pe"], 1)
            pe.wait_ge(s["wt_ev"], 5)

            def mix0(n, j):
                pe.wait_ge(s["wbd"], n + 1)
                wait_from(pe, s["x2"], n - 1)
                t_.matmul(psMix[j][:, 0:256], wbd[:, j, 0, :],
                          xres[:, bass.ds(n, 1), :].rearrange("p o f -> p (o f)"), start=True, stop=True).then_inc(s["l0"], 1)

            def mix1(n, j):
                pe.wait_ge(s["x1"], n + 1)
                t_.matmul(psMix[j][:, 0:256], wbd[:, j, 1, :], x1s[:, j, :], start=True, stop=True
                          ).then_inc(s["l1"], 1)

            def xT(n, j):
                pe.wait_ge(s["x2"], n + 1)
                wait_from(pe, s["qte"], n - 3)
                for c in range(2):
                    ins = t_.transpose(psT[j][:, P * c:P * c + P], x2s[:, j, P * c:P * c + P], ident[:])
                ins.then_inc(s["xt"], 1)

            def qkv(n, j):
                pe.wait_ge(s["xte"], n + 1)
                wait_from(pe, s["norm"], n - 1)
                wait_from(pe, s["vcopy"], n - 1)
                for c in range(2):
                    ins = t_.matmul(psQKV[j][:, :], x2T[:, j, c, :], wqkvT[:, c, :], start=(c == 0), stop=(c == 1))
                ins.then_inc(s["qkv"], 1)

            def qT(n, j, more):
                pe.wait_ge(s["roped"], n + 1)
                if more:
                    pe.wait_ge(s["xte"], n + 3)
                for u in range(2):
                    ins = t_.transpose(psT[j][:, P * u:P * u + P], stage[:, j, P * u:P * u + P], ident[:])
                ins.then_inc(s["qt"], 1)

            def part2(i, nxt):
                if nxt:
                    for j in range(2):
                        mix0(i * 2 + 2 + j, j)
                for j in range(2):
                    qkv(i * 2 + j, j)
                if nxt:
                    for j in range(2):
                        mix1(i * 2 + 2 + j, j)
                    for j in range(2):
                        xT(i * 2 + 2 + j, j)
                for j in range(2):
                    qT(i * 2 + j, j, nxt)

            pe.wait_ge(s["ld_x"], 16)
            for f in (mix0, mix1, xT):
                for j in range(2):
                    f(j, j)
            part2(0, True)
            with pe.Fori(1, TILES // 2 - 1) as i:
                part2(i, True)
            part2(TILES // 2 - 1, False)
            pe.wait_ge(s["qte"], TILES)
            pe.wait_ge(s["norm"], TILES)

            def unit(grp, u, first):
                if not (first and u < 2):
                    pe.wait_ge(s["unite"], grp * UNITS + (u - 1))
                if u % 4 == 0 and u < 8:
                    pe.wait_ge(s["turned"], grp * 2 + (u // 4 + 1))
                if u < 8:
                    kv = 1 if u < 4 else 0
                    for o in range(4):
                        off = 4 * (u % 4) + o
                        ins = t_.transpose(psR[u % 2][:, o * GR:(o + 1) * GR], block_in[0:GR, 1, kv, P * off:P * off + P],
                                           ident[0:GR, 0:GR])
                else:
                    if u == 8:
                        pe.wait_ge(s["unite"], grp * UNITS + 4)
                    for k in range(2):
                        b = 2 * (u - 8) + k
                        for h in range(2):
                            ins = t_.transpose(psR[u % 2][0:HALF, P * (2 * k + h):P * (2 * k + h) + P],
                                               vT[:, b, HALF * h:HALF * h + HALF], ident[:])
                ins.then_inc(s["unit"], 1)

            def scores(n, b, par, grp, m):
                if not (isinstance(n, int) and n < 2):
                    pe.wait_ge(s["expd"], n - 1)
                if b % 4 == 0:
                    pe.wait_ge(s["qbd"], m + 1)
                    pe.wait_ge(s["mask4"], m + 1)
                if b == 0:
                    pe.wait_ge(s["unite"], grp * UNITS + 8)
                both = psS[b % 2][:, 0:2 * KEYS].rearrange("p (c k) -> p c k", c=2)
                t_.matmul(both, mask4[:, (b // 4) % 2, b % 4, :], spread(maskB[:].rearrange("p o i -> p (o i)"), 1, 2),
                          start=True, stop=True, skip_group_check=True)
                for c in range(2):
                    ins = t_.matmul(psS[b % 2][:, c * KEYS:(c + 1) * KEYS], qbd[:, (b // 4) % 2, b % 4, c, :],
                                    kT[:, bass.ds(par, 1), :, WS * b:WS * b + WB].rearrange("p u o i -> p (u o) i"),
                                    start=False, stop=True, skip_group_check=True)
                ins.then_inc(s["scores"], 1)

            def probs_T(n, b):
                pe.wait_ge(s["expd"], n + 1)
                if not (isinstance(n, int) and n < 2):
                    pe.wait_ge(s["pte"], n - 1)
                for h in range(2):
                    for c in range(2):
                        ins = t_.transpose(psP[b % 2][0:HALF, 256 * h + P * c:256 * h + P * c + P],
                                           prob[:, b % 2, c, HALF * h:HALF * h + HALF], ident[:])
                ins.then_inc(s["pt"], 1)

            def values(n, b, par, grp, m):
                pe.wait_ge(s["pte"], n + 1)
                if b == 0:
                    pe.wait_ge(s["unite"], grp * UNITS + UNITS)
                if b % 4 == 0:
                    wait_from(pe, s["oev"], m)
                for c in range(2):
                    for h in range(2):
                        ins = t_.matmul(psO[:, P * (b % 4) + 64 * c:P * (b % 4) + 64 * c + 64], probT[:, b % 2, h, c, :],
                                        drop(vnat[0:HALF, bass.ds(par, 1), 256 * b + P * h + 64 * c:256 * b + P * h + 64 * c + 64]),
                                        start=(h == 0), stop=(h == 1))
                ins.then_inc(s["pv"], 1)

            def project(m):
                pe.wait_ge(s["oT"], m + 1)
                wait_from(pe, s["y"], m)
                for c in range(2):
                    ins = t_.matmul(psZ[:, 0:256], oT[:, c, :], woT[:, c, :], start=(c == 0), stop=(c == 1))
                ins.then_inc(s["wo"], 1)

            def x3_T(m):
                pe.wait_ge(s["x3"], m + 1)
                wait_from(pe, s["y"], m)
                for c in range(2):
                    ins = t_.transpose(psZ[:, 256 + P * c:256 + P * c + P], x3s[:, P * c:P * c + P], ident[:])
                ins.then_inc(s["x3t"], 1)

            def adapter(m):
                pe.wait_ge(s["x3te"], m + 1)
                for c in range(2):
                    ins = t_.matmul(psZ[:, 0:P], laT[:, c, :], x3T[:, c, :], start=(c == 0), stop=(c == 1))
                ins.then_inc(s["xa"], 1)

            def last(m):
                pe.wait_ge(s["xam"], m + 1)
                for c in range(2):
                    t_.matmul(psZ[:, 256:512], x3T[:, c, :], w3T[:, c, :], start=(c == 0), stop=False)
                t_.matmul(psZ[:, 256:512], xam, lbT[:], start=False, stop=True).then_inc(s["l3"], 1)

            def group(grp, first, final):
                for b in range(SPG):
                    n, k, t = grp * SPG + b, b % 4, grp * 2 + (b // 4 - 1)
                    if not (final and b == SPG - 1):
                        wrap = (b + 1) // SPG
                        scores(n + 1, (b + 1) % SPG, (grp + wrap) % 2, grp + wrap, grp * 2 + (b + 1) // 4)
                    if k == 0:
                        if not first:
                            last(t - 1)
                    elif not (first and b < 4):
                        (project, x3_T, adapter)[k - 1](t)
                    if not final:
                        for u in UNITS_AT[b]:
                            unit(grp + 1, u, False)
                    probs_T(n, b)
                    if b > 0:
                        values(n - 1, b - 1, grp % 2, grp, grp * 2 + (b - 1) // 4)
                    elif not (first and b == 0):
                        values(n - 1, SPG - 1, (grp + 1) % 2, grp - 1, grp * 2 - 1)

            for u in range(UNITS):
                unit(0, u, True)
            scores(0, 0, 0, 0, 0)
            group(0, True, False)
            with pe.Fori(1, GROUPS - 1) as grp:
                group(grp, False, False)
            group(GROUPS - 1, False, True)
            values(SEQS - 1, SPG - 1, (GROUPS - 1) % 2, GROUPS - 1, TILES - 1)
            last(TILES - 2)
            project(TILES - 1)
            x3_T(TILES - 1)
            adapter(TILES - 1)
            last(TILES - 1)


_INS = ("x", "itok_B_0_7", "itok_B_1_198", "itok_Bx257_0_4111", "itok_B_37_3939", "itok_B_0_6",
        "L0_cond_weights", "L1_cond_weights", "L2_cond_Wq", "L2_cond_Wk", "L2_cond_Wv", "L2_cond_Wo",
        "L2_cond_q_norm_scale", "L2_cond_k_norm_scale", "L2_cond_k_blocks", "L2_cond_v_blocks",
        "L3_cond_W", "L3_cond_A", "L3_cond_Bm", "L3_cond_scalings")


def kernel(**inputs):
    import numpy as _np
    import concourse.bacc as _bacc
    from concourse import mybir as _mybir
    from concourse.bass_utils import run_bass_kernel_spmd as _run

    nc = _bacc.Bacc("TRN2", target_bir_lowering=False, num_devices=1)
    arrays, args = {}, []
    for name in _INS:
        a = _np.ascontiguousarray(inputs[name])
        arrays[f"in_{name}"] = a
        args.append(nc.dram_tensor(f"in_{name}", a.shape, _mybir.dt.from_np(a.dtype), kind="ExternalInput").ap())
    out = nc.dram_tensor("out", (SEQS, ROWS, FEAT), _mybir.dt.float32, kind="ExternalOutput").ap()
    build(nc, *args, out)
    r = _run(nc, [arrays], core_ids=[0])
    return r.results[0]["out"]
```

```python
from contextlib import ExitStack

import numpy as np

import concourse.bass as bass
from concourse import mybir

ALU = mybir.AluOpType
ACT = mybir.ActivationFunctionType
F32 = mybir.dt.float32
BF16 = mybir.dt.bfloat16
I32 = mybir.dt.int32
AX_X = mybir.AxisListType.X

P = 128
SEQS = 128
ROWS = 32
FEAT = 256
TILES = 32
PAIRS = TILES // 2
SPT = 4
HEADS, KVH, HD = 8, 4, 32
BLOCK = 16
BLKW = KVH * BLOCK * HD
NBLOCKS = 16 * 257
SLOTS = 257
WINDOW = 128
WB = 11
WS = 12
SPG = 8
GROUPS = SEQS // SPG
GR = SPG * WS
KEYS = WB * BLOCK
HALF = KEYS // 2
ENT = 3 * SEQS
FIRST_ENT = WINDOW // BLOCK
SKIP = 65536
ADAPTERS, RANK = 8, 16
UNITS = 12
UNITS_AT = ((0, 1), (2, 3), (4, 5), (6, 7), (8,), (9,), (10,), (11,))
NEG = -1.0e30
EPS = 1e-6
MAGIC = 12582912.0
TWO_PI = 6.283185307179586
PI2_HI = 6.28125
PI2_MID = float(np.float32(round((TWO_PI - PI2_HI) * 2**21) / 2**21))
PI2_LO = TWO_PI - PI2_HI - PI2_MID


class Chain:

    def __init__(self, engine, sem):
        self.engine, self.sem, self.base, self.n = engine, sem, 0, 0

    def mark(self, instruction):
        instruction.then_inc(self.sem, 1)
        self.n += 1

    def wait(self):
        self.engine.wait_ge(self.sem, self.base + self.n)

    def link(self, instruction):
        self.mark(instruction)
        self.wait()

    def start(self, base):
        self.base, self.n = base, 0


def spread(ap, axis, n):
    ap = ap.unsqueeze(axis)
    shape = list(ap.shape)
    shape[axis] = n
    return ap.broadcast_to(shape)


def drop(ap):
    return ap.rearrange("p o n -> p (o n)")


def wait_from(engine, sem, value):
    if isinstance(value, int) and value <= 0:
        return
    engine.wait_ge(sem, value)


def build(nc, x, subj, cond, table, lens, adapt, w0, w1, wq, wk, wv, wo, qns, kns, kblk, vblk,
          w3, la, lb, lsc, out):
    with ExitStack() as ctx:
        ctx.enter_context(nc.allow_non_contiguous_dma(reason="index columns and adapter factors"))

        def sb(name, shape, dt=F32):
            return ctx.enter_context(nc.sbuf_tensor(name, shape, dt))

        def sem(name):
            return ctx.enter_context(nc.semaphore(name))

        def dram(name, shape, dt=F32):
            return nc.dram_tensor(name, shape, dt).ap()

        d_mix = dram("mix_scratch", [2, SEQS, ROWS * ROWS])
        d_ent = dram("entry_scratch", [SEQS, 3])
        d_win = dram("window_scratch", [2, SEQS, WS], I32)
        d_row = dram("row_scratch", [SEQS, ROWS], I32)
        d_new = dram("new_scratch", [ENT * BLOCK, 2 * KVH * HD])
        d_k2 = dram("patched_k", [ENT, BLKW])
        d_v2 = dram("patched_v", [ENT, BLKW])

        xres = sb("xres", [P, TILES, FEAT])
        qtres = sb("qtres", [P, TILES, 256])
        block_in = sb("block_in", [P, 2, 2, BLKW])
        r1 = sb("window", [P, 2 * 1536 + 1536 + 2 * 2048])
        region = r1[:, 0:2 * 4096].rearrange("p (a n) -> p a n", a=2)
        rp = sb("rope", [P, TILES * 4 * HD])
        rope = rp[:].rearrange("p (t w d) -> p t w d", w=4, d=HD)
        ident = sb("ident", [P, P])
        wqkvT = sb("wqkvT", [P, 2, 512])
        woT = sb("woT", [P, 2, 256])
        w3T = sb("w3T", [P, 2, 256])
        laT = sb("laT", [P, 2, P])
        lbT = sb("lbT", [P, 256])
        mixw = sb("mixw", [P, 2, TILES, ROWS])
        bdmask = sb("bdmask", [P, SPT, ROWS])
        maskA = sb("maskA", [96, SEQS, ROWS], BF16)
        maskB = sb("maskB", [96, BLOCK, WB], BF16)
        mask4 = sb("mask4", [96, 2, SPT, P], BF16)
        admask = sb("admask", [P, SEQS])
        rowidx = sb("rowidx", [P, TILES], I32)
        winidx = sb("winidx", [GR, 2, GROUPS], I32)
        rowcol = sb("rowcol", [P, 2], I32)
        wincol = sb("wincol", [GR, 2], I32)

        kT = r1[:, 0:2 * 1536].rearrange("p (u o r) -> p u o r", u=2, r=GR)
        vT = r1[:, 3072:3072 + SPG * KEYS].rearrange("p (b k) -> p b k", b=SPG)
        vnat = r1[:, 4608:4608 + 4096].rearrange("p (u n) -> p u n", u=2)

        q1 = qtres[:].rearrange("p a n -> p (a n)")
        used = [0]

        def tmp(n, dt=F32):
            a = q1[:, used[0]:used[0] + n]
            used[0] += n
            return a if dt == F32 else a.bitcast(dt)

        eqall = tmp(WB * ENT)
        bounds = tmp(2 * ENT)
        blk_bc = tmp(ENT)
        e_plus = tmp(ENT)
        v_upper = tmp(ENT)
        v_lower = tmp(ENT)
        rel = tmp(SLOTS)
        tabf = tmp(SLOTS)
        junk = tmp(SLOTS)

        tabi = tmp(SLOTS, I32)
        leni = sb("leni", [P, 1], I32)
        remi = sb("remi", [P, 1], I32)
        lens_bc = sb("lens_bc", [P, SEQS], I32)
        rem_bci = sb("rem_bci", [P, SEQS], I32)
        lent = sb("lent", [P, TILES], I32)
        adapt_bc = sb("adapt_bc", [P, SEQS], I32)
        mixi = sb("mixi", [P, 2], I32)
        sc_bc = sb("sc_bc", [P, ADAPTERS])
        ns_bc = sb("ns_bc", [P, 2, HD])
        idf = sb("idf", [P, 24])
        rem_bc = sb("rem_bc", [P, SEQS])
        len_f = sb("len_f", [P, SEQS])
        start_bc = sb("start_bc", [P, SEQS])
        blkw = sb("blkw", [P, WS])
        entf = sb("entf", [P, WS])
        enti = sb("enti", [P, 3], I32)
        own = sb("own", [P, 3])
        ub = sb("ub", [P, 3])
        lo = sb("lo", [P, 3])
        difs = sb("difs", [P, 3, 2])
        tok = sb("tok", [P, 12, ROWS])
        rows_i = sb("rows_i", [P, ROWS], I32)
        win_i = sb("win_i", [P, 2, WS], I32)
        pidx = sb("pidx", [P, 4], I32)
        pf = sb("pf", [P, 4])
        ad_f = sb("ad_f", [P, SEQS])
        kmt = sb("kmt", [64, ROWS])
        negk = sb("negk", [P, 1])
        iota8 = sb("iota8", [P, ADAPTERS])
        iotat = sb("iotat", [P, ROWS])
        j8 = sb("j8", [P, ADAPTERS])
        invf = sb("invf", [P, 16])
        pos = sb("pos", [P, TILES])
        nscale = sb("nscale", [P, 2, 2, HD])
        halfpi = sb("halfpi", [P, 1])
        gates = sb("gates", [1, 4])
        epsb = sb("epsb", [P, 1])
        ang = r1[:, 0:512].rearrange("p (t j) -> p t j", j=16)
        kq = r1[:, 512:1024].rearrange("p (t j) -> p t j", j=16)
        cosb = r1[:, 1024:1536].rearrange("p (t j) -> p t j", j=16)
        sinb = r1[:, 1536:2048].rearrange("p (t j) -> p t j", j=16)

        wraw = block_in[:, 1].rearrange("p a n -> p (a n)")
        wqkv_raw = wraw[:, 0:1024].rearrange("p (o f) -> p o f", o=4)
        wo_raw = wraw[:, 1024:1536].rearrange("p (o f) -> p o f", o=2)
        w3_raw = wraw[:, 1536:2048].rearrange("p (o f) -> p o f", o=2)
        la_raw = wraw[:, 2048:2304]
        lb_raw = wraw[:, 2304:2560].rearrange("p (c n) -> p c n", c=2)
        mix_raw = r1[:, 2048:4096].rearrange("p (l n) -> p l n", l=2)

        wbd = sb("wbd", [P, 2, 2, SPT * ROWS])
        x1s = sb("x1s", [P, 2, FEAT])
        x2s = sb("x2s", [P, 2, FEAT])
        x2T = sb("x2T", [P, 2, 2, P])
        early = sb("early", [P, 4, 2, 384])
        sq, qn, rc, rs = (early[:, k] for k in range(4))
        ss = sb("ss", [P, 2, 12])
        sd = sb("sd", [P, 2, 12])
        ri = sb("ri", [P, 2, 12])
        stage = sb("stage", [P, 2, 512])
        vnew = tok[:, 0:8, :].rearrange("p (j a) d -> p j (a d)", j=2)

        qbd = rp[:, 0:2048].rearrange("p (a b c q) -> p a b c q", a=2, b=SPT, c=2)
        prob = rp[:, 2048:2048 + 4 * KEYS].rearrange("p (a c k) -> p a c k", a=2, c=2)
        negm = sb("negm", [P, 2, 2])
        sums = sb("sums", [P, 2, SPT, 2])
        rinv = sb("rinv", [P, SPT, 2])
        probT = rp[0:HALF, 3072:4096].rearrange("p (a h c q) -> p a h c q", a=2, h=2, c=2)
        e1 = early[:].rearrange("p a b n -> p (a b n)")
        osb = e1[:, 0:256].rearrange("p (c b d) -> p c b d", c=2, b=SPT)
        oT = e1[:, 256:512].rearrange("p (c n) -> p c n", c=2)
        x3s = e1[:, 512:768]
        x3T = e1[:, 768:1024].rearrange("p (c n) -> p c n", c=2)
        xam = e1[:, 1024:1152]
        ys = e1[:, 1152:1664].rearrange("p (a n) -> p a n", a=2)

        ps = [ctx.enter_context(nc.psum_tensor(f"bank{i}", [P, 512], F32)) for i in range(8)]
        psMix, psT, psQKV, psQT = [ps[0], ps[1]], [ps[2], ps[3]], [ps[4], ps[5]], [ps[6], ps[7]]
        psS = [ps[0], ps[1]]
        psP = [ps[2], ps[3]]
        psR = [ps[4], ps[5]]
        psO, psZ = ps[6], ps[7]

        s = {n: sem(n) for n in (
            "ld_idx", "ld_w", "ld_x", "consts", "mix_col", "mix_gather", "mix_store", "mix_load",
            "ent_out", "ent_bc", "win_out", "win_in", "row_out", "row_in", "ent_idx", "angles", "trig",
            "blk_in0", "blk_in1", "blk_re", "blk_st0", "blk_st1", "wt_pe", "wt_ev", "pool_chain", "dve_chain",
            "wbd", "l0", "x1", "l1", "x2", "xcopy", "xt", "xte", "qkv", "square", "sumsq", "root", "norm",
            "swap", "roped", "vcopy", "qt", "qte", "scat0", "scat1", "vrow",
            "pk_in0", "pk_in1", "pk_out0", "pk_out1", "raw_v", "raw_k",
            "scores", "negmax", "expd", "pt", "pte", "pv", "unit", "unite", "qbd", "oev", "oT", "win_idx", "row_idx", "pk_rek", "turned", "mask4", "qzero", "masks", "pk_rev",
            "wo", "x3", "x3t", "x3te", "xa", "xam", "l3", "y", "out0", "out1")}
        s_scat = [s["scat0"], s["scat1"]]
        s_out = [s["out0"], s["out1"]]
        s_blk_in, s_blk_st = [s["blk_in0"], s["blk_in1"]], [s["blk_st0"], s["blk_st1"]]
        s_pk_in, s_pk_out = [s["pk_in0"], s["pk_in1"]], [s["pk_out0"], s["pk_out1"]]
        N_IDX, N_W = 14, 16

        d_new_blocks = d_new.rearrange("(b s t) n -> s b (t n)", s=3, t=BLOCK)
        k2_by = d_k2.rearrange("(b s) n -> s b n", s=3)
        v2_by = d_v2.rearrange("(b s) n -> s b n", s=3)
        kflat = kblk.rearrange("n g t d -> n (g t d)")
        vflat = vblk.rearrange("n g t d -> n (g t d)")

        def col(v):
            return v.rearrange("(b o) -> b o", o=1)

        def bcast(v, n):
            return v.partition_broadcast(n)

        block = ctx.enter_context(nc.Block())

        @block.sync
        def _(sp):
            il = s["ld_idx"]
            sp.dma_start(mixi[:, 0:1], col(subj)).then_inc(il, 16)
            sp.dma_start(mixi[:, 1:2], col(cond)).then_inc(il, 16)
            sp.dma_start(leni[:], col(lens)).then_inc(il, 16)
            sp.dma_start(tabi, table).then_inc(il, 16)
            sp.dma_start(lens_bc[:], bcast(lens, P)).then_inc(il, 16)
            for b in range(SPT):
                sp.dma_start(lent[32 * b:32 * b + 32, :],
                             lens.rearrange("(t b) -> b t", b=SPT)[b].partition_broadcast(ROWS)).then_inc(il, 16)
            sp.dma_start(adapt_bc[:], bcast(adapt, P)).then_inc(il, 16)
            sp.dma_start(sc_bc[:], bcast(lsc, P)).then_inc(il, 16)
            sp.dma_start(ns_bc[:, 0, :], bcast(qns, P)).then_inc(il, 16)
            sp.dma_start(ns_bc[:, 1, :], bcast(kns, P)).then_inc(il, 16)
            sp.dma_start(la_raw, la.rearrange("a r f -> (a r) f")).then_inc(il, 16)
            wl = s["ld_w"]
            for o in range(2):
                for h in range(KVH):
                    sp.dma_start(wqkv_raw[HD * h:HD * h + HD, o, :],
                                 wq[HD * (2 * h + o):HD * (2 * h + o) + HD, :]).then_inc(wl, 16)
                sp.dma_start(wo_raw[:, o, :], wo[P * o:P * o + P, :]).then_inc(wl, 16)
                sp.dma_start(w3_raw[:, o, :], w3[P * o:P * o + P, :]).then_inc(wl, 16)
                sp.dma_start(lb_raw[:, o, :].rearrange("p (a r) -> p a r", a=ADAPTERS),
                             lb[:, P * o:P * o + P, :].rearrange("a o r -> o a r")).then_inc(wl, 16)
            sp.dma_start(wqkv_raw[:, 2, :], wk).then_inc(wl, 16)
            sp.dma_start(wqkv_raw[:, 3, :], wv).then_inc(wl, 16)
            sp.dma_start(xres[:], x.rearrange("(t b) c f -> (b c) t f", b=SPT)).then_inc(s["ld_x"], 16)
            sp.wait_ge(s["mix_gather"], 32)
            sp.dma_start(d_mix.rearrange("l b n -> b l n"), mix_raw).then_inc(s["mix_store"], 16)
            sp.wait_ge(s["mix_store"], 16)
            for l in range(2):
                sp.dma_start(mixw[:, l, :, :], d_mix[l].rearrange("(t b) (c d) -> (b c) t d", b=SPT, d=ROWS)
                             ).then_inc(s["mix_load"], 16)
            sp.wait_ge(s["ent_idx"], 1)
            sp.dma_start(d_ent, blkw[:, FIRST_ENT:FIRST_ENT + 3]).then_inc(s["ent_out"], 16)
            sp.wait_ge(s["ent_out"], 16)
            sp.dma_start(blk_bc, d_ent.rearrange("b s -> (b s)").partition_broadcast(P)).then_inc(s["ent_bc"], 16)
            sp.wait_ge(s["row_idx"], 1)
            sp.dma_start(d_row, rows_i[:]).then_inc(s["row_out"], 16)
            sp.wait_ge(s["win_idx"], 2)
            sp.dma_start(d_win.rearrange("k b i -> b k i"), win_i[:]).then_inc(s["win_out"], 16)
            sp.wait_ge(s["row_out"], 16)
            sp.dma_start(rowidx[:], d_row.rearrange("(t b) c -> (b c) t", b=SPT)).then_inc(s["row_in"], 16)
            sp.wait_ge(s["win_out"], 16)
            for k in range(2):
                sp.dma_start(winidx[:, k, :], d_win[k].rearrange("(g b) i -> (b i) g", b=SPG)).then_inc(s["win_in"], 16)
            for e in range(3):
                sp.wait_ge(s["blk_re"], 2 * e + 2)
                sp.dma_start(d_new_blocks[e], region[:, e % 2, :]).then_inc(s_blk_st[e % 2], 16)
            for e in range(3):
                if e == 0:
                    sp.wait_ge(s_scat[0], 16 * TILES // 2)
                    sp.wait_ge(s_scat[1], 16 * TILES // 2)
                if e == 2:
                    sp.wait_ge(s["pk_rek"], 1)
                    sp.wait_ge(s["pk_rev"], 1)
                sp.dma_start(region[:, e % 2, :], d_new_blocks[e]).then_inc(s_pk_in[e % 2], 16)
            for e in range(3):
                sp.wait_ge(s["pk_rek"], e + 1)
                sp.wait_ge(s["pk_rev"], e + 1)
                sp.dma_start(k2_by[e], block_in[:, e % 2, 0, :]).then_inc(s_pk_out[e % 2], 16)
                sp.dma_start(v2_by[e], block_in[:, e % 2, 1, :]).then_inc(s_pk_out[e % 2], 16)

            def store(m, par):
                sp.wait_ge(s["y"], m + 1)
                sp.dma_start(out.rearrange("(t b) c f -> t (b c) f", b=SPT)[bass.ds(m, 1)].rearrange("t p f -> p (t f)"),
                             ys[:, par, :]).then_inc(s_out[par], 16)

            with sp.Fori(0, TILES // 2) as i:
                store(i * 2, 0)
                store(i * 2 + 1, 1)
            sp.wait_ge(s_out[0], 16 * TILES // 2)
            sp.wait_ge(s_out[1], 16 * TILES // 2)

        @block.gpsimd
        def _(pool):
            ch = Chain(pool, s["pool_chain"])
            g = nc.gpsimd
            kw = dict(allow_small_or_imprecise_dtypes=True)
            pool.wait_ge(s["ld_idx"], 16 * N_IDX)
            for l, w in ((0, w0), (1, w1)):
                g.indirect_dma_start(mix_raw[:, l, :], None, w.rearrange("n c d -> n (c d)"),
                                     bass.IndirectOffsetOnAxis(ap=mixi[:, l:l + 1], axis=0),
                                     bounds_check=w.shape[0] - 1, oob_is_err=False).then_inc(s["mix_gather"], 16)
            g.iota(rel, pattern=[[1, SLOTS]], base=0, channel_multiplier=0, **kw)
            g.iota(e_plus, pattern=[[1, ENT]], base=1, channel_multiplier=0, **kw)
            g.iota(own[:], pattern=[[1, 3]], base=1, channel_multiplier=3, **kw)
            g.iota(pidx[:, 0:1], pattern=[[0, 1]], base=0, channel_multiplier=1)
            g.iota(kmt[:], pattern=[[-1, ROWS]], base=0, channel_multiplier=1, **kw)
            g.iota(iota8[:], pattern=[[1, ADAPTERS]], base=0, channel_multiplier=0, **kw)
            g.iota(iotat[:], pattern=[[1, ROWS]], base=0, channel_multiplier=0, **kw)
            g.memset(v_upper.rearrange("p (b s) -> p b s", s=3)[:, :, 1:2], 99.0)
            g.memset(v_upper.rearrange("p (b s) -> p b s", s=3)[:, :, 2:3], 0.0)
            g.memset(v_lower.rearrange("p (b s) -> p b s", s=3)[:, :, 0:2], 0.0)
            g.memset(halfpi[:], TWO_PI / 4)
            g.memset(epsb[:], EPS)
            for j in range(16):
                g.memset(invf[:, j:j + 1], float(np.float32(1.0) / np.float32(10000.0 ** (j / 16))))
            ch.mark(g.memset(ident[:], 0.0))
            ch.mark(g.memset(bdmask[:], 1.0))
            ch.link(g.memset(maskB[:], 0.0))
            ch.mark(g.affine_select(out=ident[:], in_=ident[:], compare_op=ALU.not_equal, fill=1.0, base=0,
                                    pattern=[[-1, P]], channel_multiplier=1))
            ch.mark(g.affine_select(out=bdmask[:], in_=bdmask[:], compare_op=ALU.is_ge, fill=0.0, base=0,
                                    pattern=[[-ROWS, SPT], [0, ROWS]], channel_multiplier=1))
            ch.link(g.affine_select(out=maskB[0:64], in_=maskB[0:64], compare_op=ALU.is_ge, fill=NEG, base=-1,
                                    pattern=[[1, BLOCK], [BLOCK, WB]], channel_multiplier=-1))
            ch.mark(g.affine_select(out=maskB[0:64], in_=maskB[0:64], compare_op=ALU.is_ge, fill=NEG, base=WINDOW,
                                    pattern=[[-1, BLOCK], [-BLOCK, WB]], channel_multiplier=1))
            ch.link(g.affine_select(out=bdmask[:], in_=bdmask[:], compare_op=ALU.is_ge, fill=0.0, base=ROWS - 1,
                                    pattern=[[ROWS, SPT], [0, ROWS]], channel_multiplier=-1))
            gates_set = g.memset(gates[:], 0.0)
            gates_set.then_inc(s["consts"], 1)
            pool.wait_ge(s["mix_gather"], 32)
            pool.wait_ge(s["consts"], 1)
            ch.mark(g.iota(negk[64:96, :], pattern=[[0, 1]], base=0, channel_multiplier=-1, **kw))
            ch.link(g.affine_select(out=maskB[64:96], in_=maskB[64:96], compare_op=ALU.not_equal, fill=NEG, base=0,
                                    pattern=[[0, BLOCK], [1, WB]], channel_multiplier=-1))
            g.memset(gates[:], 0.0).then_inc(s["masks"], 1)

            pool.wait_ge(s["ent_idx"], 1)

            def entry_gather(e):
                for kv, src in enumerate((kflat, vflat)):
                    g.indirect_dma_start(block_in[:, e % 2, kv, :], None, src,
                                         bass.IndirectOffsetOnAxis(ap=enti[:, e:e + 1], axis=0),
                                         bounds_check=NBLOCKS - 1, oob_is_err=False).then_inc(s_blk_in[e % 2], 16)

            entry_gather(0)
            pool.wait_ge(s["wt_pe"], 5)
            entry_gather(1)
            pool.wait_ge(s["blk_re"], 2)
            entry_gather(2)

            def gate():
                ch.wait()
                ch.mark(g.tensor_tensor(gates[0:1, 0:1], gates[0:1, 1:2], gates[0:1, 2:3], ALU.add))

            def mix_weights(n, j):
                wait_from(pool, s["l1"], n - 1)
                g.tensor_tensor(wbd[:, j].rearrange("p l (b d) -> p l b d", b=SPT),
                                spread(mixw[:, :, bass.ds(n, 1), :].rearrange("p l o d -> p l (o d)"), 2, SPT),
                                spread(bdmask[:], 1, 2), ALU.mult).then_inc(s["wbd"], 1)

            def swap(n, j):
                pool.wait_ge(s["norm"], n + 1)
                wait_from(pool,  s["roped"], n - 1)
                src = qn[:, j, :].rearrange("p (h u d) -> p h u d", u=2, d=16)
                dst = rs[:, j, :].rearrange("p (h u d) -> p h u d", u=2, d=16)
                for a, b, w in ((0, 8, 1), (8, 12, 3)):
                    for u in range(2):
                        ins = g.tensor_tensor(dst[:, a:b, u, :], src[:, a:b, 1 - u, :],
                                              spread(drop(rope[:, bass.ds(n, 1), w, 16 * u:16 * u + 16]), 1, b - a), ALU.mult)
                ins.then_inc(s["swap"], 1)

            def scatter(n, j, first):
                if not first:
                    pool.wait_ge(s_scat[j], (n - j) * 8)
                ch.link(g.tensor_copy(rowcol[:, j:j + 1], rowidx[:, bass.ds(n, 1)]))
                pool.wait_ge(s["roped"], n + 1)
                pool.wait_ge(s["vrow"], n + 1)
                gate()
                g.indirect_dma_start(d_new, bass.IndirectOffsetOnAxis(ap=rowcol[:, j:j + 1], axis=0),
                                     stage[:, j, 256:512], None, bounds_check=ENT * BLOCK - 1, oob_is_err=False
                                     ).then_inc(s_scat[j], 16)

            def part2(i, first, weights):
                for j in range(2):
                    swap(i * 2 + j, j)
                if weights:
                    for j in range(2):
                        mix_weights(i * 2 + 6 + j, j)
                if first:
                    pool.wait_ge(s["row_in"], 16)
                    pool.wait_ge(s_blk_st[0], 32)
                    pool.wait_ge(s_blk_st[1], 16)
                for j in range(2):
                    scatter(i * 2 + j, j, first)

            pool.wait_ge(s["mix_load"], 32)
            for n in range(6):
                mix_weights(n, n % 2)
            part2(0, True, True)
            base = ch.base + ch.n
            with pool.Fori(1, PAIRS - 3) as i:
                ch.start(base + (i - 1) * 4)
                part2(i, False, True)
                assert ch.n == 4
            ch.start(base + 4 * (PAIRS - 4))
            for i in range(PAIRS - 3, PAIRS):
                part2(i, False, False)

            def gather(grp, kv, first):
                done = s["raw_v" if kv else "raw_k"]
                for k, src in enumerate(((kflat, vflat)[kv], (d_k2, d_v2)[kv])):
                    if k == 0 and not first:
                        pool.wait_ge(s["turned"], grp * 2 - kv)
                        gate()
                    if k == 1:
                        pool.wait_ge(done, grp * 32 + 16)
                        gate()
                    g.indirect_dma_start(block_in[0:GR, 0, kv, :], None, src,
                                         bass.IndirectOffsetOnAxis(ap=wincol[:, k:k + 1], axis=0),
                                         bounds_check=src.shape[0] - 1, oob_is_err=False).then_inc(done, 16)

            def columns(grp, first):
                if not first:
                    pool.wait_ge(s["raw_k"], grp * 32)
                    gate()
                ch.link(g.tensor_copy(wincol[:], winidx[:, :, bass.ds(grp, 1)].rearrange("p k o -> p (k o)")))
                gate()

            def masks(m, par, first):
                if not first:
                    pool.wait_ge(s["scores"], m * 4 - 4)
                g.tensor_copy(mask4[:, par].rearrange("p b (r t) -> p b r t", r=4),
                              spread(maskA[:, bass.ds(m * SPT, SPT), :], 2, 4)).then_inc(s["mask4"], 1)

            pool.wait_ge(s["win_in"], 32)
            pool.wait_ge(s_pk_out[0], 64)
            pool.wait_ge(s_pk_out[1], 32)
            ch.link(g.memset(block_in[0:GR, 0, :, :], 0.0))
            columns(0, True)
            gather(0, 1, True)
            gather(0, 0, True)
            pool.wait_ge(s["roped"], TILES)
            g.memset(rp[:, 0:2048], 0.0).then_inc(s["qzero"], 1)
            for grp in (1, 2):
                columns(grp, False)
                gather(grp, 1, False)
                if grp == 2:
                    masks(0, 0, True)
                    masks(1, 1, True)
                gather(grp, 0, False)

            def part3(grp, more):
                if more:
                    columns(grp + 3, False)
                    gather(grp + 3, 1, False)
                masks(grp * 2 + 2, 0, False)
                masks(grp * 2 + 3, 1, False)
                if more:
                    gather(grp + 3, 0, False)

            base = ch.base + ch.n
            with pool.Fori(0, GROUPS - 3) as grp:
                ch.start(base + grp * 7)
                part3(grp, True)
                assert ch.n == 7
            ch.start(base + 7 * (GROUPS - 3))
            for grp in (GROUPS - 3, GROUPS - 2):
                part3(grp, False)

        @block.scalar
        def _(act):
            a = nc.scalar
            for n, (dst, w) in enumerate(((wqkvT[:, 0, :], 512), (wqkvT[:, 1, :], 512),
                                          (woT.rearrange("p c n -> p (c n)"), 512),
                                          (w3T[:].rearrange("p c n -> p (c n)"), 512), (None, 0))):
                act.wait_ge(s["wt_pe"], n + 1)
                if dst is not None:
                    a.copy(dst, ps[n % 2][:, 0:w]).then_inc(s["wt_ev"], 1)
                else:
                    a.copy(laT[:].rearrange("p c n -> p (c n)"), ps[n % 2][:, 0:256])
                    a.copy(lbT[:], ps[n % 2][:, 256:512]).then_inc(s["wt_ev"], 1)
            act.wait_ge(s["angles"], 1)
            a.activation(sinb, ang, ACT.Sin)
            a.activation(cosb, kq, ACT.Sin, bias=halfpi[:], scale=-1.0).then_inc(s["trig"], 1)

            for e in range(3):
                act.wait_ge(s_blk_in[e % 2], 32 * (e // 2 + 1))
                if e == 0:
                    act.wait_ge(s["trig"], 2)
                    act.wait_ge(s["mix_store"], 16)
                if e == 2:
                    act.wait_ge(s_blk_st[0], 16)
                for kv in range(2):
                    a.copy(region[:, e % 2, :].rearrange("p (t k g d) -> p k t g d", t=BLOCK, k=2, g=KVH)[:, kv],
                           block_in[:, e % 2, kv, :].rearrange("p (g t d) -> p t g d", g=KVH, d=HD)).then_inc(s["blk_re"], 1)

            def xT_out(n, j):
                act.wait_ge(s["xt"], n + 1)
                wait_from(act, s["qkv"], n - 1)
                a.copy(x2T[:, j].rearrange("p c n -> p (c n)"), psT[j][:, 0:256]).then_inc(s["xte"], 1)

            def keep_x(n, j):
                act.wait_ge(s["x2"], n + 1)
                a.copy(xres[:, bass.ds(n, 1), :].rearrange("p t f -> p (t f)"), x2s[:, j, :]).then_inc(s["xcopy"], 1)

            def squares(n, j):
                act.wait_ge(s["qkv"], n + 1)
                wait_from(act, s["sumsq"], n - 1)
                a.activation(sq[:, j, :], psQKV[j][:, 0:384], ACT.Square).then_inc(s["square"], 1)

            def values(n, j):
                wait_from(act, s["vrow"], n - 1)
                a.copy(vnew[:, j, :], psQKV[j][:, 384:512]).then_inc(s["vcopy"], 1)

            def value_rows(n, j, i):
                act.wait_ge(s["vcopy"], n + 1)
                wait_from(act, s_scat[j], i * 16)
                a.copy(stage[:, j, 384:512], vnew[:, j, :]).then_inc(s["vrow"], 1)

            def root(n, j):
                act.wait_ge(s["sumsq"], n + 1)
                wait_from(act, s["norm"], n - 1)
                a.activation(sd[:, j, :], ss[:, j, :], ACT.Sqrt, bias=epsb[:], scale=1.0 / HD).then_inc(s["root"], 1)

            def qT_out(n, j):
                act.wait_ge(s["qt"], n + 1)
                a.copy(qtres[:, bass.ds(n, 1), :].rearrange("p o n -> p (o n)"), psQT[j][:, 0:256]).then_inc(s["qte"], 1)

            def part2(i, s1, s2, s3):
                if s3:
                    for j in range(2):
                        value_rows(i * 2 + j, j, i)
                for j in range(2):
                    if s2:
                        squares(i * 2 + 2 + j, j)
                        values(i * 2 + 2 + j, j)
                if s1:
                    for j in range(2):
                        xT_out(i * 2 + 4 + j, j)
                if s2:
                    for j in range(2):
                        root(i * 2 + 2 + j, j)
                if s1:
                    for j in range(2):
                        keep_x(i * 2 + 4 + j, j)
                if s3:
                    for j in range(2):
                        qT_out(i * 2 + j, j)

            part2(-2, True, False, False)
            part2(-1, True, True, False)
            part2(0, True, True, True)
            with act.Fori(1, PAIRS - 2) as i:
                part2(i, True, True, True)
            part2(PAIRS - 2, False, True, True)
            part2(PAIRS - 1, False, False, True)

            for e in range(3):
                act.wait_ge(s_pk_in[e % 2], 16 * (e // 2 + 1))
                if e == 2:
                    act.wait_ge(s_pk_out[0], 32)
                a.copy(block_in[:, e % 2, 1, :].rearrange("p (g t d) -> p g t d", g=KVH, d=HD),
                       region[:, e % 2, :].rearrange("p (t k g d) -> p k g t d", t=BLOCK, k=2, g=KVH)[:, 1]).then_inc(s["pk_rev"], 1)

            def unit_out(grp, par, u):
                act.wait_ge(s["unit"], grp * UNITS + (u + 1))
                src = psR[u % 2]
                if u < 4:
                    ins = a.copy(vT[:, :, 4 * u * WB:4 * (u + 1) * WB].rearrange("p b (o i) -> p o b i", i=WB),
                                 src[:, 0:4 * GR].rearrange("p (o b i) -> p o b i", o=4, b=SPG)[:, :, :, 0:WB])
                elif u < 8:
                    if not (isinstance(grp, int) and grp < 2):
                        act.wait_ge(s["scores"], grp * SPG - SPG)
                    ins = a.copy(r1[:, bass.ds(par * 1536 + 4 * (u - 4) * GR, 4 * GR)], src[:, 0:4 * GR])
                else:
                    if not (isinstance(grp, int) and grp < 2):
                        act.wait_ge(s["pv"], grp * SPG - SPG)
                    ins = a.copy(r1[0:HALF, bass.ds(par * 2048 + (4608 + 512 * (u - 8)), 512)], src[0:HALF, :])
                ins.then_inc(s["unite"], 1)

            def exps(n, b, m, first_tiles):
                act.wait_ge(s["negmax"], n + 1)
                if not (isinstance(n, int) and n < 2):
                    act.wait_ge(s["pt"], n - 1)
                if b % 4 == 0 and not first_tiles:
                    act.wait_ge(s["oev"], m - 1)
                for c in range(2):
                    ins = a.activation(prob[:, b % 2, c, :], psS[b % 2][:, c * KEYS:(c + 1) * KEYS], ACT.Exp,
                                       bias=negm[:, b % 2, c:c + 1],
                                       accum_out=sums[:, (b // 4) % 2, b % 4, c:c + 1])
                ins.then_inc(s["expd"], 1)

            def x3T_out(m):
                act.wait_ge(s["x3t"], m + 1)
                wait_from(act, s["l3"], m)
                a.copy(x3T.rearrange("p c n -> p (c n)"), psZ[:, 256:512]).then_inc(s["x3te"], 1)

            def group(grp, first, last):
                npar = (grp + 1) % 2
                for b in range(SPG):
                    n = grp * SPG + b
                    if not (last and b == SPG - 1):
                        m = grp * 2 + (b + 1) // 4
                        exps(n + 1, (b + 1) % SPG, m, first and b + 1 < SPG)
                    if b % 4 == 3 and not (first and b < 4):
                        x3T_out(grp * 2 + (b // 4 - 1))
                    if not last:
                        for u in UNITS_AT[b]:
                            unit_out(grp + 1, npar, u)

            
            for u in range(UNITS):
                if u == 0:
                    act.wait_ge(s_pk_out[0], 64)
                    act.wait_ge(s_pk_out[1], 32)
                unit_out(0, 0, u)
            exps(0, 0, 0, True)
            group(0, True, False)
            with act.Fori(1, GROUPS - 1) as grp:
                group(grp, False, False)
            group(GROUPS - 1, False, True)
            x3T_out(TILES - 1)

        @block.vector
        def _(dve):
            v = nc.vector
            ch = Chain(dve, s["dve_chain"])
            link = ch.link
            dve.wait_ge(s["consts"], 1)
            dve.wait_ge(s["ld_idx"], 16 * N_IDX)
            ch.mark(v.tensor_scalar(remi[:], leni[:], 15, None, ALU.bitwise_and))
            ch.mark(v.tensor_scalar(rem_bci[:], lens_bc[:], 15, None, ALU.bitwise_and))
            ch.mark(v.tensor_scalar(pidx[:, 1:2], pidx[:, 0:1], 31, None, ALU.bitwise_and))
            ch.mark(v.tensor_scalar(pidx[:, 2:3], pidx[:, 0:1], 4, None, ALU.logical_shift_right))
            ch.mark(v.tensor_copy(idf[:, 3:4], leni[:]))
            ch.mark(v.tensor_copy(tabf, tabi))
            ch.mark(v.tensor_copy(len_f[:], lens_bc[:]))
            ch.mark(v.tensor_copy(pos[:], lent[:]))
            ch.mark(v.tensor_copy(ad_f[:], adapt_bc[:]))
            ch.wait()
            ch.mark(v.tensor_copy(idf[:, 0:1], remi[:]))
            ch.mark(v.tensor_copy(rem_bc[:], rem_bci[:]))
            ch.mark(v.tensor_copy(pf[:, 1:3], pidx[:, 1:3]))
            ch.wait()
            link(v.tensor_tensor(idf[:, 1:2], idf[:, 3:4], idf[:, 0:1], ALU.subtract))
            link(v.tensor_scalar(idf[:, 2:3], idf[:, 1:2], 1.0 / BLOCK, -float(FIRST_ENT), ALU.mult, ALU.add))
            link(v.tensor_scalar(rel, rel, idf[:, 2:3], None, ALU.subtract))
            for i in range(WB):
                link(v.scalar_tensor_tensor(out=junk, in0=rel, scalar=float(i), in1=tabf, op0=ALU.is_equal,
                                            op1=ALU.mult, accum_out=blkw[:, i:i + 1]))
            v.tensor_copy(enti[:], blkw[:, FIRST_ENT:FIRST_ENT + 3]).then_inc(s["ent_idx"], 1)

            link(v.tensor_scalar(pos[:], pos[:], pf[:, 1:2], None, ALU.add))
            link(v.tensor_tensor(ang, spread(pos[:], 2, 16), spread(invf[:], 1, TILES), ALU.mult))
            link(v.tensor_scalar(kq, ang, 1.0 / TWO_PI, MAGIC, ALU.mult, ALU.add))
            link(v.tensor_scalar(kq, kq, MAGIC, None, ALU.subtract))
            for c in (PI2_HI, PI2_MID, PI2_LO):
                link(v.scalar_tensor_tensor(out=ang, in0=kq, scalar=-c, in1=ang, op0=ALU.mult, op1=ALU.add))
            link(v.tensor_scalar(ang, ang, 3.1415925, -3.1415925, ALU.min, ALU.max))
            v.scalar_tensor_tensor(out=kq, in0=ang, scalar=-1.0, in1=ang, op0=ALU.mult, op1=ALU.max).then_inc(s["angles"], 1)
            ch.mark(v.tensor_scalar(nscale[:, 0, 0, :], ns_bc[:, 0, :], 1.0, float(FEAT) ** -0.5, ALU.add, ALU.mult))
            ch.mark(v.tensor_scalar(nscale[:, 1, 0, :], ns_bc[:, 1, :], 1.0, None, ALU.add))
            ch.wait()
            ch.mark(v.tensor_copy(nscale[:, :, 1, 16:32], nscale[:, :, 0, 0:16]))
            ch.mark(v.tensor_scalar(nscale[:, :, 1, 0:16], nscale[:, :, 0, 16:32], -1.0, None, ALU.mult))
            ch.wait()
            dve.wait_ge(s["trig"], 1)
            for t in range(2):
                for w, src in ((0, cosb), (1, sinb)):
                    ins = v.tensor_tensor(
                        rope[:, :, 2 * t + w, :].rearrange("p t (u d) -> p t u d", u=2),
                        spread(src, 2, 2),
                        spread(nscale[:, t, w, :].rearrange("p (u d) -> p u d", u=2), 1, TILES), ALU.mult)
            ins.then_inc(s["trig"], 1)
            link(v.scalar_tensor_tensor(out=j8[:], in0=iota8[:], scalar=pf[:, 2:3], in1=sc_bc[:], op0=ALU.is_equal,
                                        op1=ALU.mult, accum_out=pf[:, 3:4]))
            ch.mark(v.tensor_scalar(admask[:], ad_f[:], pf[:, 2:3], pf[:, 3:4], ALU.is_equal, ALU.mult))
            dve.wait_ge(s["masks"], 1)
            ch.mark(v.tensor_tensor(maskA[0:64], spread(rem_bc[0:64, :], 2, ROWS),
                                    spread(kmt[:], 1, SEQS), ALU.is_equal))
            link(v.tensor_tensor(start_bc[:], len_f[:], rem_bc[:], ALU.subtract))
            link(v.tensor_scalar(start_bc[:], start_bc[:], 1.0 / BLOCK, -float(FIRST_ENT), ALU.mult, ALU.add))
            ch.mark(v.tensor_scalar(maskA[64:96], spread(start_bc[64:96, :], 2, ROWS),
                                    negk[64:96, :], None, ALU.is_lt))
            vu = v_upper.rearrange("p (b s) -> p b s", s=3)
            vl = v_lower.rearrange("p (b s) -> p b s", s=3)
            ch.mark(v.tensor_scalar(vu[:, :, 0], rem_bc[:], -1.0, 99.0, ALU.mult, ALU.add))
            ch.mark(v.tensor_copy(vl[:, :, 2], rem_bc[:]))
            ch.wait()
            dve.wait_ge(s["ent_bc"], 16)
            eq3 = eqall.rearrange("p (i e) -> p i e", e=ENT)
            for i in range(WB):
                ch.mark(v.scalar_tensor_tensor(out=eq3[:, i, :], in0=blk_bc, scalar=blkw[:, i:i + 1], in1=e_plus,
                                               op0=ALU.is_equal, op1=ALU.mult))
            ch.wait()
            link(v.tensor_reduce(entf[:, 0:WB], eq3, axis=AX_X, op=ALU.max))
            bd = bounds.rearrange("p (k e) -> p k e", k=2)
            for e in range(3):
                for k, (tab, dst) in enumerate(((v_upper, ub), (v_lower, lo))):
                    link(v.scalar_tensor_tensor(out=bd[:, k, :], in0=eq3[:, FIRST_ENT + e, :], scalar=own[:, e:e + 1],
                                                in1=tab, op0=ALU.is_gt, op1=ALU.mult))
                    link(v.tensor_reduce(dst[:, e:e + 1], bd[:, k, :], axis=AX_X, op=ALU.max))
            link(v.tensor_scalar(ub[:], ub[:], -1.0, 99.0, ALU.mult, ALU.add))
            T = lambda k: tok[:, k, :]
            link(v.tensor_scalar(T(0), iotat[:], idf[:, 0:1], None, ALU.add))
            ch.mark(v.tensor_scalar(T(1), T(0), float(BLOCK), None, ALU.is_ge))
            ch.mark(v.tensor_scalar(T(2), T(0), float(2 * BLOCK), None, ALU.is_ge))
            for k, src in enumerate((ub[:], lo[:], entf[:, FIRST_ENT:FIRST_ENT + 3])):
                ch.mark(v.tensor_tensor(difs[:, k, :], src[:, 1:3], src[:, 0:2], ALU.subtract))
            ch.wait()
            ch.mark(v.scalar_tensor_tensor(out=T(3), in0=T(1), scalar=-float(BLOCK), in1=T(0), op0=ALU.mult, op1=ALU.add))
            for k, src in enumerate((ub[:], lo[:], entf[:, FIRST_ENT:FIRST_ENT + 3])):
                ch.mark(v.tensor_scalar(T(5 + k), T(1), difs[:, k, 0:1], src[:, 0:1], ALU.mult, ALU.add))
            ch.wait()
            ch.mark(v.scalar_tensor_tensor(out=T(4), in0=T(2), scalar=-float(BLOCK), in1=T(3), op0=ALU.mult, op1=ALU.add))
            for k in range(3):
                ch.mark(v.scalar_tensor_tensor(out=T(8 + k), in0=T(2), scalar=difs[:, k, 1:2], in1=T(5 + k),
                                               op0=ALU.mult, op1=ALU.add))
            ch.wait()
            ch.mark(v.tensor_tensor(T(0), T(4), T(8), ALU.is_lt))
            ch.mark(v.tensor_tensor(T(1), T(4), T(9), ALU.is_ge))
            ch.mark(v.tensor_scalar(T(2), T(10), float(BLOCK), float(SKIP - BLOCK), ALU.mult, ALU.add))
            ch.wait()
            ch.mark(v.tensor_tensor(T(3), T(0), T(1), ALU.mult))
            ch.mark(v.tensor_tensor(T(5), T(2), T(4), ALU.add))
            ch.wait()
            v.scalar_tensor_tensor(out=rows_i[:], in0=T(3), scalar=-float(SKIP), in1=T(5), op0=ALU.mult,
                                   op1=ALU.add).then_inc(s["row_idx"], 1)
            link(v.tensor_scalar(junk[:, 0:WB], entf[:, 0:WB], 0.0, None, ALU.is_gt))
            ch.mark(v.memset(win_i[:], SKIP))
            link(v.tensor_scalar(junk[:, 16:16 + WB], entf[:, 0:WB], float(SKIP - 1), None, ALU.add))
            v.scalar_tensor_tensor(out=win_i[:, 0, 0:WB], in0=junk[:, 0:WB], scalar=float(SKIP), in1=blkw[:, 0:WB],
                                   op0=ALU.mult, op1=ALU.add).then_inc(s["win_idx"], 1)
            v.scalar_tensor_tensor(out=win_i[:, 1, 0:WB], in0=junk[:, 0:WB], scalar=-float(SKIP), in1=junk[:, 16:16 + WB],
                                   op0=ALU.mult, op1=ALU.add).then_inc(s["win_idx"], 1)

            def add1(n, j):
                dve.wait_ge(s["l0"], n + 1)
                wait_from(dve, s["l1"], n - 1)
                v.tensor_tensor(x1s[:, j, :], xres[:, bass.ds(n, 1), :].rearrange("p o f -> p (o f)"),
                                psMix[j][:, 0:256], ALU.add).then_inc(s["x1"], 1)

            def add2(n, j):
                dve.wait_ge(s["l1"], n + 1)
                wait_from(dve, s["xt"], n - 1)
                wait_from(dve, s["xcopy"], n - 1)
                v.tensor_tensor(x2s[:, j, :], x1s[:, j, :], psMix[j][:, 0:256], ALU.add).then_inc(s["x2"], 1)

            def sumsq(n, j):
                dve.wait_ge(s["square"], n + 1)
                wait_from(dve, s["root"], n - 1)
                v.tensor_reduce(ss[:, j, :], sq[:, j, :].rearrange("p (h d) -> p h d", d=HD), axis=AX_X,
                                op=ALU.add).then_inc(s["sumsq"], 1)

            def norm(n, j):
                dve.wait_ge(s["root"], n + 1)
                ch.link(v.reciprocal(ri[:, j, :], sd[:, j, :]))
                wait_from(dve, s["swap"], n - 1)
                v.tensor_tensor(qn[:, j, :].rearrange("p (h d) -> p h d", d=HD),
                                psQKV[j][:, 0:384].rearrange("p (h d) -> p h d", d=HD),
                                spread(ri[:, j, :], 2, HD), ALU.mult
                                ).then_inc(s["norm"], 1)

            def rotate(n, j):
                dve.wait_ge(s["norm"], n + 1)
                for a_, b_, w in ((0, 8, 0), (8, 12, 2)):
                    ch.mark(v.tensor_tensor(rc[:, j, 32 * a_:32 * b_].rearrange("p (h d) -> p h d", d=HD),
                                            qn[:, j, 32 * a_:32 * b_].rearrange("p (h d) -> p h d", d=HD),
                                            spread(drop(rope[:, bass.ds(n, 1), w, :]), 1, b_ - a_), ALU.mult))

            def finish(n, j, i):
                ch.wait()
                dve.wait_ge(s["swap"], n + 1)
                wait_from(dve, s["qt"], n - 1)
                wait_from(dve, s_scat[j], i * 16)
                v.tensor_tensor(stage[:, j, 0:384], rc[:, j, :], rs[:, j, :], ALU.add).then_inc(s["roped"], 1)

            def part2(i, s1, s2, s3):
                if s1:
                    for j in range(2):
                        add1(i * 2 + 4 + j, j)
                if s3:
                    for j in range(2):
                        rotate(i * 2 + j, j)
                if s1:
                    for j in range(2):
                        add2(i * 2 + 4 + j, j)
                if s2:
                    for j in range(2):
                        sumsq(i * 2 + 2 + j, j)
                if s3:
                    for j in range(2):
                        finish(i * 2 + j, j, i)
                if s2:
                    for j in range(2):
                        norm(i * 2 + 2 + j, j)

            dve.wait_ge(s["ld_x"], 16)
            part2(-2, True, False, False)
            part2(-1, True, True, False)
            part2(0, True, True, True)
            base = ch.base + ch.n
            with dve.Fori(1, PAIRS - 2) as i:
                ch.start(base + (i - 1) * 6)
                part2(i, True, True, True)
                assert ch.n == 6
            ch.start(base + 6 * (PAIRS - 3))
            part2(PAIRS - 2, False, True, True)
            part2(PAIRS - 1, False, False, True)

            for e in range(3):
                dve.wait_ge(s_pk_in[e % 2], 16 * (e // 2 + 1))
                if e == 2:
                    dve.wait_ge(s_pk_out[0], 32)
                v.tensor_copy(block_in[:, e % 2, 0, :].rearrange("p (g t d) -> p g t d", g=KVH, d=HD),
                              region[:, e % 2, :].rearrange("p (t k g d) -> p k g t d", t=BLOCK, k=2, g=KVH)[:, 0]
                              ).then_inc(s["pk_rek"], 1)

            def queries(m, par, first):
                if not first:
                    dve.wait_ge(s["scores"], m * 4 - 4)
                for h in range(KVH):
                    ins = v.tensor_copy(
                        qbd[32 * h:32 * h + 32, par, :, h // 2, 64 * (h % 2):64 * (h % 2) + 64].rearrange("p b (u t) -> p b u t", u=2),
                        qtres[32 * h:32 * h + 32, bass.ds(m, 1), :].rearrange("p o (u b t) -> p (o b) u t", u=2, b=SPT))
                    if h < KVH - 1:
                        ch.mark(ins)
                ins.then_inc(s["qbd"], 1)

            def maxes(n, b):
                dve.wait_ge(s["scores"], n + 1)
                v.tensor_reduce(negm[:, b % 2, :], psS[b % 2][:, 0:2 * KEYS].rearrange("p (c k) -> p c k", c=2),
                                axis=AX_X, op=ALU.max, negate=True).then_inc(s["negmax"], 1)

            def probT_out(n, b):
                dve.wait_ge(s["pt"], n + 1)
                if not (isinstance(n, int) and n < 2):
                    dve.wait_ge(s["pv"], n - 1)
                v.tensor_copy(probT[:, b % 2].rearrange("p a c q -> p (a c q)"), psP[b % 2][0:HALF, :]).then_inc(s["pte"], 1)

            def heads_out(m, par):
                dve.wait_ge(s["pv"], m * 4 + 4)
                ch.link(v.reciprocal(rinv[:], sums[:, par]))
                ov = psO[:].rearrange("p (b c g d) -> p g c b d", b=SPT, c=2, g=2)
                for h in range(2):
                    ins = v.tensor_tensor(osb[64 * h:64 * h + 64], ov[64 * h:64 * h + 64, h],
                                          spread(rinv[64 * h:64 * h + 64].rearrange("p b c -> p c b"), 3, HD),
                                          ALU.mult)
                    if h == 0:
                        ch.mark(ins)
                ins.then_inc(s["oev"], 1)

            def heads_T(m):
                dve.wait_ge(s["oev"], m + 1)
                ch.wait()
                wait_from(dve, s["wo"], m)
                v.transpose(oT.rearrange("p c n -> p (c n)"), osb.rearrange("p c b d -> p (c b d)")).then_inc(s["oT"], 1)

            def add3(m):
                dve.wait_ge(s["wo"], m + 1)
                v.tensor_tensor(x3s, xres[:, bass.ds(m, 1), :].rearrange("p o f -> p (o f)"), psZ[:, 0:256],
                                ALU.add).then_inc(s["x3"], 1)

            def adapt_in(m):
                dve.wait_ge(s["xa"], m + 1)
                v.tensor_tensor(xam.rearrange("p (b t) -> p b t", b=SPT), psZ[:, 0:P].rearrange("p (b t) -> p b t", b=SPT),
                                spread(admask[:, bass.ds(m * SPT, SPT)], 2, ROWS),
                                ALU.mult).then_inc(s["xam"], 1)

            def add4(m, par):
                dve.wait_ge(s["l3"], m + 1)
                if isinstance(m, int) and m < 2:
                    pass
                else:
                    dve.wait_ge(s_out[par], (m - par) * 8)
                v.tensor_tensor(ys[:, par, :], x3s, psZ[:, 256:512], ALU.add).then_inc(s["y"], 1)

            def turn(grp, kv):
                dve.wait_ge(s["raw_v" if kv else "raw_k"], grp * 32 + 32)
                if not (isinstance(grp, int) and grp < 1):
                    dve.wait_ge(s["unit"], grp * UNITS - (8 if kv else 4))
                v.tensor_copy(block_in[0:GR, 1, kv, :].rearrange("p (t g d) -> p t g d", t=BLOCK, g=KVH),
                              block_in[0:GR, 0, kv, :].rearrange("p (g t d) -> p t g d", g=KVH, d=HD)).then_inc(s["turned"], 1)

            def group(grp, first, last, turns):
                for b in range(SPG):
                    n = grp * SPG + b
                    if not (last and b == SPG - 1):
                        maxes(n + 1, b + 1)
                    k, t = b % 4, grp * 2 + (b // 4 - 1)
                    if k == 0 and not first:
                        adapt_in(t - 1)
                    if k == 0 and first and b == 4:
                        pass
                    if not (first and b < 4):
                        if k == 1:
                            heads_T(t)
                        if k == 2:
                            add3(t)
                    probT_out(n, b)
                    if k == 1 and not first:
                        add4(t - 1, b // 4)
                    if k == 1 and not (last and b > 4):
                        queries(grp * 2 + (b // 4 + 1), (b // 4 + 1) % 2, first and b < 4)
                    if k == 0 and not (first and b == 0):
                        heads_out(t, (b // 4 + 1) % 2)
                    if k == 3 and turns:
                        turn(grp + 2, 1 - b // 4)

            for grp in range(2):
                for kv in (1, 0):
                    turn(grp, kv)
                if grp == 0:
                    dve.wait_ge(s["qte"], TILES)
                    dve.wait_ge(s["xcopy"], TILES)
                    dve.wait_ge(s["qzero"], 1)
                    queries(0, 0, True)
            maxes(0, 0)
            group(0, True, False, True)
            base = ch.base + ch.n
            with dve.Fori(1, GROUPS - 2) as grp:
                ch.start(base + (grp - 1) * 10)
                group(grp, False, False, True)
                assert ch.n == 10
            ch.start(base + 10 * (GROUPS - 3))
            group(GROUPS - 2, False, False, False)
            group(GROUPS - 1, False, True, False)
            adapt_in(TILES - 2)
            heads_out(TILES - 1, 1)
            heads_T(TILES - 1)
            add4(TILES - 2, 0)
            add3(TILES - 1)
            adapt_in(TILES - 1)
            add4(TILES - 1, 1)

        @block.tensor
        def _(pe):
            t_ = nc.tensor
            pe.wait_ge(s["consts"], 1)
            pe.wait_ge(s["ld_w"], 16 * N_W)
            pe.wait_ge(s["ld_idx"], 16 * N_IDX)
            packs = [[wqkv_raw[:, o, 0:P] for o in range(4)],
                     [wqkv_raw[:, o, P:2 * P] for o in range(4)],
                     [wo_raw[:, o, P * c:P * c + P] for c in range(2) for o in range(2)],
                     [w3_raw[:, o, P * c:P * c + P] for c in range(2) for o in range(2)],
                     [la_raw[:, 0:P], la_raw[:, P:2 * P], lb_raw[:, 0, :], lb_raw[:, 1, :]]]
            for n, pack in enumerate(packs):
                if n >= 2:
                    pe.wait_ge(s["wt_ev"], n - 1)
                for k, src in enumerate(pack):
                    ins = t_.transpose(ps[n % 2][:, P * k:P * k + P], src, ident[:])
                ins.then_inc(s["wt_pe"], 1)
            pe.wait_ge(s["wt_ev"], 5)

            def mix0(n, j):
                pe.wait_ge(s["wbd"], n + 1)
                wait_from(pe, s["x2"], n - 1)
                t_.matmul(psMix[j][:, 0:256], wbd[:, j, 0, :],
                          xres[:, bass.ds(n, 1), :].rearrange("p o f -> p (o f)"), start=True, stop=True).then_inc(s["l0"], 1)

            def mix1(n, j):
                pe.wait_ge(s["x1"], n + 1)
                t_.matmul(psMix[j][:, 0:256], wbd[:, j, 1, :], x1s[:, j, :], start=True, stop=True
                          ).then_inc(s["l1"], 1)

            def xT(n, j):
                pe.wait_ge(s["x2"], n + 1)
                wait_from(pe, s["xte"], n - 1)
                for c in range(2):
                    ins = t_.transpose(psT[j][:, P * c:P * c + P], x2s[:, j, P * c:P * c + P], ident[:])
                ins.then_inc(s["xt"], 1)

            def qkv(n, j):
                pe.wait_ge(s["xte"], n + 1)
                wait_from(pe, s["norm"], n - 1)
                wait_from(pe, s["vcopy"], n - 1)
                for c in range(2):
                    ins = t_.matmul(psQKV[j][:, :], x2T[:, j, c, :], wqkvT[:, c, :], start=(c == 0), stop=(c == 1))
                ins.then_inc(s["qkv"], 1)

            def qT(n, j):
                pe.wait_ge(s["roped"], n + 1)
                wait_from(pe, s["qte"], n - 1)
                for u in range(2):
                    ins = t_.transpose(psQT[j][:, P * u:P * u + P], stage[:, j, P * u:P * u + P], ident[:])
                ins.then_inc(s["qt"], 1)

            def part2(i, s1, s2, s3):
                if s1:
                    for j in range(2):
                        mix0(i * 2 + 4 + j, j)
                if s2:
                    qkv(i * 2 + 2, 0)
                if s1:
                    for j in range(2):
                        mix1(i * 2 + 4 + j, j)
                if s2:
                    qkv(i * 2 + 3, 1)
                if s1:
                    for j in range(2):
                        xT(i * 2 + 4 + j, j)
                if s3:
                    for j in range(2):
                        qT(i * 2 + j, j)

            pe.wait_ge(s["ld_x"], 16)
            part2(-2, True, False, False)
            part2(-1, True, True, False)
            part2(0, True, True, True)
            with pe.Fori(1, PAIRS - 2) as i:
                part2(i, True, True, True)
            part2(PAIRS - 2, False, True, True)
            part2(PAIRS - 1, False, False, True)
            pe.wait_ge(s["qte"], TILES)
            pe.wait_ge(s["norm"], TILES)

            def unit(grp, u, first):
                if not (first and u < 2):
                    pe.wait_ge(s["unite"], grp * UNITS + (u - 1))
                if u % 4 == 0 and u < 8:
                    pe.wait_ge(s["turned"], grp * 2 + (u // 4 + 1))
                if u < 8:
                    kv = 1 if u < 4 else 0
                    for o in range(4):
                        off = 4 * (u % 4) + o
                        ins = t_.transpose(psR[u % 2][:, o * GR:(o + 1) * GR], block_in[0:GR, 1, kv, P * off:P * off + P],
                                           ident[0:GR, 0:GR])
                else:
                    if u == 8:
                        pe.wait_ge(s["unite"], grp * UNITS + 4)
                    for k in range(2):
                        b = 2 * (u - 8) + k
                        for h in range(2):
                            ins = t_.transpose(psR[u % 2][0:HALF, P * (2 * k + h):P * (2 * k + h) + P],
                                               vT[:, b, HALF * h:HALF * h + HALF], ident[:])
                ins.then_inc(s["unit"], 1)

            def scores(n, b, par, grp, m):
                if not (isinstance(n, int) and n < 2):
                    pe.wait_ge(s["expd"], n - 1)
                if b % 4 == 0:
                    pe.wait_ge(s["qbd"], m + 1)
                    pe.wait_ge(s["mask4"], m + 1)
                if b == 0:
                    pe.wait_ge(s["unite"], grp * UNITS + 8)
                both = psS[b % 2][:, 0:2 * KEYS].rearrange("p (c k) -> p c k", c=2)
                t_.matmul(both, mask4[:, (b // 4) % 2, b % 4, :], spread(maskB[:].rearrange("p o i -> p (o i)"), 1, 2),
                          start=True, stop=True, skip_group_check=True)
                for c in range(2):
                    ins = t_.matmul(psS[b % 2][:, c * KEYS:(c + 1) * KEYS], qbd[:, (b // 4) % 2, b % 4, c, :],
                                    kT[:, bass.ds(par, 1), :, WS * b:WS * b + WB].rearrange("p u o i -> p (u o) i"),
                                    start=False, stop=True, skip_group_check=True)
                ins.then_inc(s["scores"], 1)

            def probs_T(n, b):
                pe.wait_ge(s["expd"], n + 1)
                if not (isinstance(n, int) and n < 2):
                    pe.wait_ge(s["pte"], n - 1)
                for h in range(2):
                    for c in range(2):
                        ins = t_.transpose(psP[b % 2][0:HALF, 256 * h + P * c:256 * h + P * c + P],
                                           prob[:, b % 2, c, HALF * h:HALF * h + HALF], ident[:])
                ins.then_inc(s["pt"], 1)

            def values(n, b, par, grp, m):
                pe.wait_ge(s["pte"], n + 1)
                if b == 0:
                    pe.wait_ge(s["unite"], grp * UNITS + UNITS)
                if b % 4 == 0:
                    wait_from(pe, s["oev"], m)
                for c in range(2):
                    for h in range(2):
                        ins = t_.matmul(psO[:, P * (b % 4) + 64 * c:P * (b % 4) + 64 * c + 64], probT[:, b % 2, h, c, :],
                                        drop(vnat[0:HALF, bass.ds(par, 1), 256 * b + P * h + 64 * c:256 * b + P * h + 64 * c + 64]),
                                        start=(h == 0), stop=(h == 1))
                ins.then_inc(s["pv"], 1)

            def project(m):
                pe.wait_ge(s["oT"], m + 1)
                wait_from(pe, s["y"], m)
                for c in range(2):
                    ins = t_.matmul(psZ[:, 0:256], oT[:, c, :], woT[:, c, :], start=(c == 0), stop=(c == 1))
                ins.then_inc(s["wo"], 1)

            def x3_T(m):
                pe.wait_ge(s["x3"], m + 1)
                wait_from(pe, s["y"], m)
                for c in range(2):
                    ins = t_.transpose(psZ[:, 256 + P * c:256 + P * c + P], x3s[:, P * c:P * c + P], ident[:])
                ins.then_inc(s["x3t"], 1)

            def adapter(m):
                pe.wait_ge(s["x3te"], m + 1)
                for c in range(2):
                    ins = t_.matmul(psZ[:, 0:P], laT[:, c, :], x3T[:, c, :], start=(c == 0), stop=(c == 1))
                ins.then_inc(s["xa"], 1)

            def last(m):
                pe.wait_ge(s["xam"], m + 1)
                for c in range(2):
                    t_.matmul(psZ[:, 256:512], x3T[:, c, :], w3T[:, c, :], start=(c == 0), stop=False)
                t_.matmul(psZ[:, 256:512], xam, lbT[:], start=False, stop=True).then_inc(s["l3"], 1)

            def group(grp, first, final):
                for b in range(SPG):
                    n, k, t = grp * SPG + b, b % 4, grp * 2 + (b // 4 - 1)
                    if not (final and b == SPG - 1):
                        wrap = (b + 1) // SPG
                        scores(n + 1, (b + 1) % SPG, (grp + wrap) % 2, grp + wrap, grp * 2 + (b + 1) // 4)
                    if k < 2 and not first:
                        (adapter, last)[k](t - 1)
                    if k >= 2 and not (first and b < 4):
                        (project, x3_T)[k - 2](t)
                    if not final:
                        for u in UNITS_AT[b]:
                            unit(grp + 1, u, False)
                    probs_T(n, b)
                    if b > 0:
                        values(n - 1, b - 1, grp % 2, grp, grp * 2 + (b - 1) // 4)
                    elif not (first and b == 0):
                        values(n - 1, SPG - 1, (grp + 1) % 2, grp - 1, grp * 2 - 1)

            for u in range(UNITS):
                unit(0, u, True)
            scores(0, 0, 0, 0, 0)
            group(0, True, False)
            with pe.Fori(1, GROUPS - 1) as grp:
                group(grp, False, False)
            group(GROUPS - 1, False, True)
            values(SEQS - 1, SPG - 1, (GROUPS - 1) % 2, GROUPS - 1, TILES - 1)
            adapter(TILES - 2)
            last(TILES - 2)
            project(TILES - 1)
            x3_T(TILES - 1)
            adapter(TILES - 1)
            last(TILES - 1)


_INS = ("x", "itok_B_0_7", "itok_B_1_198", "itok_Bx257_0_4111", "itok_B_37_3939", "itok_B_0_6",
        "L0_cond_weights", "L1_cond_weights", "L2_cond_Wq", "L2_cond_Wk", "L2_cond_Wv", "L2_cond_Wo",
        "L2_cond_q_norm_scale", "L2_cond_k_norm_scale", "L2_cond_k_blocks", "L2_cond_v_blocks",
        "L3_cond_W", "L3_cond_A", "L3_cond_Bm", "L3_cond_scalings")


def kernel(**inputs):
    import numpy as _np
    import concourse.bacc as _bacc
    from concourse import mybir as _mybir
    from concourse.bass_utils import run_bass_kernel_spmd as _run

    nc = _bacc.Bacc("TRN2", target_bir_lowering=False, num_devices=1)
    arrays, args = {}, []
    for name in _INS:
        a = _np.ascontiguousarray(inputs[name])
        arrays[f"in_{name}"] = a
        args.append(nc.dram_tensor(f"in_{name}", a.shape, _mybir.dt.from_np(a.dtype), kind="ExternalInput").ap())
    out = nc.dram_tensor("out", (SEQS, ROWS, FEAT), _mybir.dt.float32, kind="ExternalOutput").ap()
    build(nc, *args, out)
    r = _run(nc, [arrays], core_ids=[0])
    return r.results[0]["out"]
```

```python
from contextlib import ExitStack

import numpy as np

import concourse.bass as bass
from concourse import mybir

ALU = mybir.AluOpType
ACT = mybir.ActivationFunctionType
F32 = mybir.dt.float32
BF16 = mybir.dt.bfloat16
I32 = mybir.dt.int32
AX_X = mybir.AxisListType.X

P = 128
SEQS = 128
ROWS = 32
FEAT = 256
TILES = 32
PAIRS = TILES // 2
SPT = 4
HEADS, KVH, HD = 8, 4, 32
BLOCK = 16
BLKW = KVH * BLOCK * HD
NBLOCKS = 16 * 257
SLOTS = 257
WINDOW = 128
WB = 11
WS = 12
SPG = 8
GROUPS = SEQS // SPG
GR = SPG * WS
KEYS = WB * BLOCK
HALF = KEYS // 2
ENT = 3 * SEQS
FIRST_ENT = WINDOW // BLOCK
SKIP = 65536
ADAPTERS, RANK = 8, 16
UNITS = 4
UNITS_AT = ((), (), (0, 1), (2, 3), (), (), (), ())
TURN_AT = {0: (1, 0, BLOCK // 2), 1: (1, BLOCK // 2, BLOCK // 2), 3: (0, 0, BLOCK // 2), 4: (0, BLOCK // 2, BLOCK // 2)}
NEG = -1.0e30
EPS = 1e-6
MAGIC = 12582912.0
TWO_PI = 6.283185307179586
PI2_HI = 6.28125
PI2_MID = float(np.float32(round((TWO_PI - PI2_HI) * 2**21) / 2**21))
PI2_LO = TWO_PI - PI2_HI - PI2_MID


class Chain:

    def __init__(self, engine, sem):
        self.engine, self.sem, self.base, self.n = engine, sem, 0, 0

    def mark(self, instruction):
        instruction.then_inc(self.sem, 1)
        self.n += 1

    def wait(self):
        self.engine.wait_ge(self.sem, self.base + self.n)

    def link(self, instruction):
        self.mark(instruction)
        self.wait()

    def start(self, base):
        self.base, self.n = base, 0


def spread(ap, axis, n):
    ap = ap.unsqueeze(axis)
    shape = list(ap.shape)
    shape[axis] = n
    return ap.broadcast_to(shape)


def drop(ap):
    return ap.rearrange("p o n -> p (o n)")


def wait_from(engine, sem, value):
    if isinstance(value, int) and value <= 0:
        return
    engine.wait_ge(sem, value)


def build(nc, x, subj, cond, table, lens, adapt, w0, w1, wq, wk, wv, wo, qns, kns, kblk, vblk,
          w3, la, lb, lsc, out):
    with ExitStack() as ctx:
        ctx.enter_context(nc.allow_non_contiguous_dma(reason="index columns and adapter factors"))

        def sb(name, shape, dt=F32):
            return ctx.enter_context(nc.sbuf_tensor(name, shape, dt))

        def sem(name):
            return ctx.enter_context(nc.semaphore(name))

        def dram(name, shape, dt=F32):
            return nc.dram_tensor(name, shape, dt).ap()

        d_mix = dram("mix_scratch", [2, SEQS, ROWS * ROWS])
        d_ent = dram("entry_scratch", [SEQS, 3])
        d_win = dram("window_scratch", [2, SEQS, WS], I32)
        d_row = dram("row_scratch", [SEQS, ROWS], I32)
        d_new = dram("new_scratch", [ENT * BLOCK, 2 * KVH * HD])

        xres = sb("xres", [P, TILES, FEAT])
        qtres = sb("qtres", [P, TILES, 256])
        block_in = sb("block_in", [P, 2, 2 * BLKW])
        blk_raw = block_in[:].rearrange("p a (k n) -> p a k n", k=2)
        r1 = sb("window", [P, 2 * 1536 + 1536 + 2 * 2048])
        region = r1[:, 0:2 * 4096].rearrange("p (a n) -> p a n", a=2)
        rp = sb("rope", [P, TILES * 4 * HD])
        rope = rp[:].rearrange("p (t w d) -> p t w d", w=4, d=HD)
        ident = sb("ident", [P, P])
        work2 = sb("work2", [P, 2 * BLKW])
        turned = [block_in[:, 1], work2[:]]
        wqkvT = work2[:, 2048:3072].rearrange("p (c n) -> p c n", c=2)
        woT = sb("woT", [P, 2, 256])
        w3T = sb("w3T", [P, 2, 256])
        laT = sb("laT", [P, 2, P])
        lbT = sb("lbT", [P, 256])
        mixw = work2[:, 0:2048].rearrange("p (l t d) -> p l t d", l=2, t=TILES)
        bdmask = sb("bdmask", [P, SPT, ROWS])
        maskA = sb("maskA", [96, SEQS, ROWS], BF16)
        maskB = sb("maskB", [96, WB, BLOCK], BF16)
        mask4 = sb("mask4", [96, 2, SPT, P], BF16)
        admask = sb("admask", [P, SEQS])
        rowidx = sb("rowidx", [P, TILES], I32)
        winidx = sb("winidx", [GR, 2, GROUPS], I32)
        rowcol = sb("rowcol", [P, 2], I32)
        wincol = sb("wincol", [GR, 2, 2], I32)

        kT = r1[:, 0:2 * GR * BLOCK].rearrange("p (u r t) -> p u r t", u=2, t=BLOCK)
        vnat = r1[0:HALF, 2 * GR * BLOCK:2 * GR * BLOCK + 2 * SPG * 256].rearrange("p (u b h n) -> p u b h n", u=2, b=SPG, h=2)

        q1 = qtres[:].rearrange("p a n -> p (a n)")
        used = [0]

        def tmp(n, dt=F32):
            a = q1[:, used[0]:used[0] + n]
            used[0] += n
            return a if dt == F32 else a.bitcast(dt)

        eqall = tmp(WB * ENT)
        blk_bc = tmp(ENT)
        e_plus = tmp(ENT)
        v_upper = tmp(ENT)
        v_lower = tmp(ENT)
        rel = tmp(SLOTS)
        tabf = tmp(SLOTS)
        junk = tmp(SLOTS)

        tabi = tmp(SLOTS, I32)
        leni = sb("leni", [P, 1], I32)
        remi = sb("remi", [P, 1], I32)
        len_rem = sb("len_rem", [P, 2, SEQS])
        lens_bc = len_rem[:, 0].bitcast(I32)
        rem_bci = len_rem[:, 1].bitcast(I32)
        lent = sb("lent", [P, TILES], I32)
        adapt_bc = sb("adapt_bc", [P, SEQS], I32)
        mixi = sb("mixi", [P, 2], I32)
        sc_bc = sb("sc_bc", [P, ADAPTERS])
        ns_bc = sb("ns_bc", [P, 2, HD])
        idf = sb("idf", [P, 24])
        rem_bc = sb("rem_bc", [P, SEQS])
        len_f = sb("len_f", [P, SEQS])
        start_bc = sb("start_bc", [P, SEQS])
        blkw = sb("blkw", [P, WS])
        entf = sb("entf", [P, WS])
        enti = sb("enti", [P, 3], I32)
        own = sb("own", [P, 3])
        later = sb("later", [P, 2, 3])
        ub, lo = later[:, 0], later[:, 1]
        difs = sb("difs", [P, 3, 2])
        tok = sb("tok", [P, 12, ROWS])
        rows_i = sb("rows_i", [P, ROWS], I32)
        win_i = sb("win_i", [P, 2, WS], I32)
        pidx = sb("pidx", [P, 4], I32)
        pf = sb("pf", [P, 4])
        ad_f = sb("ad_f", [P, SEQS])
        kmt = sb("kmt", [64, ROWS])
        negk = sb("negk", [P, 1])
        iota8 = sb("iota8", [P, ADAPTERS])
        iotat = sb("iotat", [P, ROWS])
        j8 = sb("j8", [P, ADAPTERS])
        invf = sb("invf", [P, 16])
        pos = sb("pos", [P, TILES])
        nscale = sb("nscale", [P, 2, 2, HD])
        halfpi = sb("halfpi", [P, 1])
        gates = sb("gates", [1, 4])
        epsb = sb("epsb", [P, 1])
        ang = r1[:, 0:512].rearrange("p (t j) -> p t j", j=16)
        kq = r1[:, 512:1024].rearrange("p (t j) -> p t j", j=16)
        cosb = r1[:, 1024:1536].rearrange("p (t j) -> p t j", j=16)
        sinb = r1[:, 1536:2048].rearrange("p (t j) -> p t j", j=16)

        wraw = block_in[:, 1]
        wqkv_raw = wraw[:, 0:1024].rearrange("p (o f) -> p o f", o=4)
        wo_raw = wraw[:, 1024:1536].rearrange("p (o f) -> p o f", o=2)
        w3_raw = wraw[:, 1536:2048].rearrange("p (o f) -> p o f", o=2)
        la_raw = wraw[:, 2048:2304]
        lb_raw = wraw[:, 2304:2560].rearrange("p (c n) -> p c n", c=2)
        mix_raw = r1[:, 2048:4096].rearrange("p (l n) -> p l n", l=2)

        wbd = sb("wbd", [P, 2, 2, SPT * ROWS])
        x1s = work2[:, 3072:3584].rearrange("p (j f) -> p j f", j=2)
        x2s = work2[:, 3584:4096].rearrange("p (j f) -> p j f", j=2)
        x2T = sb("x2T", [P, 2, 2, P])
        early = sb("early", [P, 4, 2, 384])
        sq, qn, rc, rs = (early[:, k] for k in range(4))
        ss = sb("ss", [P, 2, 12])
        sd = sb("sd", [P, 2, 12])
        ri = sb("ri", [P, 2, 12])
        stage = sb("stage", [P, 2, 512])
        vnew = len_rem[:]

        qbd = rp[:, 0:2048].rearrange("p (a b c q) -> p a b c q", a=2, b=SPT, c=2)
        prob = rp[:, 2048:2048 + 4 * KEYS].rearrange("p (a c k) -> p a c k", a=2, c=2)
        negm = sb("negm", [P, 2, 2])
        sums = sb("sums", [P, 2, 2])
        rinv = sb("rinv", [P, 2, 2])
        probT = rp[0:HALF, 3072:4096].rearrange("p (a h c q) -> p a h c q", a=2, h=2, c=2)
        e1 = early[:].rearrange("p a b n -> p (a b n)")
        oT = e1[:, 256:512].rearrange("p (c n) -> p c n", c=2)
        x3s = e1[:, 512:768]
        x3T = e1[:, 768:1024].rearrange("p (c n) -> p c n", c=2)
        xam = e1[:, 1024:1152]
        ys = e1[:, 1152:1664].rearrange("p (a n) -> p a n", a=2)

        ps = [ctx.enter_context(nc.psum_tensor(f"bank{i}", [P, 512], F32)) for i in range(8)]
        psMix, psT, psQKV, psQT = [ps[0], ps[1]], [ps[2], ps[3]], [ps[4], ps[5]], [ps[6], ps[7]]
        psS = [ps[0], ps[1]]
        psP = [ps[2], ps[3]]
        psR = [ps[4], ps[5]]
        psO, psZ = ps[6], ps[7]

        s = {n: sem(n) for n in (
            "ld_mix", "ld_idx", "ld_w", "ld_x", "ld_x_rest", "consts", "maskA", "mix_gather", "mix_store", "mix_load",
            "ent_out", "ent_bc", "win_out", "win_in", "row_out", "row_in", "ent_idx", "angles", "trig",
            "blk_in0", "blk_in1", "blk_re", "blk_st0", "blk_st1", "wt_pe", "wt_ev", "pool_chain", "dve_chain",
            "wbd", "l0", "x1", "l1", "x2", "xcopy", "xt", "xte", "qkv", "square", "sumsq", "root", "norm",
            "swap", "roped", "vcopy", "qt", "qte", "scat0", "scat1", "vrow",
            "raw_v", "raw_k", "patched0", "patched1", "v_out0", "v_out1", "v_in0", "v_in1",
            "scores", "negmax", "expd", "pt", "pte", "pv", "unit", "unite", "qbd",
            "normed", "oT", "win_idx", "row_idx", "turned", "mask4", "qzero", "masks",
            "wo", "x3", "x3t", "x3te", "xa", "xam", "l3", "y", "out0", "out1")}
        s_scat = [s["scat0"], s["scat1"]]
        s_out = [s["out0"], s["out1"]]
        s_v_out, s_v_in = [s["v_out0"], s["v_out1"]], [s["v_in0"], s["v_in1"]]
        s_patched = [s["patched0"], s["patched1"]]
        s_blk_in, s_blk_st = [s["blk_in0"], s["blk_in1"]], [s["blk_st0"], s["blk_st1"]]
        N_IDX, N_W = 11, 19
        X_FIRST = 8

        d_new_blocks = d_new.rearrange("(b s t) n -> s b (t n)", s=3, t=BLOCK)
        d_val = dram("value_scratch", [2, GR * BLOCK, KVH * HD])
        d_patched = d_new.rearrange("(e t) n -> e (t n)", t=BLOCK)
        kflat = kblk.rearrange("n g t d -> n (g t d)")
        vflat = vblk.rearrange("n g t d -> n (g t d)")

        def col(v):
            return v.rearrange("(b o) -> b o", o=1)

        def bcast(v, n):
            return v.partition_broadcast(n)

        block = ctx.enter_context(nc.Block())

        @block.sync
        def _(sp):
            sp.dma_start(mixi[:, 0:1], col(subj)).then_inc(s["ld_mix"], 16)
            sp.dma_start(mixi[:, 1:2], col(cond)).then_inc(s["ld_mix"], 16)
            il = s["ld_idx"]
            sp.dma_start(leni[:], col(lens)).then_inc(il, 16)
            sp.dma_start(tabi, table).then_inc(il, 16)
            sp.dma_start(lens_bc, bcast(lens, P)).then_inc(il, 16)
            for b in range(SPT):
                sp.dma_start(lent[32 * b:32 * b + 32, :],
                             lens.rearrange("(t b) -> b t", b=SPT)[b].partition_broadcast(ROWS)).then_inc(il, 16)
            sp.dma_start(adapt_bc[:], bcast(adapt, P)).then_inc(il, 16)
            sp.dma_start(sc_bc[:], bcast(lsc, P)).then_inc(il, 16)
            sp.dma_start(ns_bc[:, 0, :], bcast(qns, P)).then_inc(il, 16)
            sp.dma_start(ns_bc[:, 1, :], bcast(kns, P)).then_inc(il, 16)
            wl = s["ld_w"]
            sp.dma_start(la_raw, la.rearrange("a r f -> (a r) f")).then_inc(wl, 16)
            for o in range(2):
                for h in range(KVH):
                    sp.dma_start(wqkv_raw[HD * h:HD * h + HD, o, :],
                                 wq[HD * (2 * h + o):HD * (2 * h + o) + HD, :]).then_inc(wl, 16)
                for u in range(2):
                    sp.dma_start(wo_raw[:, o, P * u:P * u + P].rearrange("p (g d) -> p g d", d=HD),
                                 wo[P * o:P * o + P, :].rearrange("o (g u d) -> u o g d", u=2, d=HD)[u]).then_inc(wl, 16)
                sp.dma_start(w3_raw[:, o, :], w3[P * o:P * o + P, :]).then_inc(wl, 16)
                sp.dma_start(lb_raw[:, o, :].rearrange("p (a r) -> p a r", a=ADAPTERS),
                             lb[:, P * o:P * o + P, :].rearrange("a o r -> o a r")).then_inc(wl, 16)
            sp.dma_start(wqkv_raw[:, 2, :], wk).then_inc(wl, 16)
            sp.dma_start(wqkv_raw[:, 3, :], wv).then_inc(wl, 16)
            x_rows = x.rearrange("(t b) c f -> (b c) t f", b=SPT)
            sp.dma_start(xres[:, 0:X_FIRST, :], x_rows[:, 0:X_FIRST, :]).then_inc(s["ld_x"], 16)
            sp.wait_ge(s["mix_gather"], 32)
            sp.dma_start(d_mix.rearrange("l b n -> b l n"), mix_raw).then_inc(s["mix_store"], 16)
            sp.wait_ge(s["ent_idx"], 1)
            sp.dma_start(d_ent, blkw[:, FIRST_ENT:FIRST_ENT + 3]).then_inc(s["ent_out"], 16)
            sp.wait_ge(s["mix_store"], 16)
            for l in range(2):
                sp.dma_start(mixw[:, l, :, :], d_mix[l].rearrange("(t b) (c d) -> (b c) t d", b=SPT, d=ROWS)
                             ).then_inc(s["mix_load"], 16)
            sp.wait_ge(s["ent_out"], 16)
            sp.dma_start(blk_bc, d_ent.rearrange("b s -> (b s)").partition_broadcast(P)).then_inc(s["ent_bc"], 16)
            for e in range(3):
                sp.wait_ge(s["blk_re"], 2 * e + 2)
                sp.dma_start(d_new_blocks[e], region[:, (e + 1) % 2, :]).then_inc(s_blk_st[(e + 1) % 2], 16)
            sp.wait_ge(s["row_idx"], 1)
            sp.dma_start(d_row, rows_i[:]).then_inc(s["row_out"], 16)
            sp.wait_ge(s["win_idx"], 2)
            sp.dma_start(d_win.rearrange("k b i -> b k i"), win_i[:]).then_inc(s["win_out"], 16)
            sp.wait_ge(s["row_out"], 16)
            sp.dma_start(rowidx[:], d_row.rearrange("(t b) c -> (b c) t", b=SPT)).then_inc(s["row_in"], 16)
            sp.wait_ge(s["win_out"], 16)
            for k in range(2):
                sp.dma_start(winidx[:, k, :], d_win[k].rearrange("(g b) i -> (b i) g", b=SPG)).then_inc(s["win_in"], 16)
            with sp.Fori(X_FIRST // 2, PAIRS) as i:
                sp.wait_ge(s["l0"], i * 2 - 1)
                sp.dma_start(xres[:, bass.ds(i * 2, 2), :], x_rows[:, bass.ds(i * 2, 2), :]).then_inc(s["ld_x_rest"], 16)

            def store(m, par):
                sp.wait_ge(s["y"], m + 1)
                sp.dma_start(out.rearrange("(t b) c f -> t (b c) f", b=SPT)[bass.ds(m, 1)].rearrange("t p f -> p (t f)"),
                             ys[:, par, :]).then_inc(s_out[par], 16)

            def values_out(grp, par):
                sp.wait_ge(s_patched[par], (grp - par) * 8 + 16)
                sp.dma_start(d_val[par].rearrange("(r t) n -> r t n", t=BLOCK),
                             turned[par][0:GR, :].rearrange("p (t k n) -> p k t n", t=BLOCK, k=2)[:, 1]
                             ).then_inc(s_v_out[par], 16)

            def values_in(grp, par):
                sp.wait_ge(s_v_out[par], (grp - par) * 8 + 16)
                keys = d_val[par].rearrange("(b k) n -> k b n", b=SPG)
                for h in range(2):
                    sp.dma_start(vnat[:, par, :, h, :], keys[HALF * h:HALF * h + HALF]).then_inc(s_v_in[par], 16)

            def step(grp, par):
                store(grp * 2 - 2, 0)
                values_out(grp + 1, 1 - par)
                store(grp * 2 - 1, 1)
                values_in(grp + 1, 1 - par)

            sp.wait_ge(s_blk_st[0], 16)
            sp.wait_ge(s_blk_st[1], 32)
            for grp in range(2):
                values_out(grp, grp)
                values_in(grp, grp)
            with sp.Fori(0, GROUPS // 2 - 1) as two:
                step(two * 2 + 1, 1)
                step(two * 2 + 2, 0)
            for m in range(TILES - 4, TILES):
                store(m, m % 2)
            sp.wait_ge(s_out[0], 16 * TILES // 2)
            sp.wait_ge(s_out[1], 16 * TILES // 2)

        @block.gpsimd
        def _(pool):
            ch = Chain(pool, s["pool_chain"])
            g = nc.gpsimd
            kw = dict(allow_small_or_imprecise_dtypes=True)
            g.iota(rel, pattern=[[1, SLOTS]], base=0, channel_multiplier=0, **kw)
            g.iota(e_plus, pattern=[[1, ENT]], base=1, channel_multiplier=0, **kw)
            g.iota(own[:], pattern=[[1, 3]], base=1, channel_multiplier=3, **kw)
            g.iota(pidx[:, 0:1], pattern=[[0, 1]], base=0, channel_multiplier=1)
            g.iota(kmt[:], pattern=[[-1, ROWS]], base=0, channel_multiplier=1, **kw)
            g.iota(iota8[:], pattern=[[1, ADAPTERS]], base=0, channel_multiplier=0, **kw)
            g.iota(iotat[:], pattern=[[1, ROWS]], base=0, channel_multiplier=0, **kw)
            g.memset(v_upper.rearrange("p (b s) -> p b s", s=3)[:, :, 1:2], 99.0)
            g.memset(v_upper.rearrange("p (b s) -> p b s", s=3)[:, :, 2:3], 0.0)
            g.memset(v_lower.rearrange("p (b s) -> p b s", s=3)[:, :, 0:2], 0.0)
            g.memset(halfpi[:], TWO_PI / 4)
            g.memset(epsb[:], EPS)
            for j in range(16):
                g.memset(invf[:, j:j + 1], float(np.float32(1.0) / np.float32(10000.0 ** (j / 16))))
            ch.mark(g.memset(ident[:], 0.0))
            ch.mark(g.memset(bdmask[:], 1.0))
            ch.link(g.memset(maskB[:], 0.0))
            ch.mark(g.affine_select(out=ident[:], in_=ident[:], compare_op=ALU.not_equal, fill=1.0, base=0,
                                    pattern=[[-1, P]], channel_multiplier=1))
            ch.mark(g.affine_select(out=bdmask[:], in_=bdmask[:], compare_op=ALU.is_ge, fill=0.0, base=0,
                                    pattern=[[-ROWS, SPT], [0, ROWS]], channel_multiplier=1))
            ch.link(g.affine_select(out=maskB[0:64], in_=maskB[0:64], compare_op=ALU.is_ge, fill=NEG, base=-1,
                                    pattern=[[BLOCK, WB], [1, BLOCK]], channel_multiplier=-1))
            ch.mark(g.affine_select(out=maskB[0:64], in_=maskB[0:64], compare_op=ALU.is_ge, fill=NEG, base=WINDOW,
                                    pattern=[[-BLOCK, WB], [-1, BLOCK]], channel_multiplier=1))
            ch.link(g.affine_select(out=bdmask[:], in_=bdmask[:], compare_op=ALU.is_ge, fill=0.0, base=ROWS - 1,
                                    pattern=[[ROWS, SPT], [0, ROWS]], channel_multiplier=-1))
            gates_set = g.memset(gates[:], 0.0)
            gates_set.then_inc(s["consts"], 1)
            pool.wait_ge(s["consts"], 1)
            ch.mark(g.iota(negk[64:96, :], pattern=[[0, 1]], base=0, channel_multiplier=-1, **kw))
            ch.link(g.affine_select(out=maskB[64:96], in_=maskB[64:96], compare_op=ALU.not_equal, fill=NEG, base=0,
                                    pattern=[[1, WB], [0, BLOCK]], channel_multiplier=-1))
            g.memset(gates[:], 0.0).then_inc(s["masks"], 1)
            pool.wait_ge(s["ld_mix"], 32)
            for l, w in ((0, w0), (1, w1)):
                g.indirect_dma_start(mix_raw[:, l, :], None, w.rearrange("n c d -> n (c d)"),
                                     bass.IndirectOffsetOnAxis(ap=mixi[:, l:l + 1], axis=0),
                                     bounds_check=w.shape[0] - 1, oob_is_err=False).then_inc(s["mix_gather"], 16)

            def entry_gather(e):
                for kv, src in enumerate((kflat, vflat)):
                    g.indirect_dma_start(blk_raw[:, e % 2, kv, :], None, src,
                                         bass.IndirectOffsetOnAxis(ap=enti[:, e:e + 1], axis=0),
                                         bounds_check=NBLOCKS - 1, oob_is_err=False).then_inc(s_blk_in[e % 2], 16)

            def gate():
                ch.wait()
                ch.mark(g.tensor_tensor(gates[0:1, 0:1], gates[0:1, 1:2], gates[0:1, 2:3], ALU.add))

            def mix_weights(n, j):
                wait_from(pool, s["l1"], n - 1)
                g.tensor_tensor(wbd[:, j].rearrange("p l (b d) -> p l b d", b=SPT),
                                spread(mixw[:, :, bass.ds(n, 1), :].rearrange("p l o d -> p l (o d)"), 2, SPT),
                                spread(bdmask[:], 1, 2), ALU.mult).then_inc(s["wbd"], 1)

            def swap(n, j):
                pool.wait_ge(s["norm"], n + 1)
                wait_from(pool,  s["roped"], n - 1)
                src = qn[:, j, :].rearrange("p (h u d) -> p h u d", u=2, d=16)
                dst = rs[:, j, :].rearrange("p (h u d) -> p h u d", u=2, d=16)
                for a, b, w in ((0, 8, 1), (8, 12, 3)):
                    ins = g.tensor_tensor(dst[:, a:b], src[:, a:b, ::-1, :],
                                          spread(drop(rope[:, bass.ds(n, 1), w, :]).rearrange("p (u d) -> p u d", u=2), 1, b - a),
                                          ALU.mult)
                ins.then_inc(s["swap"], 1)

            def scatter(n, j, first):
                if not first:
                    pool.wait_ge(s_scat[j], (n - j) * 8)
                ch.link(g.tensor_copy(rowcol[:, j:j + 1], rowidx[:, bass.ds(n, 1)]))
                pool.wait_ge(s["roped"], n + 1)
                pool.wait_ge(s["vrow"], n + 1)
                gate()
                g.indirect_dma_start(d_new, bass.IndirectOffsetOnAxis(ap=rowcol[:, j:j + 1], axis=0),
                                     stage[:, j, 256:512], None, bounds_check=ENT * BLOCK - 1, oob_is_err=False
                                     ).then_inc(s_scat[j], 16)

            def part2(i, first, weights):
                for j in range(2):
                    swap(i * 2 + j, j)
                if weights:
                    for j in range(2):
                        mix_weights(i * 2 + 6 + j, j)
                if first:
                    pool.wait_ge(s["row_in"], 16)
                    pool.wait_ge(s_blk_st[0], 16)
                    pool.wait_ge(s_blk_st[1], 32)
                for j in range(2):
                    scatter(i * 2 + j, j, first)

            def masks(m, par, first):
                if not first:
                    pool.wait_ge(s["scores"], m * 4 - 4)
                g.tensor_copy(mask4[:, par].rearrange("p b (r t) -> p b r t", r=4),
                              spread(maskA[:, bass.ds(m * SPT, SPT), :], 2, 4)).then_inc(s["mask4"], 1)

            def columns(grp, par):
                ch.link(g.tensor_copy(wincol[:, par, :], winidx[:, :, bass.ds(grp, 1)].rearrange("p k o -> p (k o)")))
                gate()

            def from_cache(grp, par):
                for kv, src, done in ((1, vflat, s["raw_v"]), (0, kflat, s["raw_k"])):
                    g.indirect_dma_start(blk_raw[0:GR, 0, kv, :], None, src,
                                         bass.IndirectOffsetOnAxis(ap=wincol[:, par, 0:1], axis=0),
                                         bounds_check=NBLOCKS - 1, oob_is_err=False).then_inc(done, 16)

            def from_patched(grp, par):
                g.indirect_dma_start(turned[par][0:GR, :], None, d_patched,
                                     bass.IndirectOffsetOnAxis(ap=wincol[:, par, 1:2], axis=0),
                                     bounds_check=ENT - 1, oob_is_err=False).then_inc(s_patched[par], 16)

            def fetch(grp, par):
                pool.wait_ge(s["turned"], (grp + 1) * 2 * BLOCK)
                pool.wait_ge(s_patched[1 - par], (grp + par) * 8)
                gate()
                columns(grp + 1, 1 - par)
                from_cache(grp + 1, 1 - par)
                from_patched(grp, par)

            pool.wait_ge(s["mix_load"], 32)
            for j in range(2):
                mix_weights(j, j)
            pool.wait_ge(s["ent_bc"], 16)
            pool.wait_ge(s["ent_idx"], 1)
            entry_gather(0)
            pool.wait_ge(s["wt_pe"], 5)
            entry_gather(1)
            for n in range(2, 4):
                mix_weights(n, n % 2)
            pool.wait_ge(s["maskA"], 2)
            for m in range(2):
                masks(m, m, True)
            pool.wait_ge(s["blk_re"], 2)
            entry_gather(2)
            for n in range(4, 6):
                mix_weights(n, n % 2)
            part2(0, True, True)
            pool.wait_ge(s["win_in"], 32)
            pool.wait_ge(s["blk_re"], 6)
            columns(0, 0)
            from_cache(0, 0)
            part2(1, False, True)
            pool.wait_ge(s["turned"], 2 * BLOCK)
            gate()
            columns(1, 1)
            from_cache(1, 1)
            base = ch.base + ch.n
            with pool.Fori(2, PAIRS - 3) as i:
                ch.start(base + (i - 2) * 4)
                part2(i, False, True)
                assert ch.n == 4
            ch.start(base + 4 * (PAIRS - 5))
            part2(PAIRS - 3, False, False)
            part2(PAIRS - 2, False, False)
            part2(PAIRS - 1, False, False)

            for j in range(2):
                pool.wait_ge(s_scat[j], 16 * TILES // 2)
            gate()
            from_patched(0, 0)
            pool.wait_ge(s["roped"], TILES)
            g.memset(rp[:, 0:2048], 0.0).then_inc(s["qzero"], 1)
            fetch(1, 1)

            def part3(grp, par):
                masks(grp * 2 + 2, 0, False)
                fetch(grp + 2, par)
                masks(grp * 2 + 3, 1, False)

            base = ch.base + ch.n
            with pool.Fori(0, GROUPS // 2 - 2) as two:
                ch.start(base + two * 6)
                for par in range(2):
                    part3(two * 2 + par, par)
                assert ch.n == 6
            ch.start(base + 6 * (GROUPS // 2 - 2))
            part3(GROUPS - 4, 0)
            masks(TILES - 4, 0, False)
            pool.wait_ge(s["turned"], GROUPS * 2 * BLOCK)
            gate()
            from_patched(GROUPS - 1, 1)
            for m in range(TILES - 3, TILES):
                masks(m, m % 2, False)

        @block.scalar
        def _(act):
            a = nc.scalar
            act.wait_ge(s["angles"], 1)
            a.activation(sinb, ang, ACT.Sin)
            a.activation(cosb, kq, ACT.Sin, bias=halfpi[:], scale=-1.0).then_inc(s["trig"], 1)

            for n, (dst, w) in enumerate(((wqkvT[:, 0, :], 512), (wqkvT[:, 1, :], 512),
                                          (woT.rearrange("p c n -> p (c n)"), 512),
                                          (w3T[:].rearrange("p c n -> p (c n)"), 512), (None, 0))):
                act.wait_ge(s["wt_pe"], n + 1)
                if dst is not None:
                    a.copy(dst, ps[n % 2][:, 0:w]).then_inc(s["wt_ev"], 1)
                else:
                    a.copy(laT[:].rearrange("p c n -> p (c n)"), ps[n % 2][:, 0:256])
                    a.copy(lbT[:], ps[n % 2][:, 256:512]).then_inc(s["wt_ev"], 1)
            def entry_out(e):
                act.wait_ge(s_blk_in[e % 2], 32 * (e // 2 + 1))
                if e == 1:
                    act.wait_ge(s["trig"], 2)
                    act.wait_ge(s["mix_store"], 16)
                if e == 2:
                    act.wait_ge(s_blk_st[1], 16)
                for kv in range(2):
                    a.copy(region[:, (e + 1) % 2, :].rearrange("p (t k g d) -> p k t g d", t=BLOCK, k=2, g=KVH)[:, kv],
                           blk_raw[:, e % 2, kv, :].rearrange("p (g t d) -> p t g d", g=KVH, d=HD)).then_inc(s["blk_re"], 1)

            def xT_out(n, j):
                act.wait_ge(s["xt"], n + 1)
                wait_from(act, s["qkv"], n - 1)
                a.copy(x2T[:, j].rearrange("p c n -> p (c n)"), psT[j][:, 0:256]).then_inc(s["xte"], 1)

            def keep_x(n, j):
                act.wait_ge(s["x2"], n + 1)
                a.copy(xres[:, bass.ds(n, 1), :].rearrange("p t f -> p (t f)"), x2s[:, j, :]).then_inc(s["xcopy"], 1)

            def squares(n, j):
                act.wait_ge(s["qkv"], n + 1)
                wait_from(act, s["sumsq"], n - 1)
                a.activation(sq[:, j, :], psQKV[j][:, 0:384], ACT.Square).then_inc(s["square"], 1)

            def values(n, j):
                wait_from(act, s["vrow"], n - 1)
                a.copy(vnew[:, j, :], psQKV[j][:, 384:512]).then_inc(s["vcopy"], 1)

            def value_rows(n, j, i):
                act.wait_ge(s["vcopy"], n + 1)
                wait_from(act, s_scat[j], i * 16)
                a.copy(stage[:, j, 384:512], vnew[:, j, :]).then_inc(s["vrow"], 1)

            def root(n, j):
                act.wait_ge(s["sumsq"], n + 1)
                wait_from(act, s["norm"], n - 1)
                a.activation(sd[:, j, :], ss[:, j, :], ACT.Sqrt, bias=epsb[:], scale=1.0 / HD).then_inc(s["root"], 1)

            def qT_out(n, j):
                act.wait_ge(s["qt"], n + 1)
                a.copy(qtres[:, bass.ds(n, 1), :].rearrange("p o n -> p (o n)"), psQT[j][:, 0:256]).then_inc(s["qte"], 1)

            def part2(i, s1, s2, s3, s4):
                if s3:
                    for j in range(2):
                        value_rows(i * 2 + j, j, i)
                if s2:
                    squares(i * 2 + 2, 0)
                    values(i * 2 + 2, 0)
                if s4:
                    for j in range(2):
                        qT_out(i * 2 - 2 + j, j)
                if s2:
                    root(i * 2 + 2, 0)
                    squares(i * 2 + 3, 1)
                    values(i * 2 + 3, 1)
                if s1:
                    for j in range(2):
                        xT_out(i * 2 + 4 + j, j)
                if s2:
                    root(i * 2 + 3, 1)
                if s1:
                    for j in range(2):
                        keep_x(i * 2 + 4 + j, j)

            part2(-2, True, False, False, False)
            entry_out(0)
            entry_out(1)
            part2(-1, True, True, False, False)
            entry_out(2)
            part2(0, True, True, True, False)
            with act.Fori(1, PAIRS - 2) as i:
                part2(i, True, True, True, True)
            part2(PAIRS - 2, False, True, True, True)
            part2(PAIRS - 1, False, False, True, True)
            part2(PAIRS, False, False, False, True)

            def unit_out(grp, par, u):
                act.wait_ge(s["unit"], grp * UNITS + (u + 1))
                if not (isinstance(grp, int) and grp < 2):
                    act.wait_ge(s["scores"], grp * SPG - SPG)
                ins = a.copy(kT[:, par, :, 4 * u:4 * u + 4].rearrange("p r o -> p o r"),
                             psR[u % 2][:, 0:4 * GR].rearrange("p (o r) -> p o r", o=4))
                ins.then_inc(s["unite"], 1)

            def exps(n, b):
                act.wait_ge(s["negmax"], n + 1)
                if not (isinstance(n, int) and n < 2):
                    act.wait_ge(s["pt"], n - 1)
                for c in range(2):
                    ins = a.activation(prob[:, b % 2, c, :], psS[b % 2][:, c * KEYS:(c + 1) * KEYS], ACT.Exp,
                                       bias=negm[:, b % 2, c:c + 1],
                                       accum_out=sums[:, b % 2, c:c + 1])
                ins.then_inc(s["expd"], 1)

            def probT_out(n, b):
                act.wait_ge(s["pt"], n + 1)
                if not (isinstance(n, int) and n < 2):
                    act.wait_ge(s["pv"], n - 1)
                a.copy(probT[:, b % 2].rearrange("p a c q -> p (a c q)"), psP[b % 2][0:HALF, :]).then_inc(s["pte"], 1)

            def heads_out(m):
                act.wait_ge(s["pv"], m * 4 + 4)
                wait_from(act, s["wo"], m)
                a.copy(oT.rearrange("p u (b t) -> p b u t", b=SPT),
                       psO[:, 0:256].rearrange("p (b u t) -> p b u t", b=SPT, u=2)).then_inc(s["oT"], 1)

            def x3T_out(m):
                act.wait_ge(s["x3t"], m + 1)
                wait_from(act, s["l3"], m)
                a.copy(x3T.rearrange("p c n -> p (c n)"), psZ[:, 256:512]).then_inc(s["x3te"], 1)

            def group(grp, par, first, last):
                for b in range(SPG):
                    n = grp * SPG + b
                    if not (first and b == 0):
                        probT_out(n - 1, b + 1)
                    if not (last and b == SPG - 1):
                        exps(n + 1, b + 1)
                    t = grp * 2 + (b // 4 - 1)
                    if b % 4 == 2 and not (first and b < 4):
                        x3T_out(t)
                    if not last:
                        for u in UNITS_AT[b]:
                            unit_out(grp + 1, 1 - par, u)
                    if b % 4 == 0 and not (first and b == 0):
                        heads_out(t)

            act.wait_ge(s_blk_st[0], 16)
            act.wait_ge(s_blk_st[1], 32)
            for u in range(UNITS):
                unit_out(0, 0, u)
            exps(0, 0)
            for par in range(2):
                group(par, par, par == 0, False)
            with act.Fori(1, GROUPS // 2 - 1) as two:
                for par in range(2):
                    group(two * 2 + par, par, False, False)
            for par in range(2):
                group(GROUPS - 2 + par, par, False, par == 1)
            probT_out(SEQS - 1, 1)
            heads_out(TILES - 1)
            x3T_out(TILES - 1)

        @block.vector
        def _(dve):
            v = nc.vector
            ch = Chain(dve, s["dve_chain"])
            link = ch.link
            dve.wait_ge(s["consts"], 1)
            dve.wait_ge(s["ld_idx"], 16 * N_IDX)
            ch.mark(v.tensor_scalar(remi[:], leni[:], 15, None, ALU.bitwise_and))
            ch.mark(v.tensor_scalar(rem_bci, lens_bc, 15, None, ALU.bitwise_and))
            ch.mark(v.tensor_scalar(pidx[:, 1:2], pidx[:, 0:1], 31, None, ALU.bitwise_and))
            ch.mark(v.tensor_scalar(pidx[:, 2:3], pidx[:, 0:1], 4, None, ALU.logical_shift_right))
            ch.mark(v.tensor_copy(idf[:, 3:4], leni[:]))
            ch.mark(v.tensor_copy(tabf, tabi))
            ch.mark(v.tensor_copy(len_f[:], lens_bc))
            ch.mark(v.tensor_copy(pos[:], lent[:]))
            ch.mark(v.tensor_copy(ad_f[:], adapt_bc[:]))
            ch.wait()
            ch.mark(v.tensor_copy(idf[:, 0:1], remi[:]))
            ch.mark(v.tensor_copy(rem_bc[:], rem_bci))
            ch.mark(v.tensor_copy(pf[:, 1:3], pidx[:, 1:3]))
            ch.wait()
            ch.mark(v.memset(win_i[:], SKIP))
            link(v.tensor_tensor(idf[:, 1:2], idf[:, 3:4], idf[:, 0:1], ALU.subtract))
            link(v.tensor_scalar(idf[:, 2:3], idf[:, 1:2], 1.0 / BLOCK, -float(FIRST_ENT), ALU.mult, ALU.add))
            link(v.tensor_scalar(rel, rel, idf[:, 2:3], None, ALU.subtract))
            for i in range(WB):
                ch.mark(v.scalar_tensor_tensor(out=eqall[:, i * ENT:i * ENT + SLOTS], in0=rel, scalar=float(i), in1=tabf,
                                               op0=ALU.is_equal, op1=ALU.mult, accum_out=blkw[:, i:i + 1]))
            ch.wait()
            v.tensor_copy(enti[:], blkw[:, FIRST_ENT:FIRST_ENT + 3]).then_inc(s["ent_idx"], 1)

            link(v.tensor_scalar(pos[:], pos[:], pf[:, 1:2], None, ALU.add))
            link(v.tensor_tensor(ang, spread(pos[:], 2, 16), spread(invf[:], 1, TILES), ALU.mult))
            link(v.tensor_scalar(kq, ang, 1.0 / TWO_PI, MAGIC, ALU.mult, ALU.add))
            link(v.tensor_scalar(kq, kq, MAGIC, None, ALU.subtract))
            for c in (PI2_HI, PI2_MID, PI2_LO):
                link(v.scalar_tensor_tensor(out=ang, in0=kq, scalar=-c, in1=ang, op0=ALU.mult, op1=ALU.add))
            link(v.tensor_scalar(ang, ang, 3.1415925, -3.1415925, ALU.min, ALU.max))
            v.scalar_tensor_tensor(out=kq, in0=ang, scalar=-1.0, in1=ang, op0=ALU.mult, op1=ALU.max).then_inc(s["angles"], 1)
            ch.mark(v.tensor_scalar(nscale[:, 0, 0, :], ns_bc[:, 0, :], 1.0, float(FEAT) ** -0.5, ALU.add, ALU.mult))
            ch.mark(v.tensor_scalar(nscale[:, 1, 0, :], ns_bc[:, 1, :], 1.0, None, ALU.add))
            ch.wait()
            ch.mark(v.tensor_copy(nscale[:, :, 1, 16:32], nscale[:, :, 0, 0:16]))
            ch.mark(v.tensor_scalar(nscale[:, :, 1, 0:16], nscale[:, :, 0, 16:32], -1.0, None, ALU.mult))
            ch.wait()
            dve.wait_ge(s["trig"], 1)
            for t in range(2):
                for w, src in ((0, cosb), (1, sinb)):
                    ins = v.tensor_tensor(
                        rope[:, :, 2 * t + w, :].rearrange("p t (u d) -> p t u d", u=2),
                        spread(src, 2, 2),
                        spread(nscale[:, t, w, :].rearrange("p (u d) -> p u d", u=2), 1, TILES), ALU.mult)
            ins.then_inc(s["trig"], 1)
            link(v.scalar_tensor_tensor(out=j8[:], in0=iota8[:], scalar=pf[:, 2:3], in1=sc_bc[:], op0=ALU.is_equal,
                                        op1=ALU.mult, accum_out=pf[:, 3:4]))
            ch.mark(v.tensor_scalar(admask[:], ad_f[:], pf[:, 2:3], pf[:, 3:4], ALU.is_equal, ALU.mult))
            def turn(grp, par, kv, first_token, tokens):
                if first_token == 0:
                    dve.wait_ge(s["raw_v" if kv else "raw_k"], grp * 16 + 16)
                    if not (isinstance(grp, int) and grp < 2):
                        if kv:
                            dve.wait_ge(s_v_out[par], (grp - par) * 8)
                        else:
                            dve.wait_ge(s["unit"], grp * UNITS - UNITS)
                these = slice(first_token, first_token + tokens)
                v.tensor_copy(turned[par][0:GR, :].rearrange("p (t k g d) -> p k t g d", t=BLOCK, k=2, g=KVH)[:, kv, these],
                              blk_raw[0:GR, 0, kv, :].rearrange("p (g t d) -> p t g d", g=KVH, d=HD)[:, these]
                              ).then_inc(s["turned"], tokens)

            def add1(n, j):
                dve.wait_ge(s["l0"], n + 1)
                wait_from(dve, s["l1"], n - 1)
                v.tensor_tensor(x1s[:, j, :], xres[:, bass.ds(n, 1), :].rearrange("p o f -> p (o f)"),
                                psMix[j][:, 0:256], ALU.add).then_inc(s["x1"], 1)

            def add2(n, j):
                dve.wait_ge(s["l1"], n + 1)
                wait_from(dve, s["xt"], n - 1)
                wait_from(dve, s["xcopy"], n - 1)
                v.tensor_tensor(x2s[:, j, :], x1s[:, j, :], psMix[j][:, 0:256], ALU.add).then_inc(s["x2"], 1)

            def sumsq(n, j):
                dve.wait_ge(s["square"], n + 1)
                wait_from(dve, s["root"], n - 1)
                v.tensor_reduce(ss[:, j, :], sq[:, j, :].rearrange("p (h d) -> p h d", d=HD), axis=AX_X,
                                op=ALU.add).then_inc(s["sumsq"], 1)

            def norm(n, j):
                dve.wait_ge(s["root"], n + 1)
                ch.link(v.reciprocal(ri[:, j, :], sd[:, j, :]))
                wait_from(dve, s["swap"], n - 1)
                v.tensor_tensor(qn[:, j, :].rearrange("p (h d) -> p h d", d=HD),
                                psQKV[j][:, 0:384].rearrange("p (h d) -> p h d", d=HD),
                                spread(ri[:, j, :], 2, HD), ALU.mult
                                ).then_inc(s["norm"], 1)

            def rotate(n, j):
                dve.wait_ge(s["norm"], n + 1)
                for a_, b_, w in ((0, 8, 0), (8, 12, 2)):
                    ch.mark(v.tensor_tensor(rc[:, j, 32 * a_:32 * b_].rearrange("p (h d) -> p h d", d=HD),
                                            qn[:, j, 32 * a_:32 * b_].rearrange("p (h d) -> p h d", d=HD),
                                            spread(drop(rope[:, bass.ds(n, 1), w, :]), 1, b_ - a_), ALU.mult))

            def finish(n, j, i):
                ch.wait()
                dve.wait_ge(s["swap"], n + 1)
                wait_from(dve, s["qt"], n - 1)
                wait_from(dve, s_scat[j], i * 16)
                v.tensor_tensor(stage[:, j, 0:384], rc[:, j, :], rs[:, j, :], ALU.add).then_inc(s["roped"], 1)

            def part2(i, s1, s2, s3):
                if s1:
                    for j in range(2):
                        add1(i * 2 + 4 + j, j)
                if s3:
                    for j in range(2):
                        rotate(i * 2 + j, j)
                if s2:
                    sumsq(i * 2 + 2, 0)
                if s3:
                    for j in range(2):
                        finish(i * 2 + j, j, i)
                if s1:
                    for j in range(2):
                        add2(i * 2 + 4 + j, j)
                if s2:
                    norm(i * 2 + 2, 0)
                    sumsq(i * 2 + 3, 1)
                    norm(i * 2 + 3, 1)

            dve.wait_ge(s["masks"], 1)
            link(v.tensor_tensor(start_bc[:], len_f[:], rem_bc[:], ALU.subtract))
            link(v.tensor_scalar(start_bc[:], start_bc[:], 1.0 / BLOCK, -float(FIRST_ENT), ALU.mult, ALU.add))
            v.tensor_tensor(maskA[0:64], spread(rem_bc[0:64, :], 2, ROWS),
                            spread(kmt[:], 1, SEQS), ALU.is_equal).then_inc(s["maskA"], 1)
            v.tensor_scalar(maskA[64:96], spread(start_bc[64:96, :], 2, ROWS),
                            negk[64:96, :], None, ALU.is_lt).then_inc(s["maskA"], 1)
            dve.wait_ge(s["ld_x"], 16)
            for j in range(2):
                add1(j, j)
            for j in range(2):
                add2(j, j)
            vu = v_upper.rearrange("p (b s) -> p b s", s=3)
            vl = v_lower.rearrange("p (b s) -> p b s", s=3)
            ch.mark(v.tensor_scalar(vu[:, :, 0], rem_bc[:], -1.0, 99.0, ALU.mult, ALU.add))
            ch.mark(v.tensor_copy(vl[:, :, 2], rem_bc[:]))
            ch.wait()
            dve.wait_ge(s["ent_bc"], 16)
            eq3 = eqall.rearrange("p (i e) -> p i e", e=ENT)
            for i in range(WB):
                ch.mark(v.scalar_tensor_tensor(out=eq3[:, i, :], in0=blk_bc, scalar=blkw[:, i:i + 1], in1=e_plus,
                                               op0=ALU.is_equal, op1=ALU.mult))
            ch.wait()
            for j in range(2):
                add1(2 + j, j)
            link(v.tensor_reduce(entf[:, 0:WB], eq3, axis=AX_X, op=ALU.max))
            for j in range(2):
                add2(2 + j, j)
            for j in range(2):
                sumsq(j, j)
            for k, tab in enumerate((v_upper, v_lower)):
                for e in range(3):
                    ch.mark(v.scalar_tensor_tensor(out=eq3[:, 3 * k + e, :], in0=eq3[:, FIRST_ENT + e, :],
                                                   scalar=own[:, e:e + 1], in1=tab, op0=ALU.is_gt, op1=ALU.mult))
            ch.wait()
            for j in range(2):
                norm(j, j)
            link(v.tensor_reduce(later[:].rearrange("p k e -> p (k e)"), eq3[:, 0:6, :], axis=AX_X, op=ALU.max))
            link(v.tensor_scalar(ub, ub, -1.0, 99.0, ALU.mult, ALU.add))
            T = lambda k: tok[:, k, :]
            link(v.tensor_scalar(T(0), iotat[:], idf[:, 0:1], None, ALU.add))
            ch.mark(v.tensor_scalar(T(1), T(0), float(BLOCK), None, ALU.is_ge))
            ch.mark(v.tensor_scalar(T(2), T(0), float(2 * BLOCK), None, ALU.is_ge))
            for k, src in enumerate((ub, lo, entf[:, FIRST_ENT:FIRST_ENT + 3])):
                ch.mark(v.tensor_tensor(difs[:, k, :], src[:, 1:3], src[:, 0:2], ALU.subtract))
            ch.wait()
            ch.mark(v.scalar_tensor_tensor(out=T(3), in0=T(1), scalar=-float(BLOCK), in1=T(0), op0=ALU.mult, op1=ALU.add))
            for k, src in enumerate((ub, lo, entf[:, FIRST_ENT:FIRST_ENT + 3])):
                ch.mark(v.tensor_scalar(T(5 + k), T(1), difs[:, k, 0:1], src[:, 0:1], ALU.mult, ALU.add))
            ch.wait()
            ch.mark(v.scalar_tensor_tensor(out=T(4), in0=T(2), scalar=-float(BLOCK), in1=T(3), op0=ALU.mult, op1=ALU.add))
            for k in range(3):
                ch.mark(v.scalar_tensor_tensor(out=T(8 + k), in0=T(2), scalar=difs[:, k, 1:2], in1=T(5 + k),
                                               op0=ALU.mult, op1=ALU.add))
            ch.wait()
            ch.mark(v.tensor_tensor(T(0), T(4), T(8), ALU.is_lt))
            ch.mark(v.tensor_tensor(T(1), T(4), T(9), ALU.is_ge))
            ch.mark(v.tensor_scalar(T(2), T(10), float(BLOCK), float(SKIP - BLOCK), ALU.mult, ALU.add))
            ch.wait()
            ch.mark(v.tensor_tensor(T(3), T(0), T(1), ALU.mult))
            ch.mark(v.tensor_tensor(T(5), T(2), T(4), ALU.add))
            ch.wait()
            v.scalar_tensor_tensor(out=rows_i[:], in0=T(3), scalar=-float(SKIP), in1=T(5), op0=ALU.mult,
                                   op1=ALU.add).then_inc(s["row_idx"], 1)
            link(v.tensor_scalar(junk[:, 0:WB], entf[:, 0:WB], 0.0, None, ALU.is_gt))
            link(v.tensor_scalar(junk[:, 16:16 + WB], entf[:, 0:WB], float(SKIP - 1), None, ALU.add))
            v.scalar_tensor_tensor(out=win_i[:, 0, 0:WB], in0=junk[:, 0:WB], scalar=float(SKIP), in1=blkw[:, 0:WB],
                                   op0=ALU.mult, op1=ALU.add).then_inc(s["win_idx"], 1)
            v.scalar_tensor_tensor(out=win_i[:, 1, 0:WB], in0=junk[:, 0:WB], scalar=-float(SKIP), in1=junk[:, 16:16 + WB],
                                   op0=ALU.mult, op1=ALU.add).then_inc(s["win_idx"], 1)

            part2(0, True, True, True)
            part2(1, True, True, True)
            dve.wait_ge(s["blk_re"], 6)
            for kv in (1, 0):
                turn(0, 0, kv, 0, BLOCK)
            base = ch.base + ch.n
            with dve.Fori(2, PAIRS - 2) as i:
                ch.start(base + (i - 2) * 6)
                part2(i, True, True, True)
                assert ch.n == 6
            ch.start(base + 6 * (PAIRS - 4))
            part2(PAIRS - 2, False, True, True)
            part2(PAIRS - 1, False, False, True)

            def queries(m, par, first):
                if not first:
                    dve.wait_ge(s["scores"], m * 4 - 4)
                for h in range(KVH):
                    ins = v.tensor_copy(
                        qbd[32 * h:32 * h + 32, par, :, h // 2, 64 * (h % 2):64 * (h % 2) + 64].rearrange("p b (u t) -> p b u t", u=2),
                        qtres[32 * h:32 * h + 32, bass.ds(m, 1), :].rearrange("p o (u b t) -> p (o b) u t", u=2, b=SPT))
                    if h < KVH - 1:
                        ch.mark(ins)
                ins.then_inc(s["qbd"], 1)

            def maxes(n, b):
                dve.wait_ge(s["scores"], n + 1)
                v.tensor_reduce(negm[:, b % 2, :], psS[b % 2][:, 0:2 * KEYS].rearrange("p (c k) -> p c k", c=2),
                                axis=AX_X, op=ALU.max, negate=True).then_inc(s["negmax"], 1)

            def normalise(n, b):
                dve.wait_ge(s["expd"], n + 1)
                ch.link(v.reciprocal(rinv[:, b % 2, :], sums[:, b % 2, :]))
                v.tensor_tensor(prob[:, b % 2], prob[:, b % 2], spread(rinv[:, b % 2, :], 2, KEYS), ALU.mult
                                ).then_inc(s["normed"], 1)

            def add3(m):
                dve.wait_ge(s["wo"], m + 1)
                v.tensor_tensor(x3s, xres[:, bass.ds(m, 1), :].rearrange("p o f -> p (o f)"), psZ[:, 0:256],
                                ALU.add).then_inc(s["x3"], 1)

            def adapt_in(m):
                dve.wait_ge(s["xa"], m + 1)
                v.tensor_tensor(xam.rearrange("p (b t) -> p b t", b=SPT), psZ[:, 0:P].rearrange("p (b t) -> p b t", b=SPT),
                                spread(admask[:, bass.ds(m * SPT, SPT)], 2, ROWS),
                                ALU.mult).then_inc(s["xam"], 1)

            def add4(m, par):
                dve.wait_ge(s["l3"], m + 1)
                if isinstance(m, int) and m < 2:
                    pass
                else:
                    dve.wait_ge(s_out[par], (m - par) * 8)
                v.tensor_tensor(ys[:, par, :], x3s, psZ[:, 256:512], ALU.add).then_inc(s["y"], 1)

            def group(grp, par, first, last, turns):
                for b in range(SPG):
                    n = grp * SPG + b
                    normalise(n, b)
                    if not (last and b == SPG - 1):
                        maxes(n + 1, b + 1)
                    k, t = b % 4, grp * 2 + (b // 4 - 1)
                    if k == 0 and not first:
                        add4(t - 1, b // 4)
                    if not (first and b < 4):
                        if k == 1:
                            add3(t)
                        if k == 3:
                            adapt_in(t)
                    if k == 2 and not (last and b > 4):
                        queries(grp * 2 + (b // 4 + 1), (b // 4 + 1) % 2, first and b < 4)
                    if turns and b in TURN_AT:
                        turn(grp + 2, par, *TURN_AT[b])

            dve.wait_ge(s["qte"], TILES)
            dve.wait_ge(s["xcopy"], TILES)
            dve.wait_ge(s["wbd"], TILES)
            for kv in (1, 0):
                turn(1, 1, kv, 0, BLOCK)
            dve.wait_ge(s["qzero"], 1)
            queries(0, 0, True)
            maxes(0, 0)
            for par in range(2):
                group(par, par, par == 0, False, True)
            base = ch.base + ch.n
            with dve.Fori(1, GROUPS // 2 - 1) as two:
                ch.start(base + (two - 1) * 28)
                for par in range(2):
                    group(two * 2 + par, par, False, False, True)
                assert ch.n == 28
            ch.start(base + 28 * (GROUPS // 2 - 2))
            for par in range(2):
                group(GROUPS - 2 + par, par, False, par == 1, False)
            add4(TILES - 2, 0)
            add3(TILES - 1)
            adapt_in(TILES - 1)
            add4(TILES - 1, 1)

        @block.tensor
        def _(pe):
            t_ = nc.tensor
            pe.wait_ge(s["consts"], 1)
            pe.wait_ge(s["ld_w"], 16 * N_W)
            packs = [[wqkv_raw[:, o, 0:P] for o in range(4)],
                     [wqkv_raw[:, o, P:2 * P] for o in range(4)],
                     [wo_raw[:, o, P * c:P * c + P] for c in range(2) for o in range(2)],
                     [w3_raw[:, o, P * c:P * c + P] for c in range(2) for o in range(2)],
                     [la_raw[:, 0:P], la_raw[:, P:2 * P], lb_raw[:, 0, :], lb_raw[:, 1, :]]]
            for n, pack in enumerate(packs):
                if n >= 2:
                    pe.wait_ge(s["wt_ev"], n - 1)
                for k, src in enumerate(pack):
                    ins = t_.transpose(ps[n % 2][:, P * k:P * k + P], src, ident[:])
                ins.then_inc(s["wt_pe"], 1)
            pe.wait_ge(s["wt_ev"], 5)

            def mix0(n, j):
                pe.wait_ge(s["wbd"], n + 1)
                wait_from(pe, s["x2"], n - 1)
                t_.matmul(psMix[j][:, 0:256], wbd[:, j, 0, :],
                          xres[:, bass.ds(n, 1), :].rearrange("p o f -> p (o f)"), start=True, stop=True).then_inc(s["l0"], 1)

            def mix1(n, j):
                pe.wait_ge(s["x1"], n + 1)
                t_.matmul(psMix[j][:, 0:256], wbd[:, j, 1, :], x1s[:, j, :], start=True, stop=True
                          ).then_inc(s["l1"], 1)

            def xT(n, j):
                pe.wait_ge(s["x2"], n + 1)
                wait_from(pe, s["xte"], n - 1)
                for c in range(2):
                    ins = t_.transpose(psT[j][:, P * c:P * c + P], x2s[:, j, P * c:P * c + P], ident[:])
                ins.then_inc(s["xt"], 1)

            def qkv(n, j):
                pe.wait_ge(s["xte"], n + 1)
                wait_from(pe, s["norm"], n - 1)
                wait_from(pe, s["vcopy"], n - 1)
                for c in range(2):
                    ins = t_.matmul(psQKV[j][:, :], x2T[:, j, c, :], wqkvT[:, c, :], start=(c == 0), stop=(c == 1))
                ins.then_inc(s["qkv"], 1)

            def qT(n, j):
                pe.wait_ge(s["roped"], n + 1)
                wait_from(pe, s["qte"], n - 1)
                for u in range(2):
                    ins = t_.transpose(psQT[j][:, P * u:P * u + P], stage[:, j, P * u:P * u + P], ident[:])
                ins.then_inc(s["qt"], 1)

            def part2(i, s1, s2, s4):
                if s1:
                    for j in range(2):
                        mix0(i * 2 + 4 + j, j)
                if s2:
                    qkv(i * 2 + 2, 0)
                if s4:
                    for j in range(2):
                        qT(i * 2 - 2 + j, j)
                if s1:
                    for j in range(2):
                        mix1(i * 2 + 4 + j, j)
                if s2:
                    qkv(i * 2 + 3, 1)
                if s1:
                    for j in range(2):
                        xT(i * 2 + 4 + j, j)

            pe.wait_ge(s["ld_x"], 16)
            part2(-2, True, False, False)
            part2(-1, True, True, False)
            part2(0, True, True, False)
            part2(1, True, True, True)
            with pe.Fori(2, PAIRS - 2) as i:
                pe.wait_ge(s["ld_x_rest"], i * 16 - 16)
                part2(i, True, True, True)
            part2(PAIRS - 2, False, True, True)
            part2(PAIRS - 1, False, False, True)
            part2(PAIRS, False, False, True)
            pe.wait_ge(s["qte"], TILES)
            pe.wait_ge(s["norm"], TILES)

            def unit(grp, par, u, first):
                if not (first and u < 2):
                    pe.wait_ge(s["unite"], grp * UNITS + (u - 1))
                if u == 0:
                    pe.wait_ge(s_patched[par], (grp - par) * 8 + 16)
                for o in range(4):
                    ins = t_.transpose(psR[u % 2][:, o * GR:(o + 1) * GR],
                                       turned[par][0:GR, 2 * P * (4 * u + o):2 * P * (4 * u + o) + P], ident[0:GR, 0:GR])
                ins.then_inc(s["unit"], 1)

            def scores(n, b, par, grp, m):
                if not (isinstance(n, int) and n < 2):
                    pe.wait_ge(s["expd"], n - 1)
                if b % 4 == 0:
                    pe.wait_ge(s["qbd"], m + 1)
                    pe.wait_ge(s["mask4"], m + 1)
                if b == 0:
                    pe.wait_ge(s["unite"], grp * UNITS + UNITS)
                both = psS[b % 2][:, 0:2 * KEYS].rearrange("p (c k) -> p c k", c=2)
                t_.matmul(both, mask4[:, (b // 4) % 2, b % 4, :], spread(maskB[:].rearrange("p o i -> p (o i)"), 1, 2),
                          start=True, stop=True, skip_group_check=True)
                for c in range(2):
                    ins = t_.matmul(psS[b % 2][:, c * KEYS:(c + 1) * KEYS], qbd[:, (b // 4) % 2, b % 4, c, :],
                                    kT[:, par, WS * b:WS * b + WB, :],
                                    start=False, stop=True, skip_group_check=True)
                ins.then_inc(s["scores"], 1)

            def probs_T(n, b):
                pe.wait_ge(s["normed"], n + 1)
                if not (isinstance(n, int) and n < 2):
                    pe.wait_ge(s["pte"], n - 1)
                for h in range(2):
                    for c in range(2):
                        ins = t_.transpose(psP[b % 2][0:HALF, 256 * h + P * c:256 * h + P * c + P],
                                           prob[:, b % 2, c, HALF * h:HALF * h + HALF], ident[:])
                ins.then_inc(s["pt"], 1)

            def values(n, b, par, grp, m):
                pe.wait_ge(s["pte"], n + 1)
                if b == 0:
                    pe.wait_ge(s_v_in[par], (grp - par) * 16 + 32)
                if b % 4 == 0:
                    wait_from(pe, s["oT"], m)
                for h in range(2):
                    for g_ in range(KVH):
                        ins = t_.matmul(psO[HD * g_:HD * g_ + HD, 64 * (b % 4):64 * (b % 4) + 64],
                                        vnat[:, par, b, h, HD * g_:HD * g_ + HD],
                                        probT[:, b % 2, h, g_ // 2, 64 * (g_ % 2):64 * (g_ % 2) + 64],
                                        start=(h == 0), stop=(h == 1), skip_group_check=True)
                ins.then_inc(s["pv"], 1)

            def project(m):
                pe.wait_ge(s["oT"], m + 1)
                wait_from(pe, s["y"], m)
                for c in range(2):
                    ins = t_.matmul(psZ[:, 0:256], oT[:, c, :], woT[:, c, :], start=(c == 0), stop=(c == 1))
                ins.then_inc(s["wo"], 1)

            def x3_T(m):
                pe.wait_ge(s["x3"], m + 1)
                wait_from(pe, s["y"], m)
                for c in range(2):
                    ins = t_.transpose(psZ[:, 256 + P * c:256 + P * c + P], x3s[:, P * c:P * c + P], ident[:])
                ins.then_inc(s["x3t"], 1)

            def adapter(m):
                pe.wait_ge(s["x3te"], m + 1)
                for c in range(2):
                    ins = t_.matmul(psZ[:, 0:P], laT[:, c, :], x3T[:, c, :], start=(c == 0), stop=(c == 1))
                ins.then_inc(s["xa"], 1)

            def last(m):
                pe.wait_ge(s["xam"], m + 1)
                for c in range(2):
                    t_.matmul(psZ[:, 256:512], x3T[:, c, :], w3T[:, c, :], start=(c == 0), stop=False)
                t_.matmul(psZ[:, 256:512], xam, lbT[:], start=False, stop=True).then_inc(s["l3"], 1)

            def group(grp, par, first, final):
                for b in range(SPG):
                    n, k, t = grp * SPG + b, b % 4, grp * 2 + (b // 4 - 1)
                    if not (first and b == 0):
                        probs_T(n - 1, b + 1)
                    if not (final and b == SPG - 1):
                        wrap = (b + 1) // SPG
                        scores(n + 1, (b + 1) % SPG, (par + wrap) % 2, grp + wrap, grp * 2 + (b + 1) // 4)
                    if k == 0:
                        if not first:
                            last(t - 1)
                    elif not (first and b < 4):
                        (project, x3_T, adapter)[k - 1](t)
                    if not final:
                        for u in UNITS_AT[b]:
                            unit(grp + 1, 1 - par, u, False)
                    if b > 0:
                        values(n - 1, b - 1, par, grp, grp * 2 + (b - 1) // 4)
                    elif not first:
                        values(n - 1, SPG - 1, 1 - par, grp - 1, grp * 2 - 1)

            for u in range(UNITS):
                unit(0, 0, u, True)
            scores(0, 0, 0, 0, 0)
            for par in range(2):
                group(par, par, par == 0, False)
            with pe.Fori(1, GROUPS // 2 - 1) as two:
                for par in range(2):
                    group(two * 2 + par, par, False, False)
            for par in range(2):
                group(GROUPS - 2 + par, par, False, par == 1)
            probs_T(SEQS - 1, 1)
            values(SEQS - 1, SPG - 1, 1, GROUPS - 1, TILES - 1)
            last(TILES - 2)
            project(TILES - 1)
            x3_T(TILES - 1)
            adapter(TILES - 1)
            last(TILES - 1)


_INS = ("x", "itok_B_0_7", "itok_B_1_198", "itok_Bx257_0_4111", "itok_B_37_3939", "itok_B_0_6",
        "L0_cond_weights", "L1_cond_weights", "L2_cond_Wq", "L2_cond_Wk", "L2_cond_Wv", "L2_cond_Wo",
        "L2_cond_q_norm_scale", "L2_cond_k_norm_scale", "L2_cond_k_blocks", "L2_cond_v_blocks",
        "L3_cond_W", "L3_cond_A", "L3_cond_Bm", "L3_cond_scalings")


def kernel(**inputs):
    import numpy as _np
    import concourse.bacc as _bacc
    from concourse import mybir as _mybir
    from concourse.bass_utils import run_bass_kernel_spmd as _run

    nc = _bacc.Bacc("TRN2", target_bir_lowering=False, num_devices=1)
    arrays, args = {}, []
    for name in _INS:
        a = _np.ascontiguousarray(inputs[name])
        arrays[f"in_{name}"] = a
        args.append(nc.dram_tensor(f"in_{name}", a.shape, _mybir.dt.from_np(a.dtype), kind="ExternalInput").ap())
    out = nc.dram_tensor("out", (SEQS, ROWS, FEAT), _mybir.dt.float32, kind="ExternalOutput").ap()
    build(nc, *args, out)
    r = _run(nc, [arrays], core_ids=[0])
    return r.results[0]["out"]
```
